# Optimizing a Trainium2 kernel written in Bass

```python
import numpy as np
import jax
import jax.numpy as jnp

def _softmax(x, axis=-1):
    return jax.nn.softmax(x, axis=axis)

def _gelu(x):
    return jax.nn.gelu(x, approximate=True)

def _silu(x):
    return jax.nn.silu(x)

def _sigmoid(x):
    return jax.nn.sigmoid(x)

def _layernorm(x, axis=-1, eps=1e-05):
    m = jnp.mean(x, axis=axis, keepdims=True)
    v = jnp.var(x, axis=axis, keepdims=True)
    return (x - m) / jnp.sqrt(v + eps)

def _scatter_add(tgt, idx, src, axis=0):
    return tgt.at[idx].add(src)

def _segment_sum(src, seg, n):
    return jax.ops.segment_sum(src, seg, n)
kernel_name = 'mk_conv_seq_d4_conv_nchw512_r2_637e5c'

def setup_inputs(seed: int=0):
    np.random.seed(seed)
    _w = jnp.asarray

    def _rec_inputs():
        import jax
        import jax.numpy as jnp
        _gk = jax.random.key(seed)
        x = -0.0003929 + 0.9999 * jax.random.normal(jax.random.fold_in(_gk, 1), (8, 256, 32, 32), jnp.float32)
        return x
    x = _rec_inputs()

    def _L0_conv_setup():
        import jax, jax.numpy as jnp
        import numpy as np
        LATENT_CH = 32

        def conv1x1(x, w):
            gain = 1.0 / np.sqrt(w.shape[1])
            return jnp.einsum('bchw,oc->bohw', x, w * gain)

        def casual_attention(q, k, v):
            score = jnp.einsum('bcn,bcm->bnm', q, k)
            score = jax.nn.softmax(score, axis=-1)
            return jnp.einsum('bnm,bcm->bnc', score, v)
        key = jax.random.key(seed)
        ks = jax.random.split(key, 8)
        B, C, H, W = (8, 256, 32, 32)
        L, P = (LATENT_CH, 128)
        return {'feature_map': jax.random.normal(ks[0], (B, C, H, W), jnp.float32), 'concepts': jax.random.normal(ks[1], (P, L), jnp.float32), 'w_theta': jax.random.normal(ks[2], (L, C), jnp.float32), 'w_phi': jax.random.normal(ks[3], (L, C), jnp.float32), 'w_g': jax.random.normal(ks[4], (L, C), jnp.float32), 'w_o': jax.random.normal(ks[5], (C, L), jnp.float32), 'gamma_sa': jnp.float32(0.1), 'gamma_moca': jnp.float32(0.1)}
    _L0_conv_all = _L0_conv_setup()
    _L0_conv_in = {k: v for k, v in _L0_conv_all.items() if k in ('concepts', 'w_theta', 'w_phi', 'w_g', 'w_o', 'gamma_sa', 'gamma_moca')}
    del _L0_conv_all

    def _L1_conv_setup():
        import jax, jax.numpy as jnp
        import numpy as np
        B, C, H, W = (2, 256, 32, 32)
        DQK = C // 8
        key = jax.random.key(seed)
        ks = jax.random.split(key, 8)
        s = 0.05
        return {'x': jax.random.normal(ks[0], (B, C, H, W), jnp.float32), 'Wq': jax.random.normal(ks[1], (DQK, C), jnp.float32) * s, 'bq': jax.random.normal(ks[2], (DQK,), jnp.float32) * s, 'Wk': jax.random.normal(ks[3], (DQK, C), jnp.float32) * s, 'bk': jax.random.normal(ks[4], (DQK,), jnp.float32) * s, 'Wv': jax.random.normal(ks[5], (C, C), jnp.float32) * s, 'bv': jax.random.normal(ks[6], (C,), jnp.float32) * s, 'gamma': jax.random.normal(ks[7], (1,), jnp.float32)}
    _L1_conv_all = _L1_conv_setup()
    _L1_conv_in = {k: v for k, v in _L1_conv_all.items() if k in ('Wq', 'bq', 'Wk', 'bk', 'Wv', 'bv', 'gamma')}
    del _L1_conv_all

    def _L2_conv_setup():
        import jax, jax.numpy as jnp
        import numpy as np
        EPS = 1e-05

        def group_norm(x, w, b, groups):
            N, C, H, W = x.shape
            xg = x.reshape(N, groups, C // groups * H * W)
            mean = xg.mean(axis=-1, keepdims=True)
            var = xg.var(axis=-1, keepdims=True)
            xn = ((xg - mean) * jax.lax.rsqrt(var + EPS)).reshape(N, C, H, W)
            return xn * w[None, :, None, None] + b[None, :, None, None]
        key = jax.random.key(seed)
        ks = jax.random.split(key, 7)
        N, C, H, W = (8, 256, 32, 32)
        x = jax.random.normal(ks[0], (N, C, H, W), dtype=jnp.float32)
        gn_w = jnp.ones((C,), dtype=jnp.float32)
        gn_b = jnp.zeros((C,), dtype=jnp.float32)
        s = 1.0 / np.sqrt(C)
        qkv_w = jax.random.normal(ks[1], (3 * C, C), dtype=jnp.float32) * s
        qkv_b = jnp.zeros((3 * C,), dtype=jnp.float32)
        proj_w = jax.random.normal(ks[2], (C, C), dtype=jnp.float32) * s
        proj_b = jnp.zeros((C,), dtype=jnp.float32)
        return {'x': x, 'gn_w': gn_w, 'gn_b': gn_b, 'qkv_w': qkv_w, 'qkv_b': qkv_b, 'proj_w': proj_w, 'proj_b': proj_b}
    _L2_conv_all = _L2_conv_setup()
    _L2_conv_in = {k: v for k, v in _L2_conv_all.items() if k in ('gn_w', 'gn_b', 'qkv_w', 'qkv_b', 'proj_w', 'proj_b')}
    del _L2_conv_all

    def _L3_conv_setup():
        import jax, jax.numpy as jnp
        import numpy as np
        NUM_GROUPS = 32
        NUM_HEADS = 8
        EPS = 1e-05
        RESCALE = 1.0

        def _group_norm(x, gamma, beta):
            B, C, H, W = x.shape
            xg = x.reshape(B, NUM_GROUPS, C // NUM_GROUPS, H, W)
            mu = xg.mean(axis=(2, 3, 4), keepdims=True)
            var = jnp.mean(jnp.square(xg - mu), axis=(2, 3, 4), keepdims=True)
            xn = ((xg - mu) * jax.lax.rsqrt(var + EPS)).reshape(B, C, H, W)
            return xn * gamma[None, :, None, None] + beta[None, :, None, None]

        def _layer_norm(x, gamma, beta):
            mu = x.mean(axis=-1, keepdims=True)
            var = jnp.mean(jnp.square(x - mu), axis=-1, keepdims=True)
            return (x - mu) * jax.lax.rsqrt(var + EPS) * gamma + beta
        key = jax.random.key(seed)
        ks = jax.random.split(key, 12)
        C = 256
        B, H, W = (8, 32, 32)
        s = 1.0 / np.sqrt(C)
        return {'hidden_states': jax.random.normal(ks[0], (B, C, H, W), jnp.float32), 'gn_gamma': jnp.ones((C,), jnp.float32), 'gn_beta': jnp.zeros((C,), jnp.float32), 'wq': jax.random.normal(ks[1], (C, C), jnp.float32) * s, 'bq': jnp.zeros((C,), jnp.float32), 'wk': jax.random.normal(ks[2], (C, C), jnp.float32) * s, 'bk': jnp.zeros((C,), jnp.float32), 'wv': jax.random.normal(ks[3], (C, C), jnp.float32) * s, 'bv': jnp.zeros((C,), jnp.float32), 'wo': jax.random.normal(ks[4], (C, C), jnp.float32) * s, 'bo': jnp.zeros((C,), jnp.float32), 'ln_gamma': jnp.ones((C,), jnp.float32), 'ln_beta': jnp.zeros((C,), jnp.float32)}
    _L3_conv_all = _L3_conv_setup()
    _L3_conv_in = {k: v for k, v in _L3_conv_all.items() if k in ('gn_gamma', 'gn_beta', 'wq', 'bq', 'wk', 'bk', 'wv', 'bv', 'wo', 'bo', 'ln_gamma', 'ln_beta')}
    del _L3_conv_all
    return {'x': x, 'L0_conv_concepts': _L0_conv_in['concepts'], 'L0_conv_w_theta': _L0_conv_in['w_theta'], 'L0_conv_w_phi': _L0_conv_in['w_phi'], 'L0_conv_w_g': _L0_conv_in['w_g'], 'L0_conv_w_o': _L0_conv_in['w_o'], 'L0_conv_gamma_sa': _L0_conv_in['gamma_sa'], 'L0_conv_gamma_moca': _L0_conv_in['gamma_moca'], 'L1_conv_Wq': _L1_conv_in['Wq'], 'L1_conv_bq': _L1_conv_in['bq'], 'L1_conv_Wk': _L1_conv_in['Wk'], 'L1_conv_bk': _L1_conv_in['bk'], 'L1_conv_Wv': _L1_conv_in['Wv'], 'L1_conv_bv': _L1_conv_in['bv'], 'L1_conv_gamma': _L1_conv_in['gamma'], 'L2_conv_gn_w': _L2_conv_in['gn_w'], 'L2_conv_gn_b': _L2_conv_in['gn_b'], 'L2_conv_qkv_w': _L2_conv_in['qkv_w'], 'L2_conv_qkv_b': _L2_conv_in['qkv_b'], 'L2_conv_proj_w': _L2_conv_in['proj_w'], 'L2_conv_proj_b': _L2_conv_in['proj_b'], 'L3_conv_gn_gamma': _L3_conv_in['gn_gamma'], 'L3_conv_gn_beta': _L3_conv_in['gn_beta'], 'L3_conv_wq': _L3_conv_in['wq'], 'L3_conv_bq': _L3_conv_in['bq'], 'L3_conv_wk': _L3_conv_in['wk'], 'L3_conv_bk': _L3_conv_in['bk'], 'L3_conv_wv': _L3_conv_in['wv'], 'L3_conv_bv': _L3_conv_in['bv'], 'L3_conv_wo': _L3_conv_in['wo'], 'L3_conv_bo': _L3_conv_in['bo'], 'L3_conv_ln_gamma': _L3_conv_in['ln_gamma'], 'L3_conv_ln_beta': _L3_conv_in['ln_beta']}

def reference(x, L0_conv_concepts, L0_conv_w_theta, L0_conv_w_phi, L0_conv_w_g, L0_conv_w_o, L0_conv_gamma_sa, L0_conv_gamma_moca, L1_conv_Wq, L1_conv_bq, L1_conv_Wk, L1_conv_bk, L1_conv_Wv, L1_conv_bv, L1_conv_gamma, L2_conv_gn_w, L2_conv_gn_b, L2_conv_qkv_w, L2_conv_qkv_b, L2_conv_proj_w, L2_conv_proj_b, L3_conv_gn_gamma, L3_conv_gn_beta, L3_conv_wq, L3_conv_bq, L3_conv_wk, L3_conv_bk, L3_conv_wv, L3_conv_bv, L3_conv_wo, L3_conv_bo, L3_conv_ln_gamma, L3_conv_ln_beta):
    import jax
    import jax.numpy as jnp

    def _L0_conv_ref(feature_map, concepts, w_theta, w_phi, w_g, w_o, gamma_sa, gamma_moca):
        import jax, jax.numpy as jnp
        import numpy as np
        LATENT_CH = 32

        def conv1x1(x, w):
            gain = 1.0 / np.sqrt(w.shape[1])
            return jnp.einsum('bchw,oc->bohw', x, w * gain)

        def casual_attention(q, k, v):
            score = jnp.einsum('bcn,bcm->bnm', q, k)
            score = jax.nn.softmax(score, axis=-1)
            return jnp.einsum('bnm,bcm->bnc', score, v)
        B, C, H, W = feature_map.shape
        L = LATENT_CH
        HW = H * W
        th = conv1x1(feature_map, w_theta).reshape(B, L, HW)
        ph = conv1x1(feature_map, w_phi).reshape(B, L, HW)
        g = conv1x1(feature_map, w_g).reshape(B, L, HW)
        lat = casual_attention(th, ph, g).reshape(B, L, H, W)
        sa_out = gamma_sa * conv1x1(lat, w_o) + feature_map
        enc = conv1x1(sa_out, w_theta).reshape(B, L, HW)
        phi_c = concepts.T[None]
        phi_c = jnp.broadcast_to(phi_c, (B, L, concepts.shape[0]))
        lat2 = casual_attention(enc, phi_c, phi_c).reshape(B, L, H, W)
        out = gamma_moca * conv1x1(lat2, w_o) + sa_out
        return out

    def _L1_conv_ref(x, Wq, bq, Wk, bk, Wv, bv, gamma):
        import jax, jax.numpy as jnp
        import numpy as np
        B, C, H, W = (2, 256, 32, 32)
        DQK = C // 8
        b, c, h, w = x.shape
        n = h * w
        xf = x.reshape(b, c, n)
        q = jnp.einsum('dc,bcn->bnd', Wq, xf) + bq
        k = jnp.einsum('dc,bcn->bdn', Wk, xf) + bk[:, None]
        scores = jnp.einsum('bnd,bdm->bnm', q, k)
        atten = jax.nn.softmax(scores, axis=-1)
        v = jnp.einsum('dc,bcn->bdn', Wv, xf) + bv[:, None]
        res = jnp.einsum('bcj,bij->bci', v, atten)
        out = res.reshape(b, c, h, w) * gamma + x
        return out

    def _L2_conv_ref(x, gn_w, gn_b, qkv_w, qkv_b, proj_w, proj_b):
        import jax, jax.numpy as jnp
        import numpy as np
        EPS = 1e-05

        def group_norm(x, w, b, groups):
            N, C, H, W = x.shape
            xg = x.reshape(N, groups, C // groups * H * W)
            mean = xg.mean(axis=-1, keepdims=True)
            var = xg.var(axis=-1, keepdims=True)
            xn = ((xg - mean) * jax.lax.rsqrt(var + EPS)).reshape(N, C, H, W)
            return xn * w[None, :, None, None] + b[None, :, None, None]
        N, C, H, W = x.shape
        T = H * W
        groups = min(32, C)
        h = group_norm(x, gn_w, gn_b, groups)
        hf = h.reshape(N, C, T)
        qkv = jnp.einsum('dc,nct->ndt', qkv_w, hf) + qkv_b[None, :, None]
        q, k, v = jnp.split(qkv, 3, axis=1)
        q = q.transpose(0, 2, 1)
        k = k.transpose(0, 2, 1)
        v = v.transpose(0, 2, 1)
        scale = jnp.asarray(C, x.dtype) ** (-0.5)
        attn = jnp.einsum('nqc,nkc->nqk', q, k) * scale
        attn = jax.nn.softmax(attn, axis=-1)
        o = jnp.einsum('nqk,nkc->nqc', attn, v)
        o = o.transpose(0, 2, 1)
        o = jnp.einsum('dc,nct->ndt', proj_w, o) + proj_b[None, :, None]
        return x + o.reshape(N, C, H, W)

    def _L3_conv_ref(hidden_states, gn_gamma, gn_beta, wq, bq, wk, bk, wv, bv, wo, bo, ln_gamma, ln_beta):
        import jax, jax.numpy as jnp
        import numpy as np
        NUM_GROUPS = 32
        NUM_HEADS = 8
        EPS = 1e-05
        RESCALE = 1.0

        def _group_norm(x, gamma, beta):
            B, C, H, W = x.shape
            xg = x.reshape(B, NUM_GROUPS, C // NUM_GROUPS, H, W)
            mu = xg.mean(axis=(2, 3, 4), keepdims=True)
            var = jnp.mean(jnp.square(xg - mu), axis=(2, 3, 4), keepdims=True)
            xn = ((xg - mu) * jax.lax.rsqrt(var + EPS)).reshape(B, C, H, W)
            return xn * gamma[None, :, None, None] + beta[None, :, None, None]

        def _layer_norm(x, gamma, beta):
            mu = x.mean(axis=-1, keepdims=True)
            var = jnp.mean(jnp.square(x - mu), axis=-1, keepdims=True)
            return (x - mu) * jax.lax.rsqrt(var + EPS) * gamma + beta
        residual = hidden_states
        B, C, H, W = hidden_states.shape
        x = _group_norm(hidden_states, gn_gamma, gn_beta)
        x = x.reshape(B, C, H * W).transpose(0, 2, 1)
        q = x @ wq.T + bq
        k = x @ wk.T + bk
        v = x @ wv.T + bv
        T = H * W
        dh = C // NUM_HEADS
        q = q.reshape(B, T, NUM_HEADS, dh).transpose(0, 2, 1, 3)
        k = k.reshape(B, T, NUM_HEADS, dh).transpose(0, 2, 1, 3)
        v = v.reshape(B, T, NUM_HEADS, dh).transpose(0, 2, 1, 3)
        scale = 1.0 / np.sqrt(np.sqrt(dh))
        scores = jnp.einsum('bhid,bhjd->bhij', q * scale, k)
        probs = jax.nn.softmax(scores.astype(jnp.float32), axis=-1).astype(scores.dtype)
        ctx = jnp.einsum('bhij,bhjd->bhid', probs, v)
        ctx = ctx.transpose(0, 2, 1, 3).reshape(B, T, C)
        out = _layer_norm(ctx @ wo.T + bo, ln_gamma, ln_beta)
        out = out.transpose(0, 2, 1).reshape(B, C, H, W)
        return (out + residual) / RESCALE

    def _gn(v, G=32, eps=1e-05):
        B_, C_, H_, W_ = v.shape
        g = v.reshape(B_, G, C_ // G, H_, W_)
        m = jnp.mean(g, axis=(2, 3, 4), keepdims=True)
        s = jnp.var(g, axis=(2, 3, 4), keepdims=True)
        return ((g - m) / jnp.sqrt(s + eps)).reshape(v.shape)

    def _ln_c(v, eps=1e-06):
        m = jnp.mean(v, axis=1, keepdims=True)
        s = jnp.var(v, axis=1, keepdims=True)
        return (v - m) / jnp.sqrt(s + eps)

    def _ln_t(v, eps=1e-05):
        m = jnp.mean(v, axis=-1, keepdims=True)
        s = jnp.var(v, axis=-1, keepdims=True)
        return (v - m) / jnp.sqrt(s + eps)

    def _to_tokens(v):
        B_, C_, H_, W_ = v.shape
        return v.reshape(B_, C_, H_ * W_).transpose(0, 2, 1)

    def _from_tokens(t, like):
        B_, C_, H_, W_ = like.shape
        return t.transpose(0, 2, 1).reshape(B_, C_, H_, W_)
    x = _L0_conv_ref(x, L0_conv_concepts, L0_conv_w_theta, L0_conv_w_phi, L0_conv_w_g, L0_conv_w_o, L0_conv_gamma_sa, L0_conv_gamma_moca)
    x = _L1_conv_ref(x, L1_conv_Wq, L1_conv_bq, L1_conv_Wk, L1_conv_bk, L1_conv_Wv, L1_conv_bv, L1_conv_gamma)
    x = _L2_conv_ref(x, L2_conv_gn_w, L2_conv_gn_b, L2_conv_qkv_w, L2_conv_qkv_b, L2_conv_proj_w, L2_conv_proj_b)
    x = _L3_conv_ref(x, L3_conv_gn_gamma, L3_conv_gn_beta, L3_conv_wq, L3_conv_bq, L3_conv_wk, L3_conv_bk, L3_conv_wv, L3_conv_bv, L3_conv_wo, L3_conv_bo, L3_conv_ln_gamma, L3_conv_ln_beta)
    return x

_drawn_inputs = setup_inputs


def setup_inputs(seed=0):
    import zlib

    import numpy as np

    out = dict(_drawn_inputs(seed))
    spreads = {'L2_conv_gn_w': (1.0, 0.2),
     'L2_conv_gn_b': (0.0, 0.1),
     'L2_conv_qkv_b': (0.0, 0.1),
     'L2_conv_proj_b': (0.0, 0.1),
     'L3_conv_gn_gamma': (1.0, 0.2),
     'L3_conv_gn_beta': (0.0, 0.1),
     'L3_conv_bq': (0.0, 0.1),
     'L3_conv_bk': (0.0, 0.8),
     'L3_conv_bv': (0.0, 0.1),
     'L3_conv_bo': (0.0, 0.1),
     'L3_conv_ln_gamma': (1.0, 0.2),
     'L3_conv_ln_beta': (0.0, 0.1)}
    factors = {'L1_conv_bq': 8.0, 'L1_conv_bk': 8.0, 'L1_conv_bv': 5.673}
    for name, (base, spread) in spreads.items():
        noise = np.random.default_rng([zlib.crc32(name.encode()), seed]).standard_normal(out[name].shape)
        drawn = base * np.exp(spread * noise) if base else spread * noise
        out[name] = jnp.asarray(drawn.astype(out[name].dtype))
    for name, factor in factors.items():
        out[name] = (out[name] * factor).astype(out[name].dtype)
    return out
```

```python
from contextlib import ExitStack

import concourse.bass as bass
from concourse import mybir

F32 = mybir.dt.float32
F32R = mybir.dt.float32r
ALU = mybir.AluOpType
ACT = mybir.ActivationFunctionType
AX = mybir.AxisListType

B = 8
C = 256
T = 1024
P = 128
CH = C // P
IC, IW = 2, 512
NT = T // P
L = 32
HEADS = C // L
QUAD = P // L
STACK = 3 * L
ROW = STACK
EPS = 1e-5
GROUP = C // 32

W_COLS = {}
_at = 0
for _name, _n in (("theta", STACK), ("phi", STACK), ("g", L), ("q1", STACK), ("k1", STACK), ("v1", C),
                  ("q2", C), ("k2", C), ("v2", C), ("o2", C), ("q3", C), ("k3", C), ("v3", C), ("o3", C)):
    W_COLS[_name] = slice(_at, _at + _n)
    _at += _n
W_TOTAL = _at
V_COLS = {}
_at = 0
for _name, _n in (("gn_w2", 2), ("gn_b2", 2), ("bq2", 2), ("bk2", 2), ("bo2", 2), ("gn_w3", 2), ("gn_b3", 2),
                  ("bq3", 2), ("bk3", 2), ("bo3", 2), ("ln_w", 2), ("ln_b", 2), ("bq1", 1), ("bk1", 1),
                  ("gamma_sa", 1), ("gamma_moca", 1), ("gamma1", 1)):
    V_COLS[_name] = slice(_at, _at + _n)
    _at += _n
V_TOTAL = _at


class Signal:

    def __init__(self, sem, per_batch):
        self.sem, self.per_batch = sem, per_batch

    def at(self, b, n):
        return b * self.per_batch + n


def attention_layers(nc, x, weights, vectors, value_biases, small, concepts, constants, lat_dram, out):
    with ExitStack() as ctx:
        def sb(name, shape, dt=F32):
            return ctx.enter_context(nc.sbuf_tensor(name, shape, dt))

        def signal(name, per_batch=1):
            return Signal(ctx.enter_context(nc.semaphore(name)), per_batch)

        ps = ctx.enter_context(nc.psum_tensor("ps", [P, 8, IW], F32))

        w = sb("w", [P, CH, W_TOTAL])
        vec = sb("vec", [P, V_TOTAL])
        vbias = sb("vbias", [P, 3, C])
        wo_con = sb("wo_con", [L, C + P])
        con1 = sb("con1", [P, L + 1])
        cst = sb("cst", [P, 2, P])
        ident, group_avg = cst[:, 0, :], cst[:, 1, :]
        ident_r = sb("ident_r", [P, P], F32R)
        ones = sb("ones", [P, P])
        ones_over_p = sb("ones_over_p", [P, P], F32R)
        ones_over_c = sb("ones_over_c", [P, P])
        eps = sb("eps", [P, 1])
        wo_mean = sb("wo_mean", [P, CH])

        x_in = sb("x_in", [P, CH, T])
        xa = sb("xa", [P, CH, T])
        xb = sb("xb", [P, CH, T])
        xc = sb("xc", [P, CH, T])
        xd = sb("xd", [P, CH, T])
        h = sb("h", [P, CH, T])
        qs = sb("qs", [P, HEADS, T], F32R)
        ks = sb("ks", [P, HEADS, T], F32R)
        part = sb("part", [P, 4, T], F32R)
        v = sb("v", [P, NT, C])
        vg = sb("vg", [P, NT, L + 1])
        pr = sb("pr", [P, 2, QUAD, IW])
        acc = sb("acc", [P, 2, 2, IW])
        rden = sb("rden", [P, 2, IW])
        cx = h
        shift = sb("shift", [P, T], F32R)
        nmx = sb("nmx", [P, HEADS, NT])
        nmx_r = sb("nmx_r", [P, HEADS, NT], F32R)
        lat = sb("lat", [P, NT, L])
        rlat = sb("rlat", [P, NT])
        e2 = pr[:, 0, 0:2, :].rearrange("p i (n c) -> p (i n) c", n=NT // 2)
        p2t = pr[:, 0, 2:4, :].rearrange("p i n -> p (i n)")
        enc = pr[0:L, 1, 0:2, :].rearrange("p i n -> p (i n)")
        lat_r = pr[0:L, 1, 2:4, :].rearrange("p i n -> p (i n)")
        m2 = sb("m2", [P, NT])
        bst = sb("bst", [P, CH, IC, 6])
        mv = sb("mv", [P, CH, 2])
        gmean = sb("gmean", [P, CH])
        gd = sb("gd", [P, CH])
        gv = sb("gv", [P, CH])
        gs = sb("gs", [P, CH])
        gr = sb("gr", [P, CH])
        ga = sb("ga", [P, CH])
        gma = sb("gma", [P, CH])
        gc = sb("gc", [P, CH])

        qh2, ql2, kh2, kl2 = (qs[:, 2 * n:2 * n + 2, :] for n in range(4))

        loaded = signal("loaded")
        setup_dve = signal("setup_dve")
        setup_pool = signal("setup_pool")
        setup_pe = signal("setup_pe")
        x_loaded = signal("x_loaded", 16)
        stored = signal("stored", 16 * 4)
        l0_qk = signal("l0_qk", 2)
        l0_qk_hi = signal("l0_qk_hi", 2)
        l0_qk_lo = signal("l0_qk_lo", 2)
        l0_g = signal("l0_g")
        l0_v = signal("l0_v")
        l0_lat_sum = signal("l0_lat_sum")
        l0_rlat = signal("l0_rlat", 2)
        l0_lat = signal("l0_lat", 2)
        l0_lat_out = signal("l0_lat_out", 32)
        l0_lat_in = signal("l0_lat_in", 32)
        l0_wo = signal("l0_wo", 8)
        l0_res = signal("l0_res", 8)
        l0_enc_ps = signal("l0_enc_ps")
        l0_enc = signal("l0_enc")
        l0_s2 = signal("l0_s2")
        l0_m2 = signal("l0_m2")
        l0_d2 = signal("l0_d2")
        l0_e2 = signal("l0_e2")
        l0_t2 = signal("l0_t2")
        l0_p2t = signal("l0_p2t")
        l1_qk = signal("l1_qk", 2)
        l1_qk_hi = signal("l1_qk_hi", 2)
        l1_qk_lo = signal("l1_qk_lo", 2)
        l1_v_ps = signal("l1_v_ps")
        l1_v = signal("l1_v")
        def attention_signals(layer, heads, steps, max_sets):
            return {
                "max_ps": signal(f"l{layer}_max_ps", NT * heads),
                "max": signal(f"l{layer}_max", NT * heads),
                "max_r": signal(f"l{layer}_max_r", max_sets),
                "shift_ps": signal(f"l{layer}_shift_ps", heads),
                "shift": signal(f"l{layer}_shift", heads),
                "scores": signal(f"l{layer}_scores", steps),
                "exp": signal(f"l{layer}_exp", steps),
                "pv": signal(f"l{layer}_pv", steps),
            }
        a0 = attention_signals(0, 1, 4, 1)
        a1 = attention_signals(1, 1, 4, 1)
        a2 = attention_signals(2, 1, 8, 1)
        a3 = attention_signals(3, HEADS, 32, 2)
        sums = {n: signal(f"l{n}_sums", c) for n, c in ((1, 4), (2, 8))}
        den = {n: signal(f"l{n}_den", IC) for n in (1, 2)}
        inv = {n: signal(f"l{n}_inv", c) for n, c in ((1, IC), (2, IC), (3, 4))}
        norm = {n: signal(f"l{n}_norm", c) for n, c in ((1, 4), (2, 4), (3, 4))}
        partial = signal("l1_partial_sums", IC)
        gm_a = signal("gn_mean_times_scale", 2)
        l1_res = signal("l1_res", 4)
        gn = {n: {s: signal(f"gn{n}_{s}", c) for s, c in
                  (("chan", 2), ("mean_ps", 1), ("mean", 1), ("dev", 1), ("dev2", 1), ("var_ps", 1),
                   ("std", 1), ("inv", 1), ("scale", 1), ("ms", 1), ("bias", 1), ("h", 2))} for n in (2, 3)}
        q_ps = {n: signal(f"l{n}_q_ps", 4) for n in (2, 3)}
        k_ps = {n: signal(f"l{n}_k_ps", 4) for n in (2, 3)}
        q_hi = {n: signal(f"l{n}_q_hi", 4) for n in (2, 3)}
        k_hi = {n: signal(f"l{n}_k_hi", 4) for n in (2, 3)}
        q_lo = {n: signal(f"l{n}_q_lo", 4) for n in (2, 3)}
        k_lo = {n: signal(f"l{n}_k_lo", 4) for n in (2, 3)}
        v_ps = {n: signal(f"l{n}_v_ps") for n in (2, 3)}
        v_sb = {n: signal(f"l{n}_v_sb") for n in (2, 3)}
        l2_proj = signal("l2_proj", 4)
        l2_res = signal("l2_res", 4)
        stacked = [signal(f"stacked{u}", 16 * 6 * QUAD) for u in range(CH)]
        l3_proj = signal("l3_proj", 4)
        l3_y = signal("l3_y", 4)
        l3_sq = signal("l3_sq", 4)
        l3_var = signal("l3_var", IC)
        l3_std = signal("l3_std", IC)
        l3_rstd = signal("l3_rstd", IC)
        l3_n = signal("l3_n", 4)
        l3_g = signal("l3_g", 4)
        l3_out = signal("l3_out", 4)

        x_v = x.rearrange("b (h p) t -> b p h t", p=P)
        out_v = out.rearrange("b (h p) t -> b p h t", p=P)
        bf32 = lambda ap: ap.bitcast(F32)

        def cols(i):
            return slice(i * IW, (i + 1) * IW)

        def tile(i):
            return slice(i * P, (i + 1) * P)

        def vcol(name, n=0):
            a = V_COLS[name].start + n
            return vec[:, a:a + 1]

        def wcol(name, kt, a, n):
            s = W_COLS[name].start + a
            return w[:, kt, s:s + n]

        block = ctx.enter_context(nc.Block())

        @block.sync
        def _(sp):
            sp.dma_start(w[:], weights.rearrange("(h p) n -> p h n", p=P)).then_inc(loaded.sem, 16)
            sp.dma_start(vec[:], vectors).then_inc(loaded.sem, 16)
            sp.dma_start(vbias[:], value_biases).then_inc(loaded.sem, 16)
            sp.dma_start(wo_con[:], small).then_inc(loaded.sem, 16)
            sp.dma_start(con1[:, 0:L], concepts).then_inc(loaded.sem, 16)
            sp.dma_start(cst[:], constants).then_inc(loaded.sem, 16)
            with sp.Fori(0, B) as b:
                for n in range(2):
                    sp.wait_ge(l0_lat.sem, l0_lat.at(b, n + 1))
                    sp.dma_start(lat_dram.rearrange("(i p) c -> p i c", p=P), lat[:]).then_inc(l0_lat_out.sem, 16)
                    sp.wait_ge(l0_lat_out.sem, l0_lat_out.at(b, 16 * (n + 1)))
                    sp.dma_start(lat_r, lat_dram.rearrange("(l r) c -> l (r c)", l=L)).then_inc(l0_lat_in.sem, 16)
                for u in range(CH):
                    for lo, src, dst, rows in ((q_hi, 0, qs, (0, 2)), (q_lo, 1, qs, (1,)),
                                               (k_hi, 2, ks, (0, 1)), (k_lo, 3, ks, (2,))):
                        sp.wait_ge(lo[3].sem, lo[3].at(b, IC * (u + 1)))
                        if dst is qs and rows == (0, 2):
                            sp.wait_ge(a2["scores"].sem, a2["scores"].at(b, 8))
                        for r in rows:
                            for g in range(QUAD):
                                sp.dma_start(bf32(dst[L * r:L * r + L, QUAD * u + g, :]),
                                             bf32(part[L * g:L * g + L, src, :])).then_inc(stacked[u].sem, 16)
                for n in range(4):
                    ic, ch = divmod(n, CH)
                    sp.wait_ge(l3_out.sem, l3_out.at(b, n + 1))
                    sp.dma_start(out_v[b, :, ch, cols(ic)], xb[:, ch, cols(ic)]).then_inc(stored.sem, 16)
            sp.wait_ge(stored.sem, 16 * 4 * B)

        @block.gpsimd
        def _(pool):
            pool.memset(ones[:], 1.0).then_inc(setup_pool.sem, 1)
            pool.memset(ones_over_c[:], 1.0 / C).then_inc(setup_pool.sem, 1)
            pool.memset(con1[:, L:L + 1], 1.0).then_inc(setup_pool.sem, 1)
            pool.memset(vg[:, :, L:L + 1], 1.0).then_inc(setup_pool.sem, 1)
            pool.memset(eps[:], EPS).then_inc(setup_pool.sem, 1)
            pool.memset(bf32(ones_over_p[:]), 1.0 / P).then_inc(setup_pool.sem, 1)
            pool.dma_start(x_in[:], x_v[0]).then_inc(x_loaded.sem, 16)
            with pool.Fori(0, B - 1) as b:
                pool.wait_ge(l0_res.sem, l0_res.at(b, 4))
                pool.dma_start(x_in[:], x_v[b + 1]).then_inc(x_loaded.sem, 16)

        @block.tensor
        def _(pe):
            pe.wait_ge(loaded.sem, 16 * 6)
            pe.wait_ge(setup_pool.sem, 6)
            for ch in range(CH):
                mm = pe.matmul(ps[:, 0, 0:1], ones_over_c[:], vcol("bo3", ch), start=ch == 0, stop=ch == CH - 1)
            mm.then_inc(setup_pe.sem, 1)
            pe.wait_ge(setup_dve.sem, 12)

            def project(bank, name, src, m0, m, ic):
                for kt in range(CH):
                    mm = pe.matmul(ps[0:m, bank, :], wcol(name, kt, m0, m), src[:, kt, cols(ic)],
                                   start=kt == 0, stop=kt == CH - 1)
                return mm

            def values(name, src, banks):
                for jt in range(NT):
                    for kt in range(CH):
                        mm = pe.matmul(ps[:, banks[jt // 2], (jt % 2) * C:(jt % 2 + 1) * C], src[:, kt, tile(jt)],
                                       wcol(name, kt, 0, C), start=kt == 0, stop=kt == CH - 1)
                return mm

            def max_tile(sig, b, n, head, it, pair, lag):
                if n >= lag:
                    pe.wait_ge(sig["max"].sem, sig["max"].at(b, n - lag + 1))
                for jc in range(IC):
                    mm = pe.matmul(ps[:, pair + jc, :], qs[0:STACK, head, tile(it)], ks[0:STACK, head, cols(jc)],
                                   start=True, stop=True)
                mm.then_inc(sig["max_ps"].sem, 1)

            def shift_rows(sig, b, head, pair):
                for it in range(NT):
                    mm = pe.matmul(ps[:, pair + it // 4, tile(it % 4)],
                                   nmx_r[:, head, it:it + 1].broadcast_to([P, P]), ident_r[:], start=True, stop=True)
                mm.then_inc(sig["shift_ps"].sem, 1)

            def stacked_scores(bank, head, jt, ic):
                return pe.matmul(ps[:, bank, :], ks[0:ROW + 1, head, tile(jt)], qs[0:ROW + 1, head, cols(ic)],
                                 start=True, stop=True)

            def layer0(b):
                pe.wait_ge(x_loaded.sem, x_loaded.at(b, 16))
                for n, name in enumerate(("theta", "phi")):
                    for ic in range(IC):
                        mm = project(2 * n + ic, name, x_in, 0, STACK, ic)
                    mm.then_inc(l0_qk.sem, 1)
                for jt in range(NT):
                    for kt in range(CH):
                        mm = pe.matmul(ps[:, 4, jt * L:(jt + 1) * L], x_in[:, kt, tile(jt)], wcol("g", kt, 0, L),
                                       start=kt == 0, stop=kt == CH - 1)
                mm.then_inc(l0_g.sem, 1)
                pe.wait_ge(l0_qk_lo.sem, l0_qk_lo.at(b, 2))
                pe.wait_ge(l0_v.sem, l0_v.at(b, 1))
                for it in range(NT):
                    max_tile(a0, b, it, 0, it, 2 * (it % 4), 4)
                pe.wait_ge(a0["max_r"].sem, a0["max_r"].at(b, 1))
                shift_rows(a0, b, 0, 6)
                pe.wait_ge(a0["shift"].sem, a0["shift"].at(b, 1))

                def scores(s):
                    ic, jg = divmod(s, 2)
                    if s:
                        pe.wait_ge(a0["exp"].sem, a0["exp"].at(b, s))
                    for j in range(4):
                        mm = stacked_scores(j, 0, 4 * jg + j, ic)
                    mm.then_inc(a0["scores"].sem, 1)

                def weigh(s):
                    ic, jg = divmod(s, 2)
                    pe.wait_ge(a0["exp"].sem, a0["exp"].at(b, s + 1))
                    for j in range(4):
                        for nt in range(4):
                            n = 4 * ic + nt
                            mm = pe.matmul(ps[:, 4, n * (L + 1):(n + 1) * (L + 1)], pr[:, s % 2, j, tile(nt)],
                                           vg[:, 4 * jg + j, :], start=s == 0 and j == 0 and nt == 0,
                                           stop=jg == 1 and j == 3, skip_group_check=True)
                    mm.then_inc(a0["pv"].sem, 1)
                    return mm

                scores(0)
                for s in range(4):
                    if s < 3:
                        scores(s + 1)
                    mm = weigh(s)
                for n in range(2):
                    if n == 1:
                        pe.wait_ge(l0_res.sem, l0_res.at(b, 4))
                        for ic in range(IC):
                            mm = project(4 + ic, "theta", xa, 0, L, ic)
                        mm.then_inc(l0_enc_ps.sem, 1)
                        pe.wait_ge(l0_enc.sem, l0_enc.at(b, 1))
                        for nt in range(NT):
                            mm = pe.matmul(ps[:, 6 + nt // 4, tile(nt % 4)], enc[:, tile(nt)], wo_con[:, C:C + P],
                                           start=True, stop=True)
                        mm.then_inc(l0_s2.sem, 1)
                        pe.wait_ge(l0_e2.sem, l0_e2.at(b, 1))
                        for nt in range(NT):
                            mm = pe.transpose(ps[:, nt // 4, tile(nt % 4)], e2[:, nt, :], ident)
                        mm.then_inc(l0_t2.sem, 1)
                        pe.wait_ge(l0_p2t.sem, l0_p2t.at(b, 1))
                        for nt in range(NT):
                            mm = pe.matmul(ps[:, 4, nt * (L + 1):(nt + 1) * (L + 1)], p2t[:, tile(nt)], con1[:],
                                           start=True, stop=True)
                        mm.then_inc(l0_lat_sum.sem, 1)
                    pe.wait_ge(l0_lat_in.sem, l0_lat_in.at(b, 16 * (n + 1)))
                    for k in range(4):
                        ic, ch = divmod(k, CH)
                        pe.matmul(ps[:, k, :], wo_con[:, tile(ch)], lat_r[:, cols(ic)],
                                  start=True, stop=True).then_inc(l0_wo.sem, 1)

            def self_attention(b, a, n, steps, scores, ctx_banks, per_step):
                half = steps // 2

                def weigh(s):
                    ic, jg = divmod(s, half)
                    pe.wait_ge(a["exp"].sem, a["exp"].at(b, s + 1))
                    for j in range(per_step):
                        jt = per_step * jg + j
                        for ch in range(CH):
                            mm = pe.matmul(ps[:, ctx_banks[ic] + ch, :], v[:, jt, tile(ch)],
                                           pr[:, s % 2, j, :], start=jt == 0, stop=jt == NT - 1)
                    mm.then_inc(a["pv"].sem, 1)

                def total(ic, after):
                    pe.wait_ge(a["exp"].sem, a["exp"].at(b, after + 1))
                    pe.wait_ge(sums[n].sem, sums[n].at(b, half * (ic + 1)))
                    for k in range(2):
                        mm = pe.matmul(ps[:, 0, :], ones[:], acc[:, ic, k, :], start=k == 0, stop=k == 1)
                    mm.then_inc(den[n].sem, 1)

                scores(0)
                for s in range(steps):
                    if s == half:
                        total(0, half)
                        if half == 2:
                            pe.wait_ge(inv[n].sem, inv[n].at(b, 1))
                    if s == half + 1 and half == 4:
                        pe.wait_ge(inv[n].sem, inv[n].at(b, 1))
                    if s < steps - 1:
                        scores(s + 1)
                    weigh(s)
                total(1, steps - 1)

            def layer1(b):
                pe.wait_ge(l0_res.sem, l0_res.at(b, 8))
                for n, name in enumerate(("q1", "k1")):
                    for ic in range(IC):
                        mm = project(2 * n + ic, name, xb, 0, STACK, ic)
                    mm.then_inc(l1_qk.sem, 1)
                values("v1", xb, (4, 5, 6, 7)).then_inc(l1_v_ps.sem, 1)
                pe.wait_ge(l1_qk_lo.sem, l1_qk_lo.at(b, 2))
                for it in range(NT):
                    if it == 2:
                        pe.wait_ge(l1_v.sem, l1_v.at(b, 1))
                    max_tile(a1, b, it, 0, it, 2 * (it % 4), 4)
                pe.wait_ge(a1["max_r"].sem, a1["max_r"].at(b, 1))
                shift_rows(a1, b, 0, 6)
                pe.wait_ge(a1["shift"].sem, a1["shift"].at(b, 1))

                def scores(s):
                    ic, jg = divmod(s, 2)
                    if s:
                        pe.wait_ge(a1["exp"].sem, a1["exp"].at(b, s))
                    for j in range(4):
                        mm = stacked_scores(j, 0, 4 * jg + j, ic)
                    mm.then_inc(a1["scores"].sem, 1)

                self_attention(b, a1, 1, 4, scores, (4, 6), 4)

            def group_norm(b, n):
                pe.wait_ge(gn[n]["chan"].sem, gn[n]["chan"].at(b, CH))
                pe.matmul(ps[:, 1, 0:CH], group_avg, mv[:, :, 0], start=True, stop=True)\
                    .then_inc(gn[n]["mean_ps"].sem, 1)
                pe.wait_ge(gn[n]["dev2"].sem, gn[n]["dev2"].at(b, 1))
                pe.matmul(ps[:, 2, 0:CH], group_avg, gv[:], start=True, stop=True).then_inc(gn[n]["var_ps"].sem, 1)

            def layer2(b):
                group_norm(b, 2)
                pe.wait_ge(gn[2]["h"].sem, gn[2]["h"].at(b, CH))
                for base, name, sig in ((0, "q2", q_ps[2]), (4, "k2", k_ps[2])):
                    for k in range(4):
                        blk, ic = divmod(k, IC)
                        project(base + k, name, h, P * blk, P, ic).then_inc(sig.sem, 1)
                pe.wait_ge(q_lo[2].sem, q_lo[2].at(b, 4))
                values("v2", h, (0, 1, 2, 3)).then_inc(v_ps[2].sem, 1)
                pe.wait_ge(k_lo[2].sem, k_lo[2].at(b, 4))
                for it in range(NT):
                    if it == 2:
                        pe.wait_ge(v_sb[2].sem, v_sb[2].at(b, 1))
                    pair = (4, 6, 0, 2)[it % 4]
                    if it >= 4:
                        pe.wait_ge(a2["max"].sem, a2["max"].at(b, it - 3))
                    for jc in range(IC):
                        for kt in range(CH):
                            mm = pe.matmul(ps[:, pair + jc, :], qh2[:, kt, tile(it)], kh2[:, kt, cols(jc)],
                                           start=kt == 0, stop=kt == CH - 1)
                    mm.then_inc(a2["max_ps"].sem, 1)
                pe.wait_ge(a2["max_r"].sem, a2["max_r"].at(b, 1))
                shift_rows(a2, b, 0, 4)
                pe.wait_ge(a2["shift"].sem, a2["shift"].at(b, 1))

                def scores(s):
                    ic, jg = divmod(s, 4)
                    if s >= 2:
                        pe.wait_ge(a2["exp"].sem, a2["exp"].at(b, s - 1))
                    for j in range(2):
                        bank, keys = 2 * (s % 2) + j, tile(2 * jg + j)
                        pe.matmul(ps[:, bank, :], ones_over_p[:], shift[:, cols(ic)], start=True, stop=False)
                        for kt in range(CH):
                            for kpart, qpart in ((kh2, qh2), (kh2, ql2), (kl2, qh2)):
                                mm = pe.matmul(ps[:, bank, :], kpart[:, kt, keys], qpart[:, kt, cols(ic)],
                                               start=False, stop=kt == CH - 1 and kpart is kl2)
                    mm.then_inc(a2["scores"].sem, 1)

                self_attention(b, a2, 2, 8, scores, (4, 6), 2)
                for k in range(4):
                    ic, ch = divmod(k, CH)
                    pe.wait_ge(norm[2].sem, norm[2].at(b, CH * (ic + 1)))
                    project((1, 2, 3, 4)[k], "o2", cx, P * ch, P, ic).then_inc(l2_proj.sem, 1)

            def layer3(b):
                group_norm(b, 3)
                pe.wait_ge(gn[3]["h"].sem, gn[3]["h"].at(b, CH))
                pe.wait_ge(l2_res.sem, l2_res.at(b, 4))
                for blk in range(CH):
                    for base, name, sig, done in ((0, "q3", q_ps[3], q_lo[3]), (2, "k3", k_ps[3], k_lo[3])):
                        if blk:
                            pe.wait_ge(done.sem, done.at(b, IC))
                        for ic in range(IC):
                            project(base + ic, name, h, P * blk, P, ic).then_inc(sig.sem, 1)
                    if blk == 0:
                        values("v3", h, (4, 5, 6, 7)).then_inc(v_ps[3].sem, 1)
                pe.wait_ge(v_sb[3].sem, v_sb[3].at(b, 1))

                def max_of(n, pair, lag):
                    g, it = divmod(n % (QUAD * NT), NT)
                    max_tile(a3, b, n, QUAD * (n // (QUAD * NT)) + g, it, pair, lag)

                def shifts(u):
                    pe.wait_ge(a3["max_r"].sem, a3["max_r"].at(b, u + 1))
                    for g in range(QUAD):
                        head = QUAD * u + g
                        if g >= 1:
                            pe.wait_ge(a3["shift"].sem, a3["shift"].at(b, head))
                        shift_rows(a3, b, head, 4)
                    pe.wait_ge(a3["shift"].sem, a3["shift"].at(b, QUAD * (u + 1)))

                def scores(u, s):
                    ic, jt = divmod(s, NT)
                    n = 16 * u + s
                    if n:
                        pe.wait_ge(a3["exp"].sem, a3["exp"].at(b, n))
                    for g in range(QUAD):
                        mm = stacked_scores(g, QUAD * u + g, jt, ic)
                    mm.then_inc(a3["scores"].sem, 1)

                def weigh(u, s):
                    ic, jt = divmod(s, NT)
                    n = 16 * u + s
                    pe.wait_ge(a3["exp"].sem, a3["exp"].at(b, n + 1))
                    if jt == 0 and n:
                        pe.wait_ge(norm[3].sem, norm[3].at(b, n // NT))
                    for g in range(QUAD):
                        pe.matmul(ps[L * g:L * g + L, 6, :], v[:, jt, L * (QUAD * u + g):L * (QUAD * u + g + 1)],
                                  pr[:, n % 2, g, :], start=jt == 0, stop=jt == NT - 1, tile_position=(0, L * g))
                    for g in range(QUAD):
                        mm = pe.matmul(ps[L * g:L * g + L, 7, :], ones[:, 0:L], pr[:, n % 2, g, :],
                                       start=jt == 0, stop=jt == NT - 1, tile_position=(0, L * g))
                    mm.then_inc(a3["pv"].sem, 1)

                pe.wait_ge(stacked[0].sem, stacked[0].at(b, 16 * 6 * QUAD))
                pe.wait_ge(k_lo[3].sem, k_lo[3].at(b, 4))
                for n in range(QUAD * NT):
                    max_of(n, 2 * (n % 2), 2)
                shifts(0)
                pe.wait_ge(stacked[1].sem, stacked[1].at(b, 16 * 6 * QUAD))
                scores(0, 0)
                for s in range(16):
                    max_of(QUAD * NT + 2 * s, 4, 1)
                    if s < 15:
                        scores(0, s + 1)
                    max_of(QUAD * NT + 2 * s + 1, 4, 1)
                    weigh(0, s)
                shifts(1)
                scores(1, 0)
                for s in range(16):
                    if s < 15:
                        scores(1, s + 1)
                    weigh(1, s)
                for k in range(4):
                    ic, ch = divmod(k, CH)
                    pe.wait_ge(norm[3].sem, norm[3].at(b, 3 + ic))
                    project(k, "o3", cx, P * ch, P, ic).then_inc(l3_proj.sem, 1)
                for ic in range(IC):
                    pe.wait_ge(l3_sq.sem, l3_sq.at(b, CH * (ic + 1)))
                    for ch in range(CH):
                        mm = pe.matmul(ps[:, 4 + ic, :], ones_over_c[:], xc[:, ch, cols(ic)],
                                       start=ch == 0, stop=ch == CH - 1)
                    mm.then_inc(l3_var.sem, 1)
                pe.wait_ge(l3_std.sem, l3_std.at(b, IC))

            with pe.Fori(0, B) as b:
                layer0(b)
                layer1(b)
                layer2(b)
                layer3(b)

        @block.scalar
        def _(act):
            act.wait_ge(loaded.sem, 16 * 6)
            act.wait_ge(setup_pool.sem, 6)
            act.wait_ge(setup_dve.sem, 12)

            def exps(b, a, s, banks, src, first, waits_pv=True):
                act.wait_ge(a["scores"].sem, a["scores"].at(b, s + 1))
                if s >= 2:
                    act.wait_ge(a["pv"].sem, a["pv"].at(b, s - 1))
                act.activation(pr[:, s % 2, 0:banks, :], ps[:, src:src + banks, :], ACT.Exp)\
                   .then_inc(a["exp"].sem, 1)

            def shift_row(b, a, n, head, pair):
                act.wait_ge(a["shift_ps"].sem, a["shift_ps"].at(b, n + 1))
                act.activation(qs[ROW:ROW + 1, head, :], ps[ROW:ROW + 1, pair:pair + 2, :], ACT.Copy)\
                   .then_inc(a["shift"].sem, 1)

            with act.Fori(0, B) as b:
                for n, (dst, sig) in enumerate(((qs, l0_qk), (ks, l0_qk))):
                    act.wait_ge(l0_qk.sem, l0_qk.at(b, n + 1))
                    act.activation(dst[0:STACK, 0, :], ps[0:STACK, 2 * n:2 * n + 2, :], ACT.Copy)\
                       .then_inc(l0_qk_hi.sem, 1)
                shift_row(b, a0, 0, 0, 6)
                for s in range(4):
                    exps(b, a0, s, 4, 0, 0)
                act.wait_ge(l0_enc_ps.sem, l0_enc_ps.at(b, 1))
                act.activation(enc, ps[0:L, 4:6, :], ACT.Copy).then_inc(l0_enc.sem, 1)
                act.wait_ge(l0_d2.sem, l0_d2.at(b, 1))
                act.activation(e2, e2, ACT.Exp).then_inc(l0_e2.sem, 1)
                act.wait_ge(l0_t2.sem, l0_t2.at(b, 1))
                act.activation(p2t, ps[:, 0:2, :], ACT.Copy).then_inc(l0_p2t.sem, 1)
                for n, (dst, bias) in enumerate(((qs, "bq1"), (ks, "bk1"))):
                    act.wait_ge(l1_qk.sem, l1_qk.at(b, n + 1))
                    act.activation(dst[0:STACK, 0, :], ps[0:STACK, 2 * n:2 * n + 2, :], ACT.Identity,
                                   bias=vcol(bias)[0:STACK, :]).then_inc(l1_qk_hi.sem, 1)
                shift_row(b, a1, 0, 0, 6)
                for s in range(4):
                    if s >= 2:
                        act.wait_ge(sums[1].sem, sums[1].at(b, s - 1))
                    exps(b, a1, s, 4, 0, 0)

                def group_std(n):
                    act.wait_ge(gn[n]["var_ps"].sem, gn[n]["var_ps"].at(b, 1))
                    act.activation(gs[:], ps[:, 2, 0:CH], ACT.Sqrt, bias=eps[:]).then_inc(gn[n]["std"].sem, 1)

                group_std(2)
                for base, hi, sig, bias, dst in ((0, q_hi, q_ps, "bq2", qh2), (4, k_hi, k_ps, "bk2", kh2)):
                    for k in range(4):
                        blk, ic = divmod(k, IC)
                        act.wait_ge(sig[2].sem, sig[2].at(b, k + 1))
                        act.activation(dst[:, blk, cols(ic)], ps[:, base + k, :], ACT.Identity,
                                       bias=vcol(bias, blk)).then_inc(hi[2].sem, 1)
                act.wait_ge(a2["shift_ps"].sem, a2["shift_ps"].at(b, 1))
                act.activation(shift[:], ps[:, 4:6, :], ACT.Copy).then_inc(a2["shift"].sem, 1)
                for s in range(8):
                    if s >= 2:
                        act.wait_ge(sums[2].sem, sums[2].at(b, s - 1))
                    exps(b, a2, s, 2, 2 * (s % 2), 0)
                group_std(3)
                for blk in range(CH):
                    for base, hi, sig, bias, slot in ((0, q_hi, q_ps, "bq3", 0), (2, k_hi, k_ps, "bk3", 2)):
                        if blk:
                            act.wait_ge(stacked[0].sem, stacked[0].at(b, 16 * 6 * QUAD))
                        for ic in range(IC):
                            act.wait_ge(sig[3].sem, sig[3].at(b, IC * blk + ic + 1))
                            act.activation(part[:, slot, cols(ic)], ps[:, base + ic, :], ACT.Identity,
                                           bias=vcol(bias, blk)).then_inc(hi[3].sem, 1)
                for u in range(CH):
                    for g in range(QUAD):
                        shift_row(b, a3, QUAD * u + g, QUAD * u + g, 4)
                    for s in range(16):
                        exps(b, a3, 16 * u + s, QUAD, 0, 0)
                for k in range(4):
                    ic, ch = divmod(k, CH)
                    act.wait_ge(l3_proj.sem, l3_proj.at(b, k + 1))
                    act.activation(xa[:, ch, cols(ic)], ps[:, k, :], ACT.Identity, bias=vcol("bo3", ch))\
                       .then_inc(l3_y.sem, 1)
                    act.activation(xc[:, ch, cols(ic)], ps[:, k, :], ACT.Square, bias=vcol("bo3", ch))\
                       .then_inc(l3_sq.sem, 1)
                for ic in range(IC):
                    act.wait_ge(l3_var.sem, l3_var.at(b, ic + 1))
                    act.activation(rden[:, ic, :], ps[:, 4 + ic, :], ACT.Sqrt, bias=eps[:]).then_inc(l3_std.sem, 1)
                for k in range(4):
                    ic, ch = divmod(k, CH)
                    act.wait_ge(l3_g.sem, l3_g.at(b, k + 1))
                    act.activation(xb[:, ch, cols(ic)], xb[:, ch, cols(ic)], ACT.Identity, bias=vcol("ln_b", ch))\
                       .then_inc(l3_out.sem, 1)

        @block.vector
        def _(dve):
            dve.wait_ge(loaded.sem, 16 * 6)
            dve.tensor_copy(ident_r[:], ident).then_inc(setup_dve.sem, 1)
            dve.memset(bf32(ks[ROW:ROW + 1, :, :]), 1.0).then_inc(setup_dve.sem, 1)
            def scale(ap, factor):
                dve.tensor_scalar(ap, ap, factor, None, ALU.mult).then_inc(setup_dve.sem, 1)
            gates = slice(W_COLS["theta"].start, W_COLS["g"].stop)
            scale(w[:, :, gates], C ** -0.5)
            scale(wo_con[:, 0:C], L ** -0.5)
            scale(w[:, :, W_COLS["q2"]], C ** -0.5)
            scale(w[:, :, W_COLS["q3"]], L ** -0.25)
            scale(vec[:, V_COLS["bq2"]], C ** -0.5)
            scale(vec[:, V_COLS["bq3"]], L ** -0.25)
            dve.tensor_reduce(wo_mean[:], w[:, :, W_COLS["o3"]], AX.X, ALU.add, negate=True)\
               .then_inc(setup_dve.sem, 1)
            dve.wait_ge(setup_dve.sem, 9)
            dve.tensor_scalar(wo_mean[:], wo_mean[:], 1.0 / C, None, ALU.mult).then_inc(setup_dve.sem, 1)
            dve.wait_ge(setup_dve.sem, 10)
            dve.tensor_tensor(w[:, :, W_COLS["o3"]], w[:, :, W_COLS["o3"]],
                              wo_mean[:].unsqueeze(2).broadcast_to([P, CH, C]), ALU.add).then_inc(setup_dve.sem, 1)
            dve.wait_ge(setup_pe.sem, 1)
            dve.tensor_scalar(vec[:, V_COLS["bo3"]], vec[:, V_COLS["bo3"]], ps[:, 0, 0:1], None, ALU.subtract)\
               .then_inc(setup_dve.sem, 1)

            def low_part(dst, bank, rows, hi, bias):
                if bias is None:
                    return dve.tensor_tensor(dst, ps[rows, bank:bank + 2, :], bf32(hi), ALU.subtract)
                return dve.scalar_tensor_tensor(out=dst, in0=ps[rows, bank:bank + 2, :], scalar=bias[rows, :],
                                                in1=bf32(hi), op0=ALU.add, op1=ALU.subtract)

            def two(ap):
                return ap.rearrange("p (i n) -> p i n", i=IC)

            def maxima(b, a, n, head, it, pair):
                dve.wait_ge(a["max_ps"].sem, a["max_ps"].at(b, n + 1))
                dve.tensor_reduce(nmx[:, head, it:it + 1], ps[:, pair:pair + 2, :], AX.XY, ALU.max, negate=True)\
                   .then_inc(a["max"].sem, 1)

            def round_maxima(b, a, tiles, first, heads):
                dve.wait_ge(a["max"].sem, a["max"].at(b, tiles))
                dve.tensor_copy(nmx_r[:, first:first + heads, :], nmx[:, first:first + heads, :])\
                   .then_inc(a["max_r"].sem, 1)

            def latents(b, n):
                sums_ap = ps[:, 4, 0:NT * (L + 1)].rearrange("p (n c) -> p n c", n=NT)
                dve.reciprocal(rlat[:], sums_ap[:, :, L]).then_inc(l0_rlat.sem, 1)
                dve.wait_ge(l0_rlat.sem, l0_rlat.at(b, n + 1))
                dve.tensor_tensor(lat[:], sums_ap[:, :, 0:L], rlat[:].unsqueeze(2).broadcast_to([P, NT, L]),
                                  ALU.mult).then_inc(l0_lat.sem, 1)

            def add_weights(b, a, n, s, half, per_step):
                dve.wait_ge(a["exp"].sem, a["exp"].at(b, s + 1))
                ic, jg = divmod(s, half)
                total = acc[:, ic, :, :]
                if jg == 0 and per_step == 2:
                    dve.tensor_copy(total, pr[:, s % 2, 0:2, :]).then_inc(sums[n].sem, 1)
                elif jg == 0:
                    dve.tensor_tensor(total, pr[:, s % 2, 0:2, :], pr[:, s % 2, 2:4, :], ALU.add)\
                       .then_inc(sums[n].sem, 1)
                else:
                    dve.wait_ge(sums[n].sem, sums[n].at(b, s))
                    for k in range(0, per_step, 2):
                        if k:
                            dve.wait_ge(partial.sem, partial.at(b, ic + 1))
                        add = dve.tensor_tensor(total, total, pr[:, s % 2, k:k + 2, :], ALU.add)
                        add.then_inc((sums[n] if k == per_step - 2 else partial).sem, 1)

            def normalise(b, a, n, ic, ctx_banks, steps):
                dve.wait_ge(den[n].sem, den[n].at(b, ic + 1))
                dve.reciprocal(rden[:, ic, :], ps[:, 0, :]).then_inc(inv[n].sem, 1)
                dve.wait_ge(inv[n].sem, inv[n].at(b, ic + 1))
                for ch in range(CH):
                    dve.tensor_tensor(cx[:, ch, cols(ic)], ps[:, ctx_banks[ic] + ch, :], rden[:, ic, :], ALU.mult)\
                       .then_inc(norm[n].sem, 1)

            def group_norm(b, n, src, ready, count):
                g = gn[n]
                for k in range(4):
                    ic, ch = divmod(k, CH)
                    dve.wait_ge(ready.sem, ready.at(b, k + 1))
                    dve.bn_stats(bst[:, ch, ic, :], src[:, ch, cols(ic)])
                dve.drain()
                for ch in range(CH):
                    dve.bn_aggr(mv[:, ch, :], bst[:, ch, :, :]).then_inc(g["chan"].sem, 1)
                dve.wait_ge(g["mean_ps"].sem, g["mean_ps"].at(b, 1))
                dve.tensor_copy(gmean[:], ps[:, 1, 0:CH]).then_inc(g["mean"].sem, 1)
                dve.wait_ge(g["mean"].sem, g["mean"].at(b, 1))
                dve.tensor_tensor(gd[:], mv[:, :, 0], gmean[:], ALU.subtract).then_inc(g["dev"].sem, 1)
                dve.wait_ge(g["dev"].sem, g["dev"].at(b, 1))
                dve.tensor_tensor(gd[:], gd[:], gd[:], ALU.mult).then_inc(g["ms"].sem, 1)
                dve.wait_ge(g["ms"].sem, g["ms"].at(b, 1))
                dve.tensor_tensor(gv[:], gd[:], mv[:, :, 1], ALU.add).then_inc(g["dev2"].sem, 1)
                dve.wait_ge(g["std"].sem, g["std"].at(b, 1))
                dve.reciprocal(gr[:], gs[:]).then_inc(g["inv"].sem, 1)
                dve.wait_ge(g["inv"].sem, g["inv"].at(b, 1))
                dve.tensor_tensor(ga[:], gr[:], vec[:, V_COLS[f"gn_w{n}"]], ALU.mult).then_inc(g["scale"].sem, 1)
                dve.wait_ge(g["scale"].sem, g["scale"].at(b, 1))
                dve.tensor_tensor(gma[:], gmean[:], ga[:], ALU.mult).then_inc(gm_a.sem, 1)
                dve.wait_ge(gm_a.sem, gm_a.at(b, n - 1))
                dve.tensor_tensor(gc[:], vec[:, V_COLS[f"gn_b{n}"]], gma[:], ALU.subtract)\
                   .then_inc(g["bias"].sem, 1)
                dve.wait_ge(g["bias"].sem, g["bias"].at(b, 1))
                for ch in range(CH):
                    dve.tensor_scalar(h[:, ch, :], src[:, ch, :], ga[:, ch:ch + 1], gc[:, ch:ch + 1],
                                      ALU.mult, ALU.add).then_inc(g["h"].sem, 1)

            def take_values(b, n, ready, done, first_bank):
                dve.wait_ge(ready.sem, ready.at(b, 1))
                dve.tensor_tensor(v[:].rearrange("p (k a) c -> p k a c", a=2),
                                  ps[:, first_bank:first_bank + 4, :].rearrange("p k (a c) -> p k a c", a=2),
                                  vbias[:, n - 1, :].unsqueeze(1).unsqueeze(1).broadcast_to([P, 4, 2, C]),
                                  ALU.add).then_inc(done.sem, 1)

            with dve.Fori(0, B) as b:
                for n, (dst, r) in enumerate(((qs, 1), (ks, 2))):
                    dve.wait_ge(l0_qk_hi.sem, l0_qk_hi.at(b, n + 1))
                    rows = slice(L * r, L * r + L)
                    low_part(two(dst[rows, 0, :]), 2 * n, rows, two(dst[rows, 0, :]), None)\
                        .then_inc(l0_qk_lo.sem, 1)
                dve.wait_ge(l0_g.sem, l0_g.at(b, 1))
                dve.tensor_copy(vg[:, :, 0:L], ps[:, 4, 0:NT * L].rearrange("p (n c) -> p n c", n=NT))\
                   .then_inc(l0_v.sem, 1)
                for it in range(NT):
                    maxima(b, a0, it, 0, it, 2 * (it % 4))
                round_maxima(b, a0, NT, 0, 1)
                for n in range(2):
                    if n == 0:
                        dve.wait_ge(a0["pv"].sem, a0["pv"].at(b, 4))
                    else:
                        dve.wait_ge(l0_s2.sem, l0_s2.at(b, 1))
                        s2 = ps[:, 6:8, :].rearrange("p i (n c) -> p (i n) c", n=4)
                        dve.tensor_reduce(m2[:], s2, AX.X, ALU.max).then_inc(l0_m2.sem, 1)
                        dve.wait_ge(l0_m2.sem, l0_m2.at(b, 1))
                        dve.tensor_tensor(e2, s2, m2[:].unsqueeze(2).broadcast_to([P, NT, P]), ALU.subtract)\
                           .then_inc(l0_d2.sem, 1)
                        dve.wait_ge(l0_lat_sum.sem, l0_lat_sum.at(b, 1))
                        dve.wait_ge(l0_lat_out.sem, l0_lat_out.at(b, 16))
                    latents(b, n)
                    for k in range(4):
                        ic, ch = divmod(k, CH)
                        src, dst = ((x_in, xa), (xa, xb))[n]
                        dve.wait_ge(l0_wo.sem, l0_wo.at(b, 4 * n + k + 1))
                        res = dve.scalar_tensor_tensor(out=dst[:, ch, cols(ic)], in0=ps[:, k, :],
                                                       scalar=vcol(("gamma_sa", "gamma_moca")[n]),
                                                       in1=src[:, ch, cols(ic)], op0=ALU.mult, op1=ALU.add)
                        res.then_inc(l0_res.sem, 1)
                for n, (dst, r, bias) in enumerate(((qs, 1, "bq1"), (ks, 2, "bk1"))):
                    dve.wait_ge(l1_qk_hi.sem, l1_qk_hi.at(b, n + 1))
                    rows = slice(L * r, L * r + L)
                    low_part(two(dst[rows, 0, :]), 2 * n, rows, two(dst[rows, 0, :]), vcol(bias))\
                        .then_inc(l1_qk_lo.sem, 1)
                take_values(b, 1, l1_v_ps, l1_v, 4)
                for it in range(NT):
                    maxima(b, a1, it, 0, it, 2 * (it % 4))
                round_maxima(b, a1, NT, 0, 1)

                def residual1(ic):
                    for ch in range(CH):
                        dve.wait_ge(norm[1].sem, norm[1].at(b, CH * ic + ch + 1))
                        dve.scalar_tensor_tensor(out=xc[:, ch, cols(ic)], in0=cx[:, ch, cols(ic)],
                                                 scalar=vcol("gamma1"), in1=xb[:, ch, cols(ic)],
                                                 op0=ALU.mult, op1=ALU.add).then_inc(l1_res.sem, 1)
                for s in range(4):
                    add_weights(b, a1, 1, s, 2, 4)
                    if s == 1:
                        normalise(b, a1, 1, 0, (4, 6), 4)
                        residual1(0)
                normalise(b, a1, 1, 1, (4, 6), 4)
                residual1(1)
                group_norm(b, 2, xc, l1_res, 4)
                for base, hi, lo, bias, hdst, ldst in ((0, q_hi, q_lo, "bq2", qh2, ql2),
                                                       (4, k_hi, k_lo, "bk2", kh2, kl2)):
                    for k in range(4):
                        blk, ic = divmod(k, IC)
                        dve.wait_ge(hi[2].sem, hi[2].at(b, k + 1))
                        dve.scalar_tensor_tensor(out=ldst[:, blk, cols(ic)], in0=ps[:, base + k, :],
                                                 scalar=vcol(bias, blk), in1=bf32(hdst[:, blk, cols(ic)]),
                                                 op0=ALU.add, op1=ALU.subtract).then_inc(lo[2].sem, 1)
                take_values(b, 2, v_ps[2], v_sb[2], 0)
                for it in range(NT):
                    maxima(b, a2, it, 0, it, (4, 6, 0, 2)[it % 4])
                round_maxima(b, a2, NT, 0, 1)
                for s in range(8):
                    add_weights(b, a2, 2, s, 4, 2)
                    if s == 3:
                        normalise(b, a2, 2, 0, (4, 6), 8)
                normalise(b, a2, 2, 1, (4, 6), 8)
                for k in range(4):
                    ic, ch = divmod(k, CH)
                    dve.wait_ge(l2_proj.sem, l2_proj.at(b, k + 1))
                    dve.scalar_tensor_tensor(out=xd[:, ch, cols(ic)], in0=ps[:, (1, 2, 3, 4)[k], :],
                                             scalar=vcol("bo2", ch), in1=xc[:, ch, cols(ic)],
                                             op0=ALU.add, op1=ALU.add).then_inc(l2_res.sem, 1)
                group_norm(b, 3, xd, l2_res, 4)
                for blk in range(CH):
                    for base, hi, lo, bias, slot in ((0, q_hi, q_lo, "bq3", 0), (2, k_hi, k_lo, "bk3", 2)):
                        if blk:
                            dve.wait_ge(stacked[0].sem, stacked[0].at(b, 16 * 6 * QUAD))
                        for ic in range(IC):
                            dve.wait_ge(hi[3].sem, hi[3].at(b, IC * blk + ic + 1))
                            dve.scalar_tensor_tensor(out=part[:, slot + 1, cols(ic)], in0=ps[:, base + ic, :],
                                                     scalar=vcol(bias, blk), in1=bf32(part[:, slot, cols(ic)]),
                                                     op0=ALU.add, op1=ALU.subtract).then_inc(lo[3].sem, 1)
                    if blk == 0:
                        take_values(b, 3, v_ps[3], v_sb[3], 4)

                def heads_maxima(n, pair):
                    u, r = divmod(n, QUAD * NT)
                    g, it = divmod(r, NT)
                    maxima(b, a3, n, QUAD * u + g, it, pair)

                def heads_output(u, ic):
                    dve.wait_ge(a3["pv"].sem, a3["pv"].at(b, 16 * u + NT * (ic + 1)))
                    dve.reciprocal(rden[:, ic, :], ps[:, 7, :]).then_inc(inv[3].sem, 1)
                    dve.wait_ge(inv[3].sem, inv[3].at(b, IC * u + ic + 1))
                    dve.tensor_tensor(cx[:, u, cols(ic)], ps[:, 6, :], rden[:, ic, :], ALU.mult)\
                       .then_inc(norm[3].sem, 1)

                for n in range(QUAD * NT):
                    heads_maxima(n, 2 * (n % 2))
                round_maxima(b, a3, QUAD * NT, 0, QUAD)
                for n in range(QUAD * NT):
                    heads_maxima(QUAD * NT + n, 4)
                    if n == 2 * NT:
                        heads_output(0, 0)
                round_maxima(b, a3, 2 * QUAD * NT, QUAD, QUAD)
                heads_output(0, 1)
                for ic in range(IC):
                    heads_output(1, ic)
                for ic in range(IC):
                    dve.wait_ge(l3_std.sem, l3_std.at(b, ic + 1))
                    dve.reciprocal(rden[:, ic, :], rden[:, ic, :]).then_inc(l3_rstd.sem, 1)
                    dve.wait_ge(l3_rstd.sem, l3_rstd.at(b, ic + 1))
                    for ch in range(CH):
                        k = CH * ic + ch
                        dve.tensor_tensor(xa[:, ch, cols(ic)], xa[:, ch, cols(ic)], rden[:, ic, :], ALU.mult)\
                           .then_inc(l3_n.sem, 1)
                        dve.wait_ge(l3_n.sem, l3_n.at(b, k + 1))
                        dve.scalar_tensor_tensor(out=xb[:, ch, cols(ic)], in0=xa[:, ch, cols(ic)],
                                                 scalar=vcol("ln_w", ch), in1=xd[:, ch, cols(ic)],
                                                 op0=ALU.mult, op1=ALU.add).then_inc(l3_g.sem, 1)


def kernel(**inputs):
    import numpy as np
    import concourse.bacc as bacc
    from concourse.bass_utils import run_bass_kernel_spmd

    a = {k: np.asarray(t) for k, t in inputs.items()}
    three = lambda t: np.concatenate([t] * 3, axis=-1)
    qkv = a["L2_conv_qkv_w"].T
    weights = np.concatenate([
        three(a["L0_conv_w_theta"].T), three(a["L0_conv_w_phi"].T), a["L0_conv_w_g"].T,
        three(a["L1_conv_Wq"].T), three(a["L1_conv_Wk"].T), a["L1_conv_Wv"].T,
        qkv, a["L2_conv_proj_w"].T,
        a["L3_conv_wq"].T, a["L3_conv_wk"].T, a["L3_conv_wv"].T, a["L3_conv_wo"].T], axis=1)
    halves = lambda t: t.reshape(CH, P).T
    column = lambda t: np.concatenate([t, np.zeros(P - len(t), t.dtype)]).reshape(P, 1)
    spread = lambda t: np.broadcast_to(t.reshape(1, 1), (P, 1))
    qkv_b = a["L2_conv_qkv_b"]
    vectors = np.concatenate([
        halves(a["L2_conv_gn_w"]), halves(a["L2_conv_gn_b"]), halves(qkv_b[0:C]), halves(qkv_b[C:2 * C]),
        halves(a["L2_conv_proj_b"]), halves(a["L3_conv_gn_gamma"]), halves(a["L3_conv_gn_beta"]),
        halves(a["L3_conv_bq"]), halves(a["L3_conv_bk"]), halves(a["L3_conv_bo"]),
        halves(a["L3_conv_ln_gamma"]), halves(a["L3_conv_ln_beta"]),
        column(three(a["L1_conv_bq"])), column(three(a["L1_conv_bk"])),
        spread(a["L0_conv_gamma_sa"]), spread(a["L0_conv_gamma_moca"]), spread(a["L1_conv_gamma"])], axis=1)
    value_biases = np.broadcast_to(
        np.stack([a["L1_conv_bv"], qkv_b[2 * C:], a["L3_conv_bv"]])[None], (P, 3, C))
    small = np.concatenate([a["L0_conv_w_o"].T, a["L0_conv_concepts"].T], axis=1)
    concepts = a["L0_conv_concepts"]
    groups = np.kron(np.eye(P // GROUP), np.full((GROUP, GROUP), 1.0 / GROUP))
    constants = np.stack([np.eye(P), groups], axis=1).astype(np.float32)
    x = a["x"].reshape(B, C, T)

    arrays = {"x": x, "weights": weights, "vectors": vectors, "value_biases": value_biases, "small": small,
              "concepts": concepts, "constants": constants}
    arrays = {f"in_{k}": np.ascontiguousarray(t) for k, t in arrays.items()}
    nc = bacc.Bacc("TRN2", target_bir_lowering=False, num_devices=1)
    args = [nc.dram_tensor(k, t.shape, mybir.dt.from_np(t.dtype), kind="ExternalInput").ap()
            for k, t in arrays.items()]
    lat_dram = nc.dram_tensor("latents", (T, L), F32).ap()
    out = nc.dram_tensor("out", (B, C, T), F32, kind="ExternalOutput").ap()
    attention_layers(nc, *args, lat_dram, out)
    r = run_bass_kernel_spmd(nc, [arrays], core_ids=[0])
    return r.results[0]["out"].reshape(B, C, 32, 32)
```

```python
from contextlib import ExitStack

import concourse.bass as bass
from concourse import mybir

F32 = mybir.dt.float32
F32R = mybir.dt.float32r
ALU = mybir.AluOpType
ACT = mybir.ActivationFunctionType
AX = mybir.AxisListType

B = 8
C = 256
T = 1024
P = 128
CH = C // P
IC, IW = 2, 512
NT = T // P
L = 32
HEADS = C // L
QUAD = P // L
STACK = 3 * L
ROW = STACK
EPS = 1e-5
GROUP = C // 32

W_COLS = {}
_at = 0
for _name, _n in (("theta", STACK), ("phi", STACK), ("g", L), ("q1", STACK), ("k1", STACK), ("v1", C),
                  ("q2", C), ("k2", C), ("v2", C), ("o2", C), ("q3", C), ("k3", C), ("v3", C), ("o3", C)):
    W_COLS[_name] = slice(_at, _at + _n)
    _at += _n
W_TOTAL = _at
V_COLS = {}
_at = 0
for _name, _n in (("gn_w2", 2), ("gn_b2", 2), ("bq2", 2), ("bk2", 2), ("bo2", 2), ("gn_w3", 2), ("gn_b3", 2),
                  ("bq3", 2), ("bk3", 2), ("bo3", 2), ("ln_w", 2), ("ln_b", 2), ("bq1", 1), ("bk1", 1),
                  ("gamma_sa", 1), ("gamma_moca", 1), ("gamma1", 1)):
    V_COLS[_name] = slice(_at, _at + _n)
    _at += _n
V_TOTAL = _at


STEPS = NT
STEPS3 = IC * NT
STEP_COSTS = {0: [2, 5], 1: [10, 8], 2: [7, 7, 8, 8]}
STEP_SLOTS = {n: len(costs) for n, costs in STEP_COSTS.items()}
CHUNK_COSTS = {n: 4 * STEP_COSTS[n] + [8, 8, 10] for n in (1, 2)}
FRONT_COSTS = (
    [32, 8] + [5] * NT + [8] + STEPS * STEP_COSTS[0] + [8, 12, 40, 20, 20, 16, 10, 50]
    + [32, 16, 16] + [5] * NT + [8] + IC * CHUNK_COSTS[1]
    + [20, 10, 20, 32, 32, 16, 16] + [5] * NT + [8] + IC * CHUNK_COSTS[2] + [32])
MAX3, SHIFT3, STEP3 = [5] * (QUAD * NT), [6, 6], [9, 9]
HEADS_COSTS = MAX3 + SHIFT3 + STEPS3 * STEP3 + [5, 10]
BACK_COSTS = (
    [20, 10, 20] + [32, 16, 16] + MAX3 + [32] + SHIFT3 + STEPS3 * STEP3 + [5, 10]
    + HEADS_COSTS + [20, 20, 30, 30])
FRONT_SLOTS, BACK_SLOTS = len(FRONT_COSTS), len(BACK_COSTS)
HEAD_SLOTS = len(HEADS_COSTS)


RUNS = (
    0, 13, 3, 3, 1, 3, 1, 6, 2, 1, 1, 1, 2, 1, 1, 1, 6, 1, 1, 1, 3, 1, 7, 1, 10, 1, 1, 1, 1, 2, 7, 3, 3, 2,
    1, 1, 7, 1, 1, 1, 1, 1, 1, 2, 1, 3, 1, 1, 1, 1, 1, 5, 4, 4, 2, 3, 2, 4, 1, 3, 2, 1, 2, 2, 1, 5, 2, 1, 2,
    1, 3, 2, 1, 1, 3, 1, 2, 3, 2, 2, 2, 4, 3, 1, 2, 1, 2, 1, 3, 2, 1, 1, 1, 1, 1, 1, 1, 1, 6, 1, 1, 1, 6, 1,
    1, 1, 3, 3, 1, 1, 1, 3, 1, 1, 4, 1, 1, 3, 4, 1, 3, 1, 2, 1, 2, 1, 1)
TURNS = [of_front for n, count in enumerate(RUNS) for of_front in [n % 2 == 1] * count]
assert TURNS.count(True) == FRONT_SLOTS and TURNS.count(False) == BACK_SLOTS


def by_turns(front, back):
    for of_front in TURNS:
        next(front if of_front else back)


def alone(side, slots):
    for _ in range(slots):
        next(side)


class Signal:

    def __init__(self, sem, per_batch):
        self.sem, self.per_batch = sem, per_batch

    def at(self, b, n):
        return b * self.per_batch + n


def attention_layers(nc, x, weights, vectors, value_biases, small, concepts, constants, lat_dram, out):
    with ExitStack() as ctx:
        def sb(name, shape, dt=F32):
            return ctx.enter_context(nc.sbuf_tensor(name, shape, dt))

        def signal(name, per_batch=1):
            return Signal(ctx.enter_context(nc.semaphore(name)), per_batch)

        ps = ctx.enter_context(nc.psum_tensor("ps", [P, 8, IW], F32))
        back0 = 4
        turn3 = (4, 5, 7)

        w = sb("w", [P, CH, W_TOTAL])
        vec = sb("vec", [P, V_TOTAL])
        vbias = sb("vbias", [P, 3, C])
        wo_con = sb("wo_con", [L, C + P])
        con1 = sb("con1", [P, L + 1])
        cst = sb("cst", [P, 2 * P + L])
        ident, group_avg, ident_quad = cst[:, 0:P], cst[:, P:2 * P], cst[:, 2 * P:]
        ident_r = sb("ident_r", [P, P], F32R)
        ones = sb("ones", [P, P])
        ones_over_p = sb("ones_over_p", [P, P], F32R)
        ones_over_c = sb("ones_over_c", [P, P])
        eps = sb("eps", [P, 1])
        wo_mean = sb("wo_mean", [P, CH])

        x_in = sb("x_in", [P, CH, T])
        xm = sb("xm", [P, CH, T])
        h = sb("h", [P, CH, T])
        q2k2 = sb("q2k2", [P, 8, T], F32R)
        ks01 = sb("ks01", [P, T], F32R)
        v = x_in.rearrange("p h (n c) -> p (h n) c", c=C)
        vg = sb("vg", [P, NT, L])
        pr = sb("pr", [P, 2, 2, IW])
        acc = sb("acc", [P, 2, IW])
        rden = sb("rden", [P, IW])
        shift = sb("shift", [P, T], F32R)
        lat = rden[:, 0:NT * L].rearrange("p (n c) -> p n c", n=NT)
        rlat = sb("rlat", [P, NT])
        m2 = sb("m2", [P, NT])
        qh2, ql2, kh2, kl2 = (q2k2[:, 2 * n:2 * n + 2, :] for n in range(4))
        qs01 = q2k2[:, 0, :]
        e2 = h[:, 0, :].rearrange("p (n c) -> p n c", n=NT)
        p2t = h[:, 1, :]
        acc0 = (h[:, 0, :].rearrange("p (k n) -> p k n", k=2), acc)
        lat_parts = h[:, 1, :]
        enc = pr[0:L, 0, :, :].rearrange("p i n -> p (i n)")
        lat_r = pr[0:L, 1, :, :].rearrange("p i n -> p (i n)")

        xd = sb("xd", [P, CH, T])
        hb = sb("hb", [P, CH, T])
        part = sb("part", [P, 4, T], F32R)
        qs = sb("qs", [P, QUAD, T], F32R)
        ks = sb("ks", [P, QUAD, T], F32R)
        vb = sb("vb", [P, NT, C])
        prb = sb("prb", [P, 2, QUAD, IW])
        accb = sb("accb", [P, QUAD, IW])
        rdenb = sb("rdenb", [P, IW])
        rstd = accb[:, 0:IC, :]
        y = prb[:, 0, :, :].rearrange("p (h i) n -> p h (i n)", h=CH)
        sq = prb[:, 1, :, :].rearrange("p (h i) n -> p h (i n)", h=CH)

        nmx = {"front": sb("nmx_f", [P, 1, NT]), "back": sb("nmx_b", [P, QUAD, NT])}
        nmx_r = {"front": sb("nmx_rf", [P, 1, NT], F32R), "back": sb("nmx_rb", [P, QUAD, NT], F32R)}
        small_sb = {n: {s: sb(f"gn{n}_{s}_sb", shape) for s, shape in
                        (("bst", [P, CH, IC, 6]), ("mv", [P, CH, 2]), ("mean", [P, CH]), ("dev", [P, CH]),
                         ("dev_sq", [P, CH]), ("var", [P, CH]), ("std", [P, CH]), ("inv", [P, CH]),
                         ("scale", [P, CH]), ("ms", [P, CH]), ("bias", [P, CH]))} for n in (2, 3)}

        loaded = signal("loaded")
        setup_dve = signal("setup_dve")
        setup_pool = signal("setup_pool")
        setup_pe = signal("setup_pe")
        setup_mean = signal("setup_mean")
        x_loaded = signal("x_loaded", 16)
        stored = signal("stored", 16 * 4)
        l0_g = signal("l0_g")
        l0_v = signal("l0_v")
        l0_parts = signal("l0_parts")
        l0_lat_sum = signal("l0_lat_sum", 2)
        l0_rlat = signal("l0_rlat", 2)
        l0_lat = signal("l0_lat", 2)
        l0_lat_out = signal("l0_lat_out", 32)
        l0_lat_in = signal("l0_lat_in", 32)
        l0_wo = signal("l0_wo", 8)
        l0_res = signal("l0_res", 8)
        l0_enc_ps = signal("l0_enc_ps")
        l0_enc = signal("l0_enc")
        l0_s2 = signal("l0_s2")
        l0_m2 = signal("l0_m2")
        l0_d2 = signal("l0_d2")
        l0_e2 = signal("l0_e2")
        l0_t2 = signal("l0_t2")
        l0_p2t = signal("l0_p2t")
        qk_ps = {n: signal(f"l{n}_qk_ps", 2) for n in (0, 1)}
        qk_hi = {n: signal(f"l{n}_qk_hi", 2) for n in (0, 1)}
        qk_lo = {n: signal(f"l{n}_qk_lo", 2) for n in (0, 1)}
        q_ps = {n: signal(f"l{n}_q_ps", 4) for n in (2, 3)}
        k_ps = {n: signal(f"l{n}_k_ps", 4) for n in (2, 3)}
        q_hi = {n: signal(f"l{n}_q_hi", 4) for n in (2, 3)}
        k_hi = {n: signal(f"l{n}_k_hi", 4) for n in (2, 3)}
        q_lo = {n: signal(f"l{n}_q_lo", 4) for n in (2, 3)}
        k_lo = {n: signal(f"l{n}_k_lo", 4) for n in (2, 3)}
        v_ps = {n: signal(f"l{n}_v_ps", 2) for n in (1, 2, 3)}
        v_sb = {n: signal(f"l{n}_v_sb", 2) for n in (1, 2, 3)}
        heads = {0: 1, 1: 1, 2: 1, 3: HEADS}
        max_ps = {n: signal(f"l{n}_max_ps", NT * heads[n]) for n in heads}
        max_sb = {n: signal(f"l{n}_max_sb", NT * heads[n]) for n in heads}
        max_r = {n: signal(f"l{n}_max_r", CH if n == 3 else 1) for n in heads}
        shift_ps = {n: signal(f"l{n}_shift_ps", heads[n]) for n in heads}
        shift_sb = {n: signal(f"l{n}_shift_sb", heads[n]) for n in heads}
        steps = {0: STEPS, 1: STEPS, 2: STEPS, 3: CH * STEPS3 * QUAD}
        scored = {n: signal(f"l{n}_scored", steps[n]) for n in heads}
        exped = {n: signal(f"l{n}_exped", steps[n]) for n in heads}
        weighed = {n: signal(f"l{n}_weighed", steps[n] // (QUAD if n == 3 else 1)) for n in heads}
        summed = {n: signal(f"l{n}_summed", 3 * IC) for n in (0, 1, 2)}
        folded = {n: signal(f"l{n}_folded", IC) for n in (0, 1, 2)}
        summed_dve = signal("l3_summed_dve", (NT - 1) * IC * CH)
        summed_pool = signal("l3_summed_pool", (NT - 1) * IC * CH)
        total = {n: signal(f"l{n}_total", c) for n, c in ((1, IC), (2, IC), (3, IC * CH))}
        inverse = {n: signal(f"l{n}_inverse", c) for n, c in ((1, IC), (2, IC), (3, IC * CH))}
        taken = signal("l3_taken", IC * CH)
        normed = {n: signal(f"l{n}_normed", 4) for n in (1, 2, 3)}
        l1_res = signal("l1_res", 4)
        l2_proj = signal("l2_proj", 4)
        l2_res = signal("l2_res", 4)
        gn = {n: {s: signal(f"gn{n}_{s}", c) for s, c in
                  (("chan", 2), ("mean_ps", 1), ("mean", 1), ("dev", 1), ("dev_sq", 1), ("var", 1), ("var_ps", 1),
                   ("std", 1), ("inv", 1), ("scale", 1), ("ms", 1), ("bias", 1), ("h", 2))} for n in (2, 3)}
        xd_copied = signal("xd_copied", 16)
        stacked = [signal(f"stacked{u}", 16 * 6 * QUAD) for u in range(CH)]
        l3_proj = signal("l3_proj", 4)
        l3_y = signal("l3_y", 4)
        l3_sq = signal("l3_sq", 4)
        l3_var = signal("l3_var", IC)
        l3_std = signal("l3_std", IC)
        l3_rstd = signal("l3_rstd", IC)
        l3_n = signal("l3_n", 4)
        l3_g = signal("l3_g", 4)
        l3_out = signal("l3_out", 4)

        def score_use(s, g):
            return QUAD * s + g + (s >= NT + 2)

        def total_use(ic):
            return (QUAD * (NT + 2), QUAD * STEPS3 + 1)[ic]

        def bank_use(u, use):
            for ic in range(IC):
                if use == total_use(ic):
                    return inverse[3], IC * u + ic + 1
            return exped[3], QUAD * STEPS3 * u + use - (use > total_use(0)) + 1

        x_v = x.rearrange("b (h p) t -> b p h t", p=P)
        out_v = out.rearrange("b (h p) t -> b p h t", p=P)

        def bf32(ap):
            return ap.bitcast(F32)

        def cols(i):
            return slice(i * IW, (i + 1) * IW)

        def tile(i):
            return slice(i * P, (i + 1) * P)

        def vcol(name, n=0):
            a = V_COLS[name].start + n
            return vec[:, a:a + 1]

        def wcol(name, kt, a, n):
            s = W_COLS[name].start + a
            return w[:, kt, s:s + n]

        block = ctx.enter_context(nc.Block())

        @block.sync
        def _(sp):
            sp.dma_start(w[:], weights.rearrange("(h p) n -> p h n", p=P)).then_inc(loaded.sem, 16)
            sp.dma_start(vec[:], vectors).then_inc(loaded.sem, 16)
            sp.dma_start(vbias[:], value_biases).then_inc(loaded.sem, 16)
            sp.dma_start(wo_con[:], small).then_inc(loaded.sem, 16)
            sp.dma_start(con1[:, 0:L], concepts).then_inc(loaded.sem, 16)
            sp.dma_start(cst[:], constants).then_inc(loaded.sem, 16)

            def latents(b, n):
                sp.wait_ge(l0_lat.sem, l0_lat.at(b, n + 1))
                sp.dma_start(lat_dram.rearrange("(i p) c -> p i c", p=P), lat).then_inc(l0_lat_out.sem, 16)
                sp.wait_ge(l0_lat_out.sem, l0_lat_out.at(b, 16 * (n + 1)))
                sp.dma_start(lat_r, lat_dram.rearrange("(l r) c -> l (r c)", l=L)).then_inc(l0_lat_in.sem, 16)

            def front(b):
                yield
                for _ in range(2 + NT + 1 + STEP_SLOTS[0] * STEPS):
                    yield
                latents(b, 0)
                yield
                for _ in range(4):
                    yield
                latents(b, 1)
                yield
                while True:
                    yield

            def stacks(b, u):
                if u:
                    sp.wait_ge(scored[3].sem, scored[3].at(b, QUAD * STEPS3))
                for done, src, dst, rows in ((q_hi, 0, qs, (0, 2)), (q_lo, 1, qs, (1,)),
                                             (k_hi, 2, ks, (0, 1)), (k_lo, 3, ks, (2,))):
                    if u == 0:
                        sp.wait_ge(done[3].sem, done[3].at(b, IC))
                    for r in rows:
                        for g in range(QUAD):
                            sp.dma_start(bf32(dst[L * r:L * r + L, g, :]),
                                         bf32(part[L * g:L * g + L, src, :])).then_inc(stacked[u].sem, 16)

            def back(b):
                sp.wait_ge(l2_res.sem, l2_res.at(b, 4))
                sp.dma_start(xd[:], xm[:]).then_inc(xd_copied.sem, 16)
                for _ in range(3):
                    yield
                stacks(b, 0)
                yield
                for _ in range(3 + HEAD_SLOTS - 2):
                    yield
                stacks(b, 1)
                yield
                for _ in range(1 + HEAD_SLOTS + 2):
                    yield
                for ic in range(IC):
                    for ch in range(CH):
                        sp.wait_ge(l3_out.sem, l3_out.at(b, CH * ic + ch + 1))
                        sp.dma_start(out_v[b, :, ch, cols(ic)], y[:, ch, cols(ic)]).then_inc(stored.sem, 16)
                    yield

            alone(front(0), FRONT_SLOTS)
            with sp.Fori(0, B - 1) as b:
                by_turns(front(b + 1), back(b))
            alone(back(B - 1), BACK_SLOTS)
            sp.wait_ge(stored.sem, stored.at(B, 1))

        @block.gpsimd
        def _(pool):
            pool.memset(ones[:], 1.0).then_inc(setup_pool.sem, 1)
            pool.memset(ones_over_c[:], 1.0 / C).then_inc(setup_pool.sem, 1)
            pool.memset(con1[:, L:L + 1], 1.0).then_inc(setup_pool.sem, 1)
            pool.memset(eps[:], EPS).then_inc(setup_pool.sem, 1)
            pool.memset(nmx["back"][:], 0.0).then_inc(stored.sem, 1)
            pool.memset(bf32(ones_over_p[:]), 1.0 / P).then_inc(setup_pool.sem, 1)

            def idle(n):
                for _ in range(n):
                    yield

            def add_step(b, n, s, into):
                ic, jg = divmod(s, 4)
                if jg:
                    pool.wait_ge(exped[n].sem, exped[n].at(b, s + 1))
                    if n and jg == 1 and ic:
                        pool.wait_ge(total[n].sem, total[n].at(b, ic))
                    if jg > 1:
                        pool.wait_ge(summed[n].sem, summed[n].at(b, 3 * ic + jg - 1))
                    pool.tensor_tensor(into[:], pr[:, (s - 1) % 2, :, :] if jg == 1 else into[:],
                                       pr[:, s % 2, :, :], ALU.add).then_inc(summed[n].sem, 1)

            def fold(b, n, ic, into):
                pool.wait_ge(summed[n].sem, summed[n].at(b, 3 * (ic + 1)))
                pool.tensor_tensor(into[:, 0, :], into[:, 0, :], into[:, 1, :], ALU.add).then_inc(folded[n].sem, 1)

            def sums(b, n):
                for ic in range(IC):
                    for jg in range(4):
                        add_step(b, n, 4 * ic + jg, acc)
                        yield from idle(STEP_SLOTS[n])
                    fold(b, n, ic, acc)
                    yield from idle(3)

            def front(b):
                pool.dma_start(x_in[:], x_v[b]).then_inc(x_loaded.sem, 16)
                yield from idle(2 + NT + 1)
                for s in range(STEPS):
                    ic = s // 4
                    add_step(b, 0, s, acc0[ic])
                    if s % 4 == 3:
                        fold(b, 0, ic, acc0[ic])
                    yield from idle(STEP_SLOTS[0])
                yield from idle(8)
                for _ in range(3 + NT + 1):
                    yield
                yield from sums(b, 1)
                for _ in range(7 + NT + 1):
                    yield
                yield from sums(b, 2)
                yield

            def back(b):
                for _ in range(3 + 3):
                    yield
                for u in range(CH):
                    for _ in range(QUAD * NT + 2 + (u == 0)):
                        yield
                    for s in range(STEPS3):
                        ic, j = divmod(s, NT)
                        yield
                        if j:
                            n = IC * u + ic
                            pool.wait_ge(exped[3].sem, exped[3].at(b, QUAD * (STEPS3 * u + s) + 4))
                            if j == 1 and n:
                                pool.wait_ge(total[3].sem, total[3].at(b, n))
                            if j > 1:
                                pool.wait_ge(summed_pool.sem, summed_pool.at(b, (NT - 1) * n + j - 1))
                            pool.tensor_tensor(accb[:, 2:4, :], prb[:, (s - 1) % 2, 2:4, :] if j == 1 else
                                               accb[:, 2:4, :], prb[:, s % 2, 2:4, :], ALU.add)\
                                .then_inc(summed_pool.sem, 1)
                        yield
                    yield
                    yield
                for _ in range(4):
                    yield

            alone(front(0), FRONT_SLOTS)
            with pool.Fori(0, B - 1) as b:
                pool.wait_ge(weighed[2].sem, weighed[2].at(b, STEPS))
                by_turns(front(b + 1), back(b))
            alone(back(B - 1), BACK_SLOTS)

        @block.tensor
        def _(pe):
            pe.wait_ge(loaded.sem, 16 * 6)
            pe.wait_ge(setup_pool.sem, 5)
            for ch in range(CH):
                mm = pe.matmul(ps[:, 0, 0:1], ones_over_c[:], vcol("bo3", ch), start=ch == 0, stop=ch == CH - 1)
            mm.then_inc(setup_pe.sem, 1)
            pe.wait_ge(setup_dve.sem, 12)

            def project(bank, name, src, m0, m, ic):
                for kt in range(CH):
                    mm = pe.matmul(ps[0:m, bank, :], wcol(name, kt, m0, m), src[:, kt, cols(ic)],
                                   start=kt == 0, stop=kt == CH - 1)
                return mm

            def values(name, src, bank, half):
                for t in range(4):
                    for kt in range(CH):
                        mm = pe.matmul(ps[:, bank + t // 2, (t % 2) * C:(t % 2 + 1) * C],
                                       src[:, kt, tile(4 * half + t)], wcol(name, kt, 0, C),
                                       start=kt == 0, stop=kt == CH - 1)
                return mm

            def max_tile(b, n, count, queries, keys, it, bank):
                if count >= 2:
                    pe.wait_ge(max_sb[n].sem, max_sb[n].at(b, count - 1))
                for jc in range(IC):
                    mm = pe.matmul(ps[:, bank + jc, :], queries[0:STACK, tile(it)], keys[0:STACK, cols(jc)],
                                   start=True, stop=True)
                mm.then_inc(max_ps[n].sem, 1)

            def shift_rows(n, side, head, bank):
                for it in range(NT):
                    mm = pe.matmul(ps[:, bank + it // 4, tile(it % 4)],
                                   nmx_r[side][:, head, it:it + 1].broadcast_to([P, P]), ident_r[:],
                                   start=True, stop=True)
                mm.then_inc(shift_ps[n].sem, 1)

            def stacked_scores(bank, queries, keys, jt, ic):
                return pe.matmul(ps[:, bank, :], keys[0:ROW + 1, tile(jt)], queries[0:ROW + 1, cols(ic)],
                                 start=True, stop=True)

            def stacks_and_maxima(b, n, names, src, extra):
                for k, name in enumerate(names):
                    for ic in range(IC):
                        mm = project(2 * k + ic, name, src, 0, STACK, ic)
                    mm.then_inc(qk_ps[n].sem, 1)
                yield
                yield from extra
                for it in range(NT):
                    max_tile(b, n, it, qs01, ks01, it, 2 * (it % 2))
                    yield
                pe.wait_ge(max_r[n].sem, max_r[n].at(b, 1))
                shift_rows(n, "front", 0, 0)
                yield

            def scores01(b, n, s):
                ic, jg = divmod(s, 4)
                if s == 0:
                    pe.wait_ge(shift_sb[n].sem, shift_sb[n].at(b, 1))
                else:
                    pe.wait_ge(exped[n].sem, exped[n].at(b, s))
                for j in range(2):
                    mm = stacked_scores(j, qs01, ks01, 2 * jg + j, ic)
                mm.then_inc(scored[n].sem, 1)

            def layer0(b, last):
                if last is not None:
                    pe.wait_ge(l2_res.sem, l2_res.at(last, 4))
                pe.wait_ge(x_loaded.sem, x_loaded.at(b, 16))

                def values0():
                    pe.wait_ge(qk_lo[0].sem, qk_lo[0].at(b, 1))
                    for jt in range(NT):
                        for kt in range(CH):
                            mm = pe.matmul(ps[:, 0, jt * L:(jt + 1) * L], x_in[:, kt, tile(jt)],
                                           wcol("g", kt, 0, L), start=kt == 0, stop=kt == CH - 1)
                    mm.then_inc(l0_g.sem, 1)
                    yield
                    pe.wait_ge(l0_v.sem, l0_v.at(b, 1))
                    pe.wait_ge(qk_lo[0].sem, qk_lo[0].at(b, 2))

                yield from stacks_and_maxima(b, 0, ("theta", "phi"), x_in, values0())

                def weigh(s):
                    ic, jg = divmod(s, 4)
                    pe.wait_ge(exped[0].sem, exped[0].at(b, s + 1))
                    for j in range(2):
                        jt = 2 * jg + j
                        g = jt % QUAD
                        mm = pe.matmul(ps[L * g:L * g + L, 2 + ic, :], vg[:, jt, :], pr[:, s % 2, j, :],
                                       start=jt < QUAD, stop=jt >= QUAD, tile_position=(0, L * g))
                    mm.then_inc(weighed[0].sem, 1)

                def add_parts():
                    pe.wait_ge(l0_parts.sem, l0_parts.at(b, 1))
                    for nt in range(NT):
                        pe.matmul(ps[:, 2, nt * (L + 1):nt * (L + 1) + L], lat_parts[:, tile(nt)], ident_quad,
                                  start=True, stop=True)
                    pe.wait_ge(folded[0].sem, folded[0].at(b, IC))
                    for nt in range(NT):
                        mm = pe.matmul(ps[:, 2, nt * (L + 1) + L:(nt + 1) * (L + 1)],
                                       acc0[nt // 4][:, 0, tile(nt % 4)], ones[:, 0:1], start=True, stop=True)
                    mm.then_inc(l0_lat_sum.sem, 1)

                def times_wo(n):
                    pe.wait_ge(l0_lat_in.sem, l0_lat_in.at(b, 16 * (n + 1)))
                    for k in range(4):
                        ic, ch = divmod(k, CH)
                        pe.matmul(ps[:, k, :], wo_con[:, tile(ch)], lat_r[:, cols(ic)],
                                  start=True, stop=True).then_inc(l0_wo.sem, 1)

                for s in range(STEPS):
                    scores01(b, 0, s)
                    yield
                    if s:
                        weigh(s - 1)
                    yield
                weigh(STEPS - 1)
                yield
                add_parts()
                yield
                times_wo(0)
                yield
                pe.wait_ge(l0_res.sem, l0_res.at(b, 4))
                for ic in range(IC):
                    mm = project(ic, "theta", xm, 0, L, ic)
                mm.then_inc(l0_enc_ps.sem, 1)
                yield
                pe.wait_ge(l0_enc.sem, l0_enc.at(b, 1))
                for nt in range(NT):
                    mm = pe.matmul(ps[:, 2 + nt // 4, tile(nt % 4)], enc[:, tile(nt)], wo_con[:, C:C + P],
                                   start=True, stop=True)
                mm.then_inc(l0_s2.sem, 1)
                yield
                pe.wait_ge(l0_e2.sem, l0_e2.at(b, 1))
                for nt in range(NT):
                    mm = pe.transpose(ps[:, nt // 4, tile(nt % 4)], e2[:, nt, :], ident)
                mm.then_inc(l0_t2.sem, 1)
                yield
                pe.wait_ge(l0_p2t.sem, l0_p2t.at(b, 1))
                for nt in range(NT):
                    mm = pe.matmul(ps[:, 2, nt * (L + 1):(nt + 1) * (L + 1)], p2t[:, tile(nt)], con1[:],
                                   start=True, stop=True)
                mm.then_inc(l0_lat_sum.sem, 1)
                yield
                times_wo(1)
                yield

            def chunks(b, n, scores):
                for ic in range(IC):
                    def weigh(jg, j):
                        s = 4 * ic + jg
                        if j == 0:
                            pe.wait_ge(exped[n].sem, exped[n].at(b, s + 1))
                            if jg == 0 and ic:
                                pe.wait_ge(normed[n].sem, normed[n].at(b, CH))
                        jt = 2 * jg + j
                        for ch in range(CH):
                            mm = pe.matmul(ps[:, 2 + ch, :], v[:, jt, tile(ch)], pr[:, s % 2, j, :],
                                           start=jt == 0, stop=jt == NT - 1)
                        if j == 1:
                            mm.then_inc(weighed[n].sem, 1)

                    for jg in range(4):
                        if jg == 0 and ic:
                            pe.wait_ge(inverse[n].sem, inverse[n].at(b, ic))
                        yield from scores(4 * ic + jg)
                        for j in range(2):
                            if jg:
                                weigh(jg - 1, j)
                            yield
                    for j in range(2):
                        weigh(3, j)
                        yield
                    pe.wait_ge(folded[n].sem, folded[n].at(b, ic + 1))
                    pe.matmul(ps[:, 0, :], ones[:], acc[:, 0, :], start=True, stop=True).then_inc(total[n].sem, 1)
                    yield

            def values_slots(b, n, name, src, bank, free):
                for half in range(2):
                    free(half)
                    values(name, src, bank + 2 * half, half).then_inc(v_ps[n].sem, 1)
                    yield
                pe.wait_ge(v_sb[n].sem, v_sb[n].at(b, 2))

            def layer1(b):
                pe.wait_ge(l0_res.sem, l0_res.at(b, 8))
                yield from stacks_and_maxima(
                    b, 1, ("q1", "k1"), xm,
                    values_slots(b, 1, "v1", xm, 0, lambda half: pe.wait_ge(qk_lo[1].sem, qk_lo[1].at(b, half + 1))))

                def scores(s):
                    scores01(b, 1, s)
                    yield from ()

                yield from chunks(b, 1, scores)

            def group_norm(b, n, bank):
                g = small_sb[n]
                pe.wait_ge(gn[n]["chan"].sem, gn[n]["chan"].at(b, CH))
                pe.matmul(ps[:, bank, 0:CH], group_avg, g["mv"][:, :, 0], start=True, stop=True)\
                    .then_inc(gn[n]["mean_ps"].sem, 1)
                yield
                pe.wait_ge(gn[n]["var"].sem, gn[n]["var"].at(b, 1))
                pe.matmul(ps[:, bank + 1, 0:CH], group_avg, g["var"][:], start=True, stop=True)\
                    .then_inc(gn[n]["var_ps"].sem, 1)
                yield
                yield
                pe.wait_ge(gn[n]["h"].sem, gn[n]["h"].at(b, CH))

            def layer2(b):
                yield from group_norm(b, 2, 0)
                for name, sig in (("q2", q_ps[2]), ("k2", k_ps[2])):
                    for k in range(4):
                        blk, ic = divmod(k, IC)
                        if name == "k2":
                            pe.wait_ge(q_lo[2].sem, q_lo[2].at(b, k + 1))
                        project(k, name, h, P * blk, P, ic).then_inc(sig.sem, 1)
                    yield
                yield from values_slots(b, 2, "v2", h, 0,
                                        lambda half: pe.wait_ge(k_lo[2].sem, k_lo[2].at(b, 2 * (half + 1))))
                for it in range(NT):
                    if it >= 2:
                        pe.wait_ge(max_sb[2].sem, max_sb[2].at(b, it - 1))
                    for jc in range(IC):
                        for kt in range(CH):
                            mm = pe.matmul(ps[:, 2 * (it % 2) + jc, :], qh2[:, kt, tile(it)], kh2[:, kt, cols(jc)],
                                           start=kt == 0, stop=kt == CH - 1)
                    mm.then_inc(max_ps[2].sem, 1)
                    yield
                pe.wait_ge(max_r[2].sem, max_r[2].at(b, 1))
                shift_rows(2, "front", 0, 0)
                yield

                def scores(s):
                    ic, jg = divmod(s, 4)
                    if s == 0:
                        pe.wait_ge(shift_sb[2].sem, shift_sb[2].at(b, 1))
                    else:
                        pe.wait_ge(exped[2].sem, exped[2].at(b, s))
                    for j in range(2):
                        keys = tile(2 * jg + j)
                        pe.matmul(ps[:, j, :], ones_over_p[:], shift[:, cols(ic)], start=True, stop=False)
                        for kt in range(CH):
                            for kpart, qpart in ((kh2, qh2), (kh2, ql2), (kl2, qh2)):
                                mm = pe.matmul(ps[:, j, :], kpart[:, kt, keys], qpart[:, kt, cols(ic)],
                                               start=False, stop=kt == CH - 1 and kpart is kl2)
                        if j == 1:
                            mm.then_inc(scored[2].sem, 1)
                        yield

                yield from chunks(b, 2, scores)
                pe.wait_ge(normed[2].sem, normed[2].at(b, 4))
                for k in range(4):
                    ic, ch = divmod(k, CH)
                    project(k, "o2", h, P * ch, P, ic).then_inc(l2_proj.sem, 1)
                yield

            def front(b, last=None):
                yield from layer0(b, last)
                yield from layer1(b)
                yield from layer2(b)

            def back(b):
                yield from group_norm(b, 3, back0)

                def queries_and_keys(blk):
                    for base, name, sig in ((0, "q3", q_ps[3]), (2, "k3", k_ps[3])):
                        for ic in range(IC):
                            project(back0 + base + ic, name, hb, P * blk, P, ic).then_inc(sig.sem, 1)

                queries_and_keys(0)
                yield
                for half in range(2):
                    done = (q_lo, k_lo)[half][3]
                    pe.wait_ge(done.sem, done.at(b, IC))
                    values("v3", hb, back0 + 2 * half, half).then_inc(v_ps[3].sem, 1)
                    yield
                pe.wait_ge(v_sb[3].sem, v_sb[3].at(b, 2))
                for u in range(CH):
                    pe.wait_ge(stacked[u].sem, stacked[u].at(b, 16 * 6 * QUAD))
                    for k in range(QUAD * NT):
                        g, it = divmod(k, NT)
                        if u and k == 1:
                            pe.wait_ge(taken.sem, taken.at(b, IC * u))
                            pe.wait_ge(inverse[3].sem, inverse[3].at(b, IC * u))
                        max_tile(b, 3, QUAD * NT * u + k, qs[:, g, :], ks[:, g, :], it, back0 + 2 * (k % 2))
                        yield
                    pe.wait_ge(max_r[3].sem, max_r[3].at(b, u + 1))
                    if u == 0:
                        queries_and_keys(1)
                        yield
                        pe.wait_ge(q_lo[3].sem, q_lo[3].at(b, 2 * IC))
                        pe.wait_ge(k_lo[3].sem, k_lo[3].at(b, 2 * IC))
                    for g in range(QUAD):
                        if g >= 2:
                            pe.wait_ge(shift_sb[3].sem, shift_sb[3].at(b, QUAD * u + g - 1))
                        shift_rows(3, "back", g, back0 + 2 * (g % 2))
                        if g % 2:
                            yield
                    pe.wait_ge(shift_sb[3].sem, shift_sb[3].at(b, QUAD * (u + 1)))

                    def take_turn(use):
                        if use >= 3:
                            done, count = bank_use(u, use - 3)
                            pe.wait_ge(done.sem, done.at(b, count))
                        return turn3[use % 3]

                    def scores(s, pair):
                        ic, jt = divmod(s, NT)
                        for g in (2 * pair, 2 * pair + 1):
                            bank = take_turn(score_use(s, g))
                            stacked_scores(bank, qs[:, g, :], ks[:, g, :], jt, ic).then_inc(scored[3].sem, 1)

                    def weigh(s):
                        ic, jt = divmod(s, NT)
                        n = STEPS3 * u + s
                        pe.wait_ge(exped[3].sem, exped[3].at(b, QUAD * (n + 1)))
                        if jt == 0 and n:
                            pe.wait_ge(taken.sem, taken.at(b, n // NT))
                        for g in range(QUAD):
                            mm = pe.matmul(ps[L * g:L * g + L, back0 + 2, :],
                                           vb[:, jt, L * (QUAD * u + g):L * (QUAD * u + g + 1)],
                                           prb[:, s % 2, g, :], start=jt == 0, stop=jt == NT - 1,
                                           tile_position=(0, L * g))
                        mm.then_inc(weighed[3].sem, 1)

                    def sum_weights(ic):
                        n = IC * u + ic
                        pe.wait_ge(summed_dve.sem, summed_dve.at(b, (NT - 1) * (n + 1)))
                        pe.wait_ge(summed_pool.sem, summed_pool.at(b, (NT - 1) * (n + 1)))
                        bank = take_turn(total_use(ic))
                        for g in range(QUAD):
                            mm = pe.matmul(ps[L * g:L * g + L, bank, :], ones[:, 0:L], accb[:, g, :],
                                           start=True, stop=True, tile_position=(0, L * g))
                        mm.then_inc(total[3].sem, 1)

                    for s in range(STEPS3):
                        scores(s, 0)
                        if s:
                            weigh(s - 1)
                        yield
                        scores(s, 1)
                        if s == NT + 1:
                            sum_weights(0)
                        yield
                    weigh(STEPS3 - 1)
                    yield
                    sum_weights(1)
                    yield
                for ic in range(IC):
                    pe.wait_ge(normed[3].sem, normed[3].at(b, 3 + ic))
                    for ch in range(CH):
                        project(back0 + 2 * ic + ch, "o3", hb, P * ch, P, ic).then_inc(l3_proj.sem, 1)
                    yield
                for ic in range(IC):
                    pe.wait_ge(l3_sq.sem, l3_sq.at(b, CH * (ic + 1)))
                    for ch in range(CH):
                        mm = pe.matmul(ps[:, back0 + 2 * ic, :], ones_over_c[:], sq[:, ch, cols(ic)],
                                       start=ch == 0, stop=ch == CH - 1)
                    mm.then_inc(l3_var.sem, 1)
                    if ic == 0:
                        yield
                pe.wait_ge(l3_std.sem, l3_std.at(b, IC))
                yield

            alone(front(0), FRONT_SLOTS)
            with pe.Fori(0, B - 1) as b:
                by_turns(front(b + 1, b), back(b))
            alone(back(B - 1), BACK_SLOTS)

        @block.scalar
        def _(act):
            act.wait_ge(loaded.sem, 16 * 6)
            act.wait_ge(setup_pool.sem, 5)
            act.wait_ge(setup_dve.sem, 12)

            def idle(n):
                for _ in range(n):
                    yield

            def to_stacks(b, n, biases):
                for k, (dst, bias) in enumerate(zip((qs01, ks01), biases)):
                    act.wait_ge(qk_ps[n].sem, qk_ps[n].at(b, k + 1))
                    src, into = ps[0:STACK, 2 * k:2 * k + 2, :], dst[0:STACK, :]
                    if bias is None:
                        act.activation(into, src, ACT.Copy).then_inc(qk_hi[n].sem, 1)
                    else:
                        act.activation(into, src, ACT.Identity, bias=vcol(bias)[0:STACK, :])\
                            .then_inc(qk_hi[n].sem, 1)
                yield

            def shift_row(b, n, count, queries, bank):
                act.wait_ge(shift_ps[n].sem, shift_ps[n].at(b, count + 1))
                act.activation(queries[ROW:ROW + 1, :], ps[ROW:ROW + 1, bank:bank + 2, :], ACT.Copy)\
                    .then_inc(shift_sb[n].sem, 1)

            def exps(b, n, s):
                act.wait_ge(scored[n].sem, scored[n].at(b, s + 1))
                if s >= 2:
                    act.wait_ge(weighed[n].sem, weighed[n].at(b, s - 1))
                    ic, jg = divmod(s - 2, 4)
                    act.wait_ge(summed[n].sem, summed[n].at(b, 3 * ic + max(jg, 1)))
                act.activation(pr[:, s % 2, :, :], ps[:, 0:2, :], ACT.Exp).then_inc(exped[n].sem, 1)

            def group_std(b, n, bank):
                yield
                act.wait_ge(gn[n]["var_ps"].sem, gn[n]["var_ps"].at(b, 1))
                act.activation(small_sb[n]["std"][:], ps[:, bank + 1, 0:CH], ACT.Sqrt, bias=eps[:])\
                    .then_inc(gn[n]["std"].sem, 1)
                yield
                yield

            def high_parts(b, n, blk, ic, which, bank, bias, dst):
                ready, done = ((q_ps, q_hi), (k_ps, k_hi))[which]
                act.wait_ge(ready[n].sem, ready[n].at(b, IC * blk + ic + 1))
                act.activation(dst, ps[:, bank, :], ACT.Identity, bias=vcol(bias, blk)).then_inc(done[n].sem, 1)

            def front(b):
                yield from to_stacks(b, 0, (None, None))
                yield from idle(1 + NT)
                shift_row(b, 0, 0, qs01, 0)
                yield
                for s in range(STEPS):
                    exps(b, 0, s)
                    yield from idle(STEP_SLOTS[0])
                act.wait_ge(weighed[0].sem, weighed[0].at(b, STEPS))
                act.activation(lat_parts, ps[:, 2:4, :], ACT.Copy).then_inc(l0_parts.sem, 1)
                yield
                yield from idle(2)
                act.wait_ge(l0_enc_ps.sem, l0_enc_ps.at(b, 1))
                act.activation(enc, ps[0:L, 0:2, :], ACT.Copy).then_inc(l0_enc.sem, 1)
                yield
                act.wait_ge(l0_d2.sem, l0_d2.at(b, 1))
                act.activation(e2, e2, ACT.Exp).then_inc(l0_e2.sem, 1)
                yield
                act.wait_ge(l0_t2.sem, l0_t2.at(b, 1))
                act.activation(p2t, ps[:, 0:2, :], ACT.Copy).then_inc(l0_p2t.sem, 1)
                yield
                yield from idle(2)
                yield from to_stacks(b, 1, ("bq1", "bk1"))
                yield from idle(2 + NT)
                shift_row(b, 1, 0, qs01, 0)
                yield
                for s in range(STEPS):
                    exps(b, 1, s)
                    yield from idle(STEP_SLOTS[1])
                    if s % 4 == 3:
                        yield from idle(3)
                yield from group_std(b, 2, 0)
                for which, bias, dst in ((0, "bq2", qh2), (1, "bk2", kh2)):
                    for k in range(4):
                        blk, ic = divmod(k, IC)
                        high_parts(b, 2, blk, ic, which, k, bias, dst[:, blk, cols(ic)])
                    yield
                yield from idle(2 + NT)
                act.wait_ge(shift_ps[2].sem, shift_ps[2].at(b, 1))
                act.activation(shift[:], ps[:, 0:2, :], ACT.Copy).then_inc(shift_sb[2].sem, 1)
                yield
                for s in range(STEPS):
                    yield
                    exps(b, 2, s)
                    yield from idle(STEP_SLOTS[2] - 1)
                    if s % 4 == 3:
                        yield from idle(3)
                yield

            def back(b):
                yield from group_std(b, 3, back0)

                def queries_and_keys(blk):
                    for which, bias in ((0, "bq3"), (1, "bk3")):
                        for ic in range(IC):
                            high_parts(b, 3, blk, ic, which, back0 + 2 * which + ic, bias,
                                       part[:, 2 * which, cols(ic)])
                    yield

                def exps3(u, s, pair):
                    n = STEPS3 * u + s
                    for g in (2 * pair, 2 * pair + 1):
                        act.wait_ge(scored[3].sem, scored[3].at(b, QUAD * n + g + 1))
                        if n >= 2 and g == 2 * pair:
                            act.wait_ge(weighed[3].sem, weighed[3].at(b, n - 1))
                            chunk, j = divmod(n - 2, NT)
                            used = (NT - 1) * chunk + max(j, 1)
                            sig = (summed_dve, summed_pool)[pair]
                            act.wait_ge(sig.sem, sig.at(b, used))
                        if n == g == 0:
                            act.wait_ge(stored.sem, stored.at(b, 1))
                        act.activation(prb[:, s % 2, g, :], ps[:, turn3[score_use(s, g) % 3], :], ACT.Exp)\
                            .then_inc(exped[3].sem, 1)

                def take(u, ic):
                    n = IC * u + ic
                    act.wait_ge(weighed[3].sem, weighed[3].at(b, NT * (n + 1)))
                    act.activation(hb[:, u, cols(ic)], ps[:, back0 + 2, :], ACT.Copy).then_inc(taken.sem, 1)

                yield from queries_and_keys(0)
                yield from idle(2)
                for u in range(CH):
                    yield from idle(QUAD * NT)
                    if u == 0:
                        act.wait_ge(stacked[0].sem, stacked[0].at(b, 16 * 6 * QUAD))
                        yield from queries_and_keys(1)
                    for g in range(QUAD):
                        shift_row(b, 3, QUAD * u + g, qs[:, g, :], back0 + 2 * (g % 2))
                        if g % 2:
                            yield
                    for s in range(STEPS3):
                        exps3(u, s, 0)
                        if s == NT:
                            take(u, 0)
                        yield
                        exps3(u, s, 1)
                        yield
                    take(u, 1)
                    yield
                    yield
                for ic in range(IC):
                    for ch in range(CH):
                        bank = back0 + 2 * ic + ch
                        act.wait_ge(l3_proj.sem, l3_proj.at(b, CH * ic + ch + 1))
                        act.activation(y[:, ch, cols(ic)], ps[:, bank, :], ACT.Identity, bias=vcol("bo3", ch))\
                            .then_inc(l3_y.sem, 1)
                        act.activation(sq[:, ch, cols(ic)], ps[:, bank, :], ACT.Square, bias=vcol("bo3", ch))\
                            .then_inc(l3_sq.sem, 1)
                    yield

                def finish(ic):
                    for ch in range(CH):
                        act.wait_ge(l3_g.sem, l3_g.at(b, CH * ic + ch + 1))
                        act.activation(y[:, ch, cols(ic)], y[:, ch, cols(ic)], ACT.Identity, bias=vcol("ln_b", ch))\
                            .then_inc(l3_out.sem, 1)

                for ic in range(IC):
                    act.wait_ge(l3_var.sem, l3_var.at(b, ic + 1))
                    act.activation(rstd[:, ic, :], ps[:, back0 + 2 * ic, :], ACT.Sqrt, bias=eps[:])\
                        .then_inc(l3_std.sem, 1)
                    finish(ic)
                    yield

            alone(front(0), FRONT_SLOTS)
            with act.Fori(0, B - 1) as b:
                by_turns(front(b + 1), back(b))
            alone(back(B - 1), BACK_SLOTS)

        @block.vector
        def _(dve):
            dve.wait_ge(loaded.sem, 16 * 6)
            dve.tensor_copy(ident_r[:], ident).then_inc(setup_dve.sem, 1)
            dve.memset(bf32(ks[ROW:ROW + 1, :, :]), 1.0).then_inc(setup_dve.sem, 1)
            dve.memset(bf32(ks01[ROW:ROW + 1, :]), 1.0).then_inc(setup_dve.sem, 1)

            def scale(ap, factor):
                dve.tensor_scalar(ap, ap, factor, None, ALU.mult).then_inc(setup_dve.sem, 1)

            scale(w[:, :, W_COLS["theta"].start:W_COLS["g"].stop], C ** -0.5)
            scale(wo_con[:, 0:C], L ** -0.5)
            scale(w[:, :, W_COLS["q2"]], C ** -0.5)
            scale(w[:, :, W_COLS["q3"]], L ** -0.25)
            scale(vec[:, V_COLS["bq2"]], C ** -0.5)
            scale(vec[:, V_COLS["bq3"]], L ** -0.25)
            dve.tensor_reduce(wo_mean[:], w[:, :, W_COLS["o3"]], AX.X, ALU.add, negate=True)\
                .then_inc(setup_mean.sem, 1)
            dve.wait_ge(setup_mean.sem, 1)
            dve.tensor_scalar(wo_mean[:], wo_mean[:], 1.0 / C, None, ALU.mult).then_inc(setup_dve.sem, 1)
            dve.wait_ge(setup_dve.sem, 10)
            dve.tensor_tensor(w[:, :, W_COLS["o3"]], w[:, :, W_COLS["o3"]],
                              wo_mean[:].unsqueeze(2).broadcast_to([P, CH, C]), ALU.add).then_inc(setup_dve.sem, 1)
            dve.wait_ge(setup_pe.sem, 1)
            dve.tensor_scalar(vec[:, V_COLS["bo3"]], vec[:, V_COLS["bo3"]], ps[:, 0, 0:1], None, ALU.subtract)\
                .then_inc(setup_dve.sem, 1)

            def idle(n):
                for _ in range(n):
                    yield

            def low_stacks(b, n, biases):
                for k, (dst, r, bias) in enumerate(zip((qs01, ks01), (1, 2), biases)):
                    dve.wait_ge(qk_hi[n].sem, qk_hi[n].at(b, k + 1))
                    rows = slice(L * r, L * r + L)
                    into = dst[rows, :].rearrange("p (i n) -> p i n", i=IC)
                    src = ps[rows, 2 * k:2 * k + 2, :]
                    if bias is None:
                        dve.tensor_tensor(into, src, bf32(into), ALU.subtract).then_inc(qk_lo[n].sem, 1)
                    else:
                        dve.scalar_tensor_tensor(out=into, in0=src, scalar=vcol(bias)[rows, :], in1=bf32(into),
                                                 op0=ALU.add, op1=ALU.subtract).then_inc(qk_lo[n].sem, 1)
                yield

            def low_parts(b, n, blk, ic, which, bank, bias, hi, dst):
                ready, done = ((q_hi, q_lo), (k_hi, k_lo))[which]
                dve.wait_ge(ready[n].sem, ready[n].at(b, IC * blk + ic + 1))
                dve.scalar_tensor_tensor(out=dst, in0=ps[:, bank, :], scalar=vcol(bias, blk), in1=bf32(hi),
                                         op0=ALU.add, op1=ALU.subtract).then_inc(done[n].sem, 1)

            def maximum(b, n, count, side, head, it, bank):
                dve.wait_ge(max_ps[n].sem, max_ps[n].at(b, count + 1))
                dve.tensor_reduce(nmx[side][:, head, it:it + 1], ps[:, bank:bank + 2, :], AX.XY, ALU.max,
                                  negate=True).then_inc(max_sb[n].sem, 1)

            def round_maxima(b, n, side, u=0):
                count = NT * (QUAD if side == "back" else 1)
                dve.wait_ge(max_sb[n].sem, max_sb[n].at(b, count * (u + 1)))
                dve.tensor_copy(nmx_r[side][:], nmx[side][:]).then_inc(max_r[n].sem, 1)

            def maxima(b, n):
                for it in range(NT):
                    maximum(b, n, it, "front", 0, it, 2 * (it % 2))
                    if it == NT - 1:
                        round_maxima(b, n, "front")
                    yield

            def latents(b, n):
                sums = ps[:, 2, 0:NT * (L + 1)].rearrange("p (n c) -> p n c", n=NT)
                dve.reciprocal(rlat[:], sums[:, :, L]).then_inc(l0_rlat.sem, 1)
                dve.wait_ge(l0_rlat.sem, l0_rlat.at(b, n + 1))
                dve.tensor_tensor(lat, sums[:, :, 0:L], rlat[:].unsqueeze(2).broadcast_to([P, NT, L]),
                                  ALU.mult).then_inc(l0_lat.sem, 1)

            def residual0(b, n, last=None):
                src, gamma = ((x_in, "gamma_sa"), (xm, "gamma_moca"))[n]
                if n == 0 and last is not None:
                    dve.wait_ge(xd_copied.sem, xd_copied.at(last, 16))
                for k in range(4):
                    ic, ch = divmod(k, CH)
                    dve.wait_ge(l0_wo.sem, l0_wo.at(b, 4 * n + k + 1))
                    dve.scalar_tensor_tensor(out=xm[:, ch, cols(ic)], in0=ps[:, k, :], scalar=vcol(gamma),
                                             in1=src[:, ch, cols(ic)], op0=ALU.mult, op1=ALU.add)\
                        .then_inc(l0_res.sem, 1)
                yield

            def take_values(b, n, dst, bank):
                for half in range(2):
                    dve.wait_ge(v_ps[n].sem, v_ps[n].at(b, half + 1))
                    base = bank + 2 * half
                    dve.tensor_tensor(dst[:, 4 * half:4 * half + 4, :].rearrange("p (k a) c -> p k a c", a=2),
                                      ps[:, base:base + 2, :].rearrange("p k (a c) -> p k a c", a=2),
                                      vbias[:, n - 1, :].unsqueeze(1).unsqueeze(1).broadcast_to([P, 2, 2, C]),
                                      ALU.add).then_inc(v_sb[n].sem, 1)
                    yield

            def chunks(b, n):
                for ic in range(IC):
                    yield from idle(4 * STEP_SLOTS[n] + 2)
                    dve.wait_ge(total[n].sem, total[n].at(b, ic + 1))
                    dve.reciprocal(rden[:], ps[:, 0, :]).then_inc(inverse[n].sem, 1)
                    dve.wait_ge(inverse[n].sem, inverse[n].at(b, ic + 1))
                    for ch in range(CH):
                        dve.tensor_tensor(h[:, ch, cols(ic)], ps[:, 2 + ch, :], rden[:], ALU.mult)\
                            .then_inc(normed[n].sem, 1)
                    if n == 1:
                        for ch in range(CH):
                            dve.wait_ge(normed[1].sem, normed[1].at(b, CH * ic + ch + 1))
                            dve.scalar_tensor_tensor(out=xm[:, ch, cols(ic)], in0=h[:, ch, cols(ic)],
                                                     scalar=vcol("gamma1"), in1=xm[:, ch, cols(ic)],
                                                     op0=ALU.mult, op1=ALU.add).then_inc(l1_res.sem, 1)
                    yield

            def group_norm(b, n, src, dst, ready, bank):
                sig, g = gn[n], small_sb[n]
                for k in range(4):
                    ic, ch = divmod(k, CH)
                    dve.wait_ge(ready.sem, ready.at(b, k + 1))
                    dve.bn_stats(g["bst"][:, ch, ic, :], src[:, ch, cols(ic)])
                dve.drain()
                for ch in range(CH):
                    dve.bn_aggr(g["mv"][:, ch, :], g["bst"][:, ch, :, :]).then_inc(sig["chan"].sem, 1)
                yield
                dve.wait_ge(sig["mean_ps"].sem, sig["mean_ps"].at(b, 1))
                dve.tensor_copy(g["mean"][:], ps[:, bank, 0:CH]).then_inc(sig["mean"].sem, 1)
                dve.wait_ge(sig["mean"].sem, sig["mean"].at(b, 1))
                dve.tensor_tensor(g["dev"][:], g["mv"][:, :, 0], g["mean"][:], ALU.subtract)\
                    .then_inc(sig["dev"].sem, 1)
                dve.wait_ge(sig["dev"].sem, sig["dev"].at(b, 1))
                dve.tensor_tensor(g["dev_sq"][:], g["dev"][:], g["dev"][:], ALU.mult).then_inc(sig["dev_sq"].sem, 1)
                dve.wait_ge(sig["dev_sq"].sem, sig["dev_sq"].at(b, 1))
                dve.tensor_tensor(g["var"][:], g["dev_sq"][:], g["mv"][:, :, 1], ALU.add).then_inc(sig["var"].sem, 1)
                yield
                dve.wait_ge(sig["std"].sem, sig["std"].at(b, 1))
                dve.reciprocal(g["inv"][:], g["std"][:]).then_inc(sig["inv"].sem, 1)
                dve.wait_ge(sig["inv"].sem, sig["inv"].at(b, 1))
                dve.tensor_tensor(g["scale"][:], g["inv"][:], vec[:, V_COLS[f"gn_w{n}"]], ALU.mult)\
                    .then_inc(sig["scale"].sem, 1)
                dve.wait_ge(sig["scale"].sem, sig["scale"].at(b, 1))
                dve.tensor_tensor(g["ms"][:], g["mean"][:], g["scale"][:], ALU.mult).then_inc(sig["ms"].sem, 1)
                dve.wait_ge(sig["ms"].sem, sig["ms"].at(b, 1))
                dve.tensor_tensor(g["bias"][:], vec[:, V_COLS[f"gn_b{n}"]], g["ms"][:], ALU.subtract)\
                    .then_inc(sig["bias"].sem, 1)
                dve.wait_ge(sig["bias"].sem, sig["bias"].at(b, 1))
                for ch in range(CH):
                    dve.tensor_scalar(dst[:, ch, :], src[:, ch, :], g["scale"][:, ch:ch + 1],
                                      g["bias"][:, ch:ch + 1], ALU.mult, ALU.add).then_inc(sig["h"].sem, 1)
                yield

            def front(b, last=None):
                yield from low_stacks(b, 0, (None, None))
                dve.wait_ge(l0_g.sem, l0_g.at(b, 1))
                dve.tensor_copy(vg[:], ps[:, 0, 0:NT * L].rearrange("p (n c) -> p n c", n=NT))\
                    .then_inc(l0_v.sem, 1)
                yield
                yield from maxima(b, 0)
                yield from idle(1 + STEP_SLOTS[0] * STEPS + 1)
                dve.wait_ge(l0_lat_sum.sem, l0_lat_sum.at(b, 1))
                latents(b, 0)
                yield
                yield from residual0(b, 0, last)
                yield
                dve.wait_ge(l0_s2.sem, l0_s2.at(b, 1))
                s2 = ps[:, 2:4, :].rearrange("p i (n c) -> p (i n) c", n=4)
                dve.tensor_reduce(m2[:], s2, AX.X, ALU.max).then_inc(l0_m2.sem, 1)
                dve.wait_ge(l0_m2.sem, l0_m2.at(b, 1))
                dve.tensor_tensor(e2, s2, m2[:].unsqueeze(2).broadcast_to([P, NT, P]), ALU.subtract)\
                    .then_inc(l0_d2.sem, 1)
                yield
                yield
                dve.wait_ge(l0_lat_sum.sem, l0_lat_sum.at(b, 2))
                latents(b, 1)
                yield
                yield from residual0(b, 1)
                yield from low_stacks(b, 1, ("bq1", "bk1"))
                yield from take_values(b, 1, v, 0)
                yield from maxima(b, 1)
                yield
                yield from chunks(b, 1)
                yield from group_norm(b, 2, xm, h, l1_res, 0)
                for which, bias, hi, lo in ((0, "bq2", qh2, ql2), (1, "bk2", kh2, kl2)):
                    for k in range(4):
                        blk, ic = divmod(k, IC)
                        low_parts(b, 2, blk, ic, which, k, bias, hi[:, blk, cols(ic)], lo[:, blk, cols(ic)])
                    yield
                yield from take_values(b, 2, v, 0)
                yield from maxima(b, 2)
                yield
                yield from chunks(b, 2)
                for k in range(4):
                    ic, ch = divmod(k, CH)
                    dve.wait_ge(l2_proj.sem, l2_proj.at(b, k + 1))
                    dve.scalar_tensor_tensor(out=xm[:, ch, cols(ic)], in0=ps[:, k, :], scalar=vcol("bo2", ch),
                                             in1=xm[:, ch, cols(ic)], op0=ALU.add, op1=ALU.add)\
                        .then_inc(l2_res.sem, 1)
                yield

            def back(b):
                yield from group_norm(b, 3, xm, hb, l2_res, back0)

                def queries_and_keys(blk):
                    for which, bias in ((0, "bq3"), (1, "bk3")):
                        for ic in range(IC):
                            low_parts(b, 3, blk, ic, which, back0 + 2 * which + ic, bias,
                                      part[:, 2 * which, cols(ic)], part[:, 2 * which + 1, cols(ic)])
                    yield

                def add_weights(u, s):
                    ic, j = divmod(s, NT)
                    n = IC * u + ic
                    if j:
                        dve.wait_ge(exped[3].sem, exped[3].at(b, QUAD * (STEPS3 * u + s) + 2))
                        if j == 1 and n:
                            dve.wait_ge(total[3].sem, total[3].at(b, n))
                        if j > 1:
                            dve.wait_ge(summed_dve.sem, summed_dve.at(b, (NT - 1) * n + j - 1))
                        dve.tensor_tensor(accb[:, 0:2, :], prb[:, (s - 1) % 2, 0:2, :] if j == 1 else
                                          accb[:, 0:2, :], prb[:, s % 2, 0:2, :], ALU.add)\
                            .then_inc(summed_dve.sem, 1)

                def normalise(u, ic):
                    n = IC * u + ic
                    dve.wait_ge(total[3].sem, total[3].at(b, n + 1))
                    dve.reciprocal(rdenb[:], ps[:, turn3[total_use(ic) % 3], :]).then_inc(inverse[3].sem, 1)
                    dve.wait_ge(taken.sem, taken.at(b, n + 1))
                    dve.wait_ge(inverse[3].sem, inverse[3].at(b, n + 1))
                    dve.tensor_tensor(hb[:, u, cols(ic)], hb[:, u, cols(ic)], rdenb[:], ALU.mult)\
                        .then_inc(normed[3].sem, 1)

                yield from queries_and_keys(0)
                yield from take_values(b, 3, vb, back0)
                for u in range(CH):
                    for k in range(QUAD * NT):
                        g, it = divmod(k, NT)
                        maximum(b, 3, QUAD * NT * u + k, "back", g, it, back0 + 2 * (k % 2))
                        if k == QUAD * NT - 1:
                            round_maxima(b, 3, "back", u)
                        yield
                    if u == 0:
                        yield from queries_and_keys(1)
                    yield from idle(2)
                    for s in range(STEPS3):
                        if s == NT + 2:
                            normalise(u, 0)
                        yield
                        add_weights(u, s)
                        yield
                    yield
                    normalise(u, 1)
                    yield
                yield from idle(2)
                dve.wait_ge(xd_copied.sem, xd_copied.at(b, 16))
                for ic in range(IC):
                    dve.wait_ge(l3_std.sem, l3_std.at(b, ic + 1))
                    dve.reciprocal(rstd[:, ic, :], rstd[:, ic, :]).then_inc(l3_rstd.sem, 1)
                    dve.wait_ge(l3_rstd.sem, l3_rstd.at(b, ic + 1))
                    for ch in range(CH):
                        k = CH * ic + ch
                        dve.tensor_tensor(y[:, ch, cols(ic)], y[:, ch, cols(ic)], rstd[:, ic, :], ALU.mult)\
                            .then_inc(l3_n.sem, 1)
                        dve.wait_ge(l3_n.sem, l3_n.at(b, k + 1))
                        dve.scalar_tensor_tensor(out=y[:, ch, cols(ic)], in0=y[:, ch, cols(ic)],
                                                 scalar=vcol("ln_w", ch), in1=xd[:, ch, cols(ic)],
                                                 op0=ALU.mult, op1=ALU.add).then_inc(l3_g.sem, 1)
                    yield

            alone(front(0), FRONT_SLOTS)
            with dve.Fori(0, B - 1) as b:
                by_turns(front(b + 1, b), back(b))
            alone(back(B - 1), BACK_SLOTS)


def kernel(**inputs):
    import numpy as np
    import concourse.bacc as bacc
    from concourse.bass_utils import run_bass_kernel_spmd

    a = {k: np.asarray(t) for k, t in inputs.items()}
    three = lambda t: np.concatenate([t] * 3, axis=-1)
    qkv = a["L2_conv_qkv_w"].T
    weights = np.concatenate([
        three(a["L0_conv_w_theta"].T), three(a["L0_conv_w_phi"].T), a["L0_conv_w_g"].T,
        three(a["L1_conv_Wq"].T), three(a["L1_conv_Wk"].T), a["L1_conv_Wv"].T,
        qkv, a["L2_conv_proj_w"].T,
        a["L3_conv_wq"].T, a["L3_conv_wk"].T, a["L3_conv_wv"].T, a["L3_conv_wo"].T], axis=1)
    halves = lambda t: t.reshape(CH, P).T
    column = lambda t: np.concatenate([t, np.zeros(P - len(t), t.dtype)]).reshape(P, 1)
    spread = lambda t: np.broadcast_to(t.reshape(1, 1), (P, 1))
    qkv_b = a["L2_conv_qkv_b"]
    vectors = np.concatenate([
        halves(a["L2_conv_gn_w"]), halves(a["L2_conv_gn_b"]), halves(qkv_b[0:C]), halves(qkv_b[C:2 * C]),
        halves(a["L2_conv_proj_b"]), halves(a["L3_conv_gn_gamma"]), halves(a["L3_conv_gn_beta"]),
        halves(a["L3_conv_bq"]), halves(a["L3_conv_bk"]), halves(a["L3_conv_bo"]),
        halves(a["L3_conv_ln_gamma"]), halves(a["L3_conv_ln_beta"]),
        column(three(a["L1_conv_bq"])), column(three(a["L1_conv_bk"])),
        spread(a["L0_conv_gamma_sa"]), spread(a["L0_conv_gamma_moca"]), spread(a["L1_conv_gamma"])], axis=1)
    value_biases = np.broadcast_to(
        np.stack([a["L1_conv_bv"], qkv_b[2 * C:], a["L3_conv_bv"]])[None], (P, 3, C))
    small = np.concatenate([a["L0_conv_w_o"].T, a["L0_conv_concepts"].T], axis=1)
    concepts = a["L0_conv_concepts"]
    groups = np.kron(np.eye(P // GROUP), np.full((GROUP, GROUP), 1.0 / GROUP))
    constants = np.concatenate([np.eye(P), groups, np.tile(np.eye(L), (QUAD, 1))], axis=1).astype(np.float32)
    x = a["x"].reshape(B, C, T)

    arrays = {"x": x, "weights": weights, "vectors": vectors, "value_biases": value_biases, "small": small,
              "concepts": concepts, "constants": constants}
    arrays = {f"in_{k}": np.ascontiguousarray(t) for k, t in arrays.items()}
    nc = bacc.Bacc("TRN2", target_bir_lowering=False, num_devices=1)
    args = [nc.dram_tensor(k, t.shape, mybir.dt.from_np(t.dtype), kind="ExternalInput").ap()
            for k, t in arrays.items()]
    lat_dram = nc.dram_tensor("latents", (T, L), F32).ap()
    out = nc.dram_tensor("out", (B, C, T), F32, kind="ExternalOutput").ap()
    attention_layers(nc, *args, lat_dram, out)
    r = run_bass_kernel_spmd(nc, [arrays], core_ids=[0])
    return r.results[0]["out"].reshape(B, C, 32, 32)
```

```python
from contextlib import ExitStack
from itertools import zip_longest

import concourse.bass as bass
from concourse import mybir

F32 = mybir.dt.float32
F32R = mybir.dt.float32r
ALU = mybir.AluOpType
ACT = mybir.ActivationFunctionType
AX = mybir.AxisListType

B = 8
C = 256
T = 1024
P = 128
CH = C // P
IC, IW = 2, 512
NT = T // P
L = 32
HEADS = C // L
QUAD = P // L
STACK = 3 * L
ROW = STACK
EPS = 1e-5
GROUP = C // 32

W_COLS = {}
_at = 0
for _name, _n in (("qk0", P), ("g", L), ("qk1", P), ("v1", C),
                  ("q2", C), ("k2", C), ("v2", C), ("o2", C), ("q3", C), ("k3", C), ("v3", C), ("o3", C)):
    W_COLS[_name] = slice(_at, _at + _n)
    _at += _n
W_TOTAL = _at
V_COLS = {}
_at = 0
for _name, _n in (("gn_w2", 2), ("gn_b2", 2), ("bq2", 2), ("bk2", 2), ("bo2", 2), ("gn_w3", 2), ("gn_b3", 2),
                  ("bq3", 2), ("bk3", 2), ("bo3", 2), ("ln_w", 2), ("ln_b", 2), ("bqk1", 1),
                  ("gamma_sa", 1), ("gamma_moca", 1), ("gamma1", 1)):
    V_COLS[_name] = slice(_at, _at + _n)
    _at += _n
V_TOTAL = _at


STEPS = NT
STEPS3 = IC * NT
STEP_SLOTS = {0: 2, 1: 2, 2: 4}
CHUNK_SLOTS = {n: 4 * STEP_SLOTS[n] + 3 for n in (1, 2)}
FRONT_SLOTS = (
    2 + NT + 1 + STEPS * STEP_SLOTS[0] + 2 + 6
    + 3 + NT + 1 + IC * CHUNK_SLOTS[1]
    + 3 + 4 + NT + 1 + IC * CHUNK_SLOTS[2] + 1)
ROUND_SLOTS = QUAD * NT + 2 + 2 * STEPS3 + 2
BACK_SLOTS = 3 + 3 + CH * ROUND_SLOTS + 1 + 4


RUNS = (
    0, 2, 3, 8, 1, 2, 1, 3, 1, 3, 2, 4, 1, 1, 3, 1, 3, 3, 2, 2, 4, 1, 2, 1, 4, 1, 1, 1, 2, 1, 5, 1, 3, 1, 3,
    1, 1, 1, 1, 1, 1, 2, 1, 1, 1, 1, 3, 1, 2, 2, 2, 1, 1, 1, 2, 9, 1, 1, 3, 2, 1, 2, 2, 2, 1, 3, 1, 2, 8, 3,
    2, 1, 2, 1, 2, 1, 2, 1, 3, 6, 5, 2, 2, 1, 1, 1, 2, 2, 2, 1, 1, 1, 2, 2, 2, 2, 2, 2, 1, 1, 2, 1, 1, 1, 1,
    1, 1, 2, 2, 1, 4, 1, 5, 1, 3, 1, 1, 2, 2, 1, 1, 1, 2, 4, 1, 1, 3, 3, 2, 1, 4, 1, 2, 1, 1, 1, 2, 1, 2, 1,
    1)
TURNS = [of_front for n, count in enumerate(RUNS) for of_front in [n % 2 == 1] * count]
assert TURNS.count(True) == FRONT_SLOTS and TURNS.count(False) == BACK_SLOTS


def by_turns(front, back):
    for of_front in TURNS:
        next(front if of_front else back)


def alone(side, slots):
    for _ in range(slots):
        next(side)


def both_rounds(maxima, middle, steps, last):
    yield from maxima(0)
    yield from middle(0)
    if last:
        for _ in zip_longest(steps(0), maxima(1)):
            yield
    else:
        yield from steps(0)
        yield from maxima(1)
    yield from middle(1)
    yield from steps(1)


def finish_alone(side):
    for _ in side:
        pass


class Signal:

    def __init__(self, sem, per_batch):
        self.sem, self.per_batch = sem, per_batch

    def at(self, b, n):
        return b * self.per_batch + n


def attention_layers(nc, x, weights, vectors, value_biases, small, concepts, constants, lat_dram, out):
    with ExitStack() as ctx:
        def sb(name, shape, dt=F32):
            return ctx.enter_context(nc.sbuf_tensor(name, shape, dt))

        def signal(name, per_batch=1):
            return Signal(ctx.enter_context(nc.semaphore(name)), per_batch)

        ps = ctx.enter_context(nc.psum_tensor("ps", [P, 8, IW], F32))
        back0 = 4
        turn3 = (4, 5, 7)

        w = sb("w", [P, CH, W_TOTAL])
        vec = sb("vec", [P, V_TOTAL])
        vbias = sb("vbias", [P, 3, C])
        wo_con = sb("wo_con", [L, C + P])
        con1 = sb("con1", [P, L + 1])
        cst = sb("cst", [P, 2 * P + L])
        ident, group_avg, ident_quad = cst[:, 0:P], cst[:, P:2 * P], cst[:, 2 * P:]
        ident_r = sb("ident_r", [P, P], F32R)
        ones = sb("ones", [P, P])
        ones_over_p = sb("ones_over_p", [P, P], F32R)
        ones_over_c = sb("ones_over_c", [P, P])
        eps = sb("eps", [P, 1])
        wo_mean = sb("wo_mean", [P, CH])

        x_in = sb("x_in", [P, CH, T])
        xm = sb("xm", [P, CH, T])
        h = sb("h", [P, CH, T])
        q2k2 = sb("q2k2", [P, 8, T], F32R)
        ks01 = sb("ks01", [P, T], F32R)
        v = x_in.rearrange("p h (n c) -> p (h n) c", c=C)
        vg = sb("vg", [P, NT, L])
        pr = sb("pr", [P, 2, 2, IW])
        acc = sb("acc", [P, 2, IW])
        rden = sb("rden", [P, IW])
        shift = sb("shift", [P, T], F32R)
        lat = rden[:, 0:NT * L].rearrange("p (n c) -> p n c", n=NT)
        rlat = sb("rlat", [P, NT])
        m2 = sb("m2", [P, NT])
        qh2, ql2, kh2, kl2 = (q2k2[:, 2 * n:2 * n + 2, :] for n in range(4))
        qs01 = q2k2[:, 0, :]
        e2 = h[:, 0, :].rearrange("p (n c) -> p n c", n=NT)
        p2t = h[:, 1, :]
        acc0 = (h[:, 0, :].rearrange("p (k n) -> p k n", k=2), acc)
        lat_parts = h[:, 1, :]
        enc = pr[0:L, 0, :, :].rearrange("p i n -> p (i n)")
        lat_r = pr[0:L, 1, :, :].rearrange("p i n -> p (i n)")

        xd = sb("xd", [P, CH, T])
        hb = sb("hb", [P, CH, T])
        part = sb("part", [P, 4, T], F32R)
        qs = sb("qs", [P, QUAD, T], F32R)
        ks = sb("ks", [P, QUAD, T], F32R)
        vb = sb("vb", [P, NT, C])
        prb = sb("prb", [P, 2, QUAD, IW])
        accb = sb("accb", [P, QUAD, IW])
        rdenb = sb("rdenb", [P, IW])
        rstd = accb[:, 0:IC, :]
        y = prb[:, 0, :, :].rearrange("p (h i) n -> p h (i n)", h=CH)
        sq = prb[:, 1, :, :].rearrange("p (h i) n -> p h (i n)", h=CH)

        def stacks3(u, last):
            return (q2k2[:, 0:QUAD, :], q2k2[:, QUAD:, :], 0) if last and u else (qs, ks, back0)

        nmx = {"front": sb("nmx_f", [P, 1, NT]), "back": sb("nmx_b", [P, QUAD, NT])}
        nmx_r = {"front": sb("nmx_rf", [P, 1, NT], F32R), "back": sb("nmx_rb", [P, QUAD, NT], F32R)}
        small_sb = {n: {s: sb(f"gn{n}_{s}_sb", shape) for s, shape in
                        (("bst", [P, CH, IC, 6]), ("mv", [P, CH, 2]), ("mean", [P, CH]), ("dev", [P, CH]),
                         ("dev_sq", [P, CH]), ("var", [P, CH]), ("std", [P, CH]), ("inv", [P, CH]),
                         ("scale", [P, CH]), ("ms", [P, CH]), ("bias", [P, CH]))} for n in (2, 3)}

        loaded = signal("loaded")
        setup_dve = signal("setup_dve")
        setup_pool = signal("setup_pool")
        setup_pe = signal("setup_pe")
        setup_mean = signal("setup_mean")
        x_loaded = signal("x_loaded", 16)
        stored = signal("stored", 16 * 4)
        l0_g = signal("l0_g")
        l0_v = signal("l0_v")
        l0_parts = signal("l0_parts")
        l0_lat_sum = signal("l0_lat_sum", 2)
        l0_rlat = signal("l0_rlat", 2)
        l0_lat = signal("l0_lat", 2)
        l0_lat_out = signal("l0_lat_out", 32)
        l0_lat_in = signal("l0_lat_in", 32)
        l0_wo = signal("l0_wo", 8)
        l0_res = signal("l0_res", 8)
        l0_enc_ps = signal("l0_enc_ps")
        l0_enc = signal("l0_enc")
        l0_s2 = signal("l0_s2")
        l0_m2 = signal("l0_m2")
        l0_d2 = signal("l0_d2")
        l0_e2 = signal("l0_e2")
        l0_t2 = signal("l0_t2")
        l0_p2t = signal("l0_p2t")
        qk_ps = {n: signal(f"l{n}_qk_ps") for n in (0, 1)}
        qk_hi = {n: signal(f"l{n}_qk_hi", 3) for n in (0, 1)}
        qk_lo = {n: signal(f"l{n}_qk_lo", 2) for n in (0, 1)}
        q_ps = {n: signal(f"l{n}_q_ps", 4) for n in (2, 3)}
        k_ps = {n: signal(f"l{n}_k_ps", 4) for n in (2, 3)}
        q_hi = {n: signal(f"l{n}_q_hi", 4) for n in (2, 3)}
        k_hi = {n: signal(f"l{n}_k_hi", 4) for n in (2, 3)}
        q_lo = {n: signal(f"l{n}_q_lo", 4) for n in (2, 3)}
        k_lo = {n: signal(f"l{n}_k_lo", 4) for n in (2, 3)}
        v_ps = {n: signal(f"l{n}_v_ps", 2) for n in (1, 2, 3)}
        v_sb = {n: signal(f"l{n}_v_sb", 2) for n in (1, 2, 3)}
        heads = {0: 1, 1: 1, 2: 1, 3: HEADS}
        max_ps = {n: signal(f"l{n}_max_ps", NT * heads[n]) for n in heads}
        max_sb = {n: signal(f"l{n}_max_sb", NT * heads[n]) for n in heads}
        max_r = {n: signal(f"l{n}_max_r", CH if n == 3 else 1) for n in heads}
        shift_ps = {n: signal(f"l{n}_shift_ps", heads[n]) for n in heads}
        shift_sb = {n: signal(f"l{n}_shift_sb", heads[n]) for n in heads}
        steps = {0: STEPS, 1: STEPS, 2: STEPS, 3: CH * STEPS3 * QUAD}
        scored = {n: signal(f"l{n}_scored", steps[n]) for n in heads}
        exped = {n: signal(f"l{n}_exped", steps[n]) for n in heads}
        weighed = {n: signal(f"l{n}_weighed", steps[n] // (QUAD if n == 3 else 1)) for n in heads}
        summed = {n: signal(f"l{n}_summed", 3 * IC) for n in (0, 1, 2)}
        folded = {n: signal(f"l{n}_folded", IC) for n in (0, 1, 2)}
        summed_dve = signal("l3_summed_dve", (NT - 1) * IC * CH)
        summed_pool = signal("l3_summed_pool", (NT - 1) * IC * CH)
        total = {n: signal(f"l{n}_total", c) for n, c in ((1, IC), (2, IC), (3, IC * CH))}
        inverse = {n: signal(f"l{n}_inverse", c) for n, c in ((1, IC), (2, IC), (3, IC * CH))}
        taken = signal("l3_taken", IC * CH)
        normed = {n: signal(f"l{n}_normed", 4) for n in (1, 2, 3)}
        l1_res = signal("l1_res", 4)
        l2_proj = signal("l2_proj", 4)
        l2_res = signal("l2_res", 4)
        gn = {n: {s: signal(f"gn{n}_{s}", c) for s, c in
                  (("chan", 2), ("mean_ps", 1), ("mean", 1), ("dev", 1), ("dev_sq", 1), ("var", 1), ("var_ps", 1),
                   ("std", 1), ("inv", 1), ("scale", 1), ("ms", 1), ("bias", 1), ("h", 2))} for n in (2, 3)}
        last_ones = signal("last_ones")
        xd_copied = signal("xd_copied", 16)
        stacked = [signal(f"stacked{u}", 16 * 6 * QUAD) for u in range(CH)]
        l3_proj = signal("l3_proj", 4)
        l3_y = signal("l3_y", 4)
        l3_sq = signal("l3_sq", 4)
        l3_var = signal("l3_var", IC)
        l3_std = signal("l3_std", IC)
        l3_rstd = signal("l3_rstd", IC)
        l3_n = signal("l3_n", 4)
        l3_g = signal("l3_g", 4)
        l3_out = signal("l3_out", 4)

        def score_use(s, g):
            return QUAD * s + g + (s >= NT + 2)

        def total_use(ic):
            return (QUAD * (NT + 2), QUAD * STEPS3 + 1)[ic]

        def bank_use(u, use):
            for ic in range(IC):
                if use == total_use(ic):
                    return inverse[3], IC * u + ic + 1
            return exped[3], QUAD * STEPS3 * u + use - (use > total_use(0)) + 1

        x_v = x.rearrange("b (h p) t -> b p h t", p=P)
        out_v = out.rearrange("b (h p) t -> b p h t", p=P)

        def bf32(ap):
            return ap.bitcast(F32)

        def cols(i):
            return slice(i * IW, (i + 1) * IW)

        def tile(i):
            return slice(i * P, (i + 1) * P)

        def vcol(name, n=0):
            a = V_COLS[name].start + n
            return vec[:, a:a + 1]

        def wcol(name, kt, a, n):
            s = W_COLS[name].start + a
            return w[:, kt, s:s + n]

        block = ctx.enter_context(nc.Block())

        @block.sync
        def _(sp):
            sp.dma_start(w[:], weights.rearrange("(h p) n -> p h n", p=P)).then_inc(loaded.sem, 16)
            sp.dma_start(vec[:], vectors).then_inc(loaded.sem, 16)
            sp.dma_start(vbias[:], value_biases).then_inc(loaded.sem, 16)
            sp.dma_start(wo_con[:], small).then_inc(loaded.sem, 16)
            sp.dma_start(con1[:, 0:L], concepts).then_inc(loaded.sem, 16)
            sp.dma_start(cst[:], constants).then_inc(loaded.sem, 16)

            def latents(b, n):
                sp.wait_ge(l0_lat.sem, l0_lat.at(b, n + 1))
                sp.dma_start(lat_dram.rearrange("(i p) c -> p i c", p=P), lat).then_inc(l0_lat_out.sem, 16)
                sp.wait_ge(l0_lat_out.sem, l0_lat_out.at(b, 16 * (n + 1)))
                sp.dma_start(lat_r, lat_dram.rearrange("(l r) c -> l (r c)", l=L)).then_inc(l0_lat_in.sem, 16)

            def front(b):
                yield
                for _ in range(2 + NT + 1 + STEP_SLOTS[0] * STEPS):
                    yield
                latents(b, 0)
                yield
                for _ in range(4):
                    yield
                latents(b, 1)
                yield
                while True:
                    yield

            def stacks(b, u, last):
                queries, keys, _ = stacks3(u, last)
                if u and not last:
                    sp.wait_ge(scored[3].sem, scored[3].at(b, QUAD * STEPS3))
                for done, src, dst, rows in ((q_hi, 0, queries, (0, 2)), (q_lo, 1, queries, (1,)),
                                             (k_hi, 2, keys, (0, 1)), (k_lo, 3, keys, (2,))):
                    if u == 0 or last:
                        sp.wait_ge(done[3].sem, done[3].at(b, IC * (u + 1)))
                    for r in rows:
                        for g in range(QUAD):
                            sp.dma_start(bf32(dst[L * r:L * r + L, g, :]),
                                         bf32(part[L * g:L * g + L, src, :])).then_inc(stacked[u].sem, 16)

            def back(b, last=False):
                sp.wait_ge(l2_res.sem, l2_res.at(b, 4))
                sp.dma_start(xd[:], xm[:]).then_inc(xd_copied.sem, 16)
                for _ in range(3):
                    yield
                stacks(b, 0, last)
                yield
                for _ in range(3 + ROUND_SLOTS - 2):
                    yield
                stacks(b, 1, last)
                yield
                for _ in range(1 + ROUND_SLOTS + 2):
                    yield
                for ic in range(IC):
                    for ch in range(CH):
                        sp.wait_ge(l3_out.sem, l3_out.at(b, CH * ic + ch + 1))
                        sp.dma_start(out_v[b, :, ch, cols(ic)], y[:, ch, cols(ic)]).then_inc(stored.sem, 16)
                    yield

            alone(front(0), FRONT_SLOTS)
            with sp.Fori(0, B - 1) as b:
                by_turns(front(b + 1), back(b))
            finish_alone(back(B - 1, last=True))
            sp.wait_ge(stored.sem, stored.at(B, 1))

        @block.gpsimd
        def _(pool):
            pool.memset(ones[:], 1.0).then_inc(setup_pool.sem, 1)
            pool.memset(ones_over_c[:], 1.0 / C).then_inc(setup_pool.sem, 1)
            pool.memset(con1[:, L:L + 1], 1.0).then_inc(setup_pool.sem, 1)
            pool.memset(eps[:], EPS).then_inc(setup_pool.sem, 1)
            pool.memset(nmx["back"][:], 0.0).then_inc(stored.sem, 1)
            pool.memset(bf32(ones_over_p[:]), 1.0 / P).then_inc(setup_pool.sem, 1)

            def idle(n):
                for _ in range(n):
                    yield

            def add_step(b, n, s, into):
                ic, jg = divmod(s, 4)
                if jg:
                    pool.wait_ge(exped[n].sem, exped[n].at(b, s + 1))
                    if n and jg == 1 and ic:
                        pool.wait_ge(total[n].sem, total[n].at(b, ic))
                    if jg > 1:
                        pool.wait_ge(summed[n].sem, summed[n].at(b, 3 * ic + jg - 1))
                    pool.tensor_tensor(into[:], pr[:, (s - 1) % 2, :, :] if jg == 1 else into[:],
                                       pr[:, s % 2, :, :], ALU.add).then_inc(summed[n].sem, 1)

            def fold(b, n, ic, into):
                pool.wait_ge(summed[n].sem, summed[n].at(b, 3 * (ic + 1)))
                pool.tensor_tensor(into[:, 0, :], into[:, 0, :], into[:, 1, :], ALU.add).then_inc(folded[n].sem, 1)

            def sums(b, n):
                for ic in range(IC):
                    for jg in range(4):
                        add_step(b, n, 4 * ic + jg, acc)
                        yield from idle(STEP_SLOTS[n])
                    fold(b, n, ic, acc)
                    yield from idle(3)

            def front(b):
                pool.dma_start(x_in[:], x_v[b]).then_inc(x_loaded.sem, 16)
                yield from idle(2 + NT + 1)
                for s in range(STEPS):
                    ic = s // 4
                    add_step(b, 0, s, acc0[ic])
                    if s % 4 == 3:
                        fold(b, 0, ic, acc0[ic])
                    yield from idle(STEP_SLOTS[0])
                yield from idle(8)
                for _ in range(3 + NT + 1):
                    yield
                yield from sums(b, 1)
                for _ in range(7 + NT + 1):
                    yield
                yield from sums(b, 2)
                yield

            def back(b, last=False):
                for _ in range(3 + 3):
                    yield
                if last:
                    pool.wait_ge(scored[2].sem, scored[2].at(b, STEPS))
                    pool.wait_ge(summed_pool.sem, summed_pool.at(b, 0))
                    pool.wait_ge(folded[2].sem, folded[2].at(b, IC))
                    pool.memset(bf32(q2k2[ROW:ROW + 1, QUAD:, :]), 1.0).then_inc(last_ones.sem, 1)

                def steps(u):
                    for s in range(STEPS3):
                        ic, j = divmod(s, NT)
                        yield
                        if j:
                            n = IC * u + ic
                            pool.wait_ge(exped[3].sem, exped[3].at(b, QUAD * (STEPS3 * u + s + 1)))
                            if last and s == 1 and u == 0:
                                pool.wait_ge(last_ones.sem, 1)
                            if j == 1 and n:
                                pool.wait_ge(total[3].sem, total[3].at(b, n))
                            if j > 1:
                                pool.wait_ge(summed_pool.sem, summed_pool.at(b, (NT - 1) * n + j - 1))
                            pool.tensor_tensor(accb[:, 2:4, :], prb[:, (s - 1) % 2, 2:4, :] if j == 1 else
                                               accb[:, 2:4, :], prb[:, s % 2, 2:4, :], ALU.add)\
                                .then_inc(summed_pool.sem, 1)
                        yield
                    yield from idle(2)

                yield from both_rounds(lambda u: idle(QUAD * NT), lambda u: idle(2 + (u == 0)), steps, last)
                for _ in range(4):
                    yield

            alone(front(0), FRONT_SLOTS)
            with pool.Fori(0, B - 1) as b:
                pool.wait_ge(weighed[2].sem, weighed[2].at(b, STEPS))
                by_turns(front(b + 1), back(b))
            finish_alone(back(B - 1, last=True))

        @block.tensor
        def _(pe):
            pe.wait_ge(loaded.sem, 16 * 6)
            pe.wait_ge(setup_pool.sem, 5)
            for ch in range(CH):
                mm = pe.matmul(ps[:, 0, 0:1], ones_over_c[:], vcol("bo3", ch), start=ch == 0, stop=ch == CH - 1)
            mm.then_inc(setup_pe.sem, 1)
            pe.wait_ge(setup_dve.sem, 12)

            def project(bank, name, src, m0, m, ic):
                for kt in range(CH):
                    mm = pe.matmul(ps[0:m, bank, :], wcol(name, kt, m0, m), src[:, kt, cols(ic)],
                                   start=kt == 0, stop=kt == CH - 1)
                return mm

            def values(name, src, bank, half):
                for t in range(4):
                    for kt in range(CH):
                        mm = pe.matmul(ps[:, bank + t // 2, (t % 2) * C:(t % 2 + 1) * C],
                                       src[:, kt, tile(4 * half + t)], wcol(name, kt, 0, C),
                                       start=kt == 0, stop=kt == CH - 1)
                return mm

            def max_tile(b, n, count, queries, keys, it, bank):
                if count >= 2:
                    pe.wait_ge(max_sb[n].sem, max_sb[n].at(b, count - 1))
                for jc in range(IC):
                    mm = pe.matmul(ps[:, bank + jc, :], queries[0:STACK, tile(it)], keys[0:STACK, cols(jc)],
                                   start=True, stop=True)
                mm.then_inc(max_ps[n].sem, 1)

            def shift_rows(n, side, head, bank):
                for it in range(NT):
                    mm = pe.matmul(ps[:, bank + it // 4, tile(it % 4)],
                                   nmx_r[side][:, head, it:it + 1].broadcast_to([P, P]), ident_r[:],
                                   start=True, stop=True)
                mm.then_inc(shift_ps[n].sem, 1)

            def stacked_scores(bank, queries, keys, jt, ic):
                return pe.matmul(ps[:, bank, :], keys[0:ROW + 1, tile(jt)], queries[0:ROW + 1, cols(ic)],
                                 start=True, stop=True)

            def stacks_and_maxima(b, n, src, extra):
                for ic in range(IC):
                    mm = project(ic, f"qk{n}", src, 0, P, ic)
                mm.then_inc(qk_ps[n].sem, 1)
                yield
                yield from extra
                for it in range(NT):
                    max_tile(b, n, it, qs01, ks01, it, 2 * (it % 2))
                    yield
                pe.wait_ge(max_r[n].sem, max_r[n].at(b, 1))
                shift_rows(n, "front", 0, 0)
                yield

            def scores01(b, n, s):
                ic, jg = divmod(s, 4)
                if s == 0:
                    pe.wait_ge(shift_sb[n].sem, shift_sb[n].at(b, 1))
                else:
                    pe.wait_ge(exped[n].sem, exped[n].at(b, s))
                for j in range(2):
                    mm = stacked_scores(j, qs01, ks01, 2 * jg + j, ic)
                mm.then_inc(scored[n].sem, 1)

            def layer0(b, last):
                if last is not None:
                    pe.wait_ge(l2_res.sem, l2_res.at(last, 4))
                pe.wait_ge(x_loaded.sem, x_loaded.at(b, 16))

                def values0():
                    for jt in range(NT):
                        for kt in range(CH):
                            mm = pe.matmul(ps[:, 2, jt * L:(jt + 1) * L], x_in[:, kt, tile(jt)],
                                           wcol("g", kt, 0, L), start=kt == 0, stop=kt == CH - 1)
                    mm.then_inc(l0_g.sem, 1)
                    yield
                    pe.wait_ge(l0_v.sem, l0_v.at(b, 1))
                    pe.wait_ge(qk_lo[0].sem, qk_lo[0].at(b, 2))

                yield from stacks_and_maxima(b, 0, x_in, values0())

                def weigh(s):
                    ic, jg = divmod(s, 4)
                    pe.wait_ge(exped[0].sem, exped[0].at(b, s + 1))
                    for j in range(2):
                        jt = 2 * jg + j
                        g = jt % QUAD
                        mm = pe.matmul(ps[L * g:L * g + L, 2 + ic, :], vg[:, jt, :], pr[:, s % 2, j, :],
                                       start=jt < QUAD, stop=jt >= QUAD, tile_position=(0, L * g))
                    mm.then_inc(weighed[0].sem, 1)

                def add_parts():
                    pe.wait_ge(l0_parts.sem, l0_parts.at(b, 1))
                    for nt in range(NT):
                        pe.matmul(ps[:, 2, nt * (L + 1):nt * (L + 1) + L], lat_parts[:, tile(nt)], ident_quad,
                                  start=True, stop=True)
                    pe.wait_ge(folded[0].sem, folded[0].at(b, IC))
                    for nt in range(NT):
                        mm = pe.matmul(ps[:, 2, nt * (L + 1) + L:(nt + 1) * (L + 1)],
                                       acc0[nt // 4][:, 0, tile(nt % 4)], ones[:, 0:1], start=True, stop=True)
                    mm.then_inc(l0_lat_sum.sem, 1)

                def times_wo(n):
                    pe.wait_ge(l0_lat_in.sem, l0_lat_in.at(b, 16 * (n + 1)))
                    for k in range(4):
                        ic, ch = divmod(k, CH)
                        pe.matmul(ps[:, k, :], wo_con[:, tile(ch)], lat_r[:, cols(ic)],
                                  start=True, stop=True).then_inc(l0_wo.sem, 1)

                for s in range(STEPS):
                    scores01(b, 0, s)
                    yield
                    if s:
                        weigh(s - 1)
                    yield
                weigh(STEPS - 1)
                yield
                add_parts()
                yield
                times_wo(0)
                yield
                pe.wait_ge(l0_res.sem, l0_res.at(b, 4))
                for ic in range(IC):
                    mm = project(ic, "qk0", xm, 0, L, ic)
                mm.then_inc(l0_enc_ps.sem, 1)
                yield
                pe.wait_ge(l0_enc.sem, l0_enc.at(b, 1))
                for nt in range(NT):
                    mm = pe.matmul(ps[:, 2 + nt // 4, tile(nt % 4)], enc[:, tile(nt)], wo_con[:, C:C + P],
                                   start=True, stop=True)
                mm.then_inc(l0_s2.sem, 1)
                yield
                pe.wait_ge(l0_e2.sem, l0_e2.at(b, 1))
                for nt in range(NT):
                    mm = pe.transpose(ps[:, nt // 4, tile(nt % 4)], e2[:, nt, :], ident)
                mm.then_inc(l0_t2.sem, 1)
                yield
                pe.wait_ge(l0_p2t.sem, l0_p2t.at(b, 1))
                for nt in range(NT):
                    mm = pe.matmul(ps[:, 2, nt * (L + 1):(nt + 1) * (L + 1)], p2t[:, tile(nt)], con1[:],
                                   start=True, stop=True)
                mm.then_inc(l0_lat_sum.sem, 1)
                yield
                times_wo(1)
                yield

            def chunks(b, n, scores):
                for ic in range(IC):
                    def weigh(jg, j):
                        s = 4 * ic + jg
                        if j == 0:
                            pe.wait_ge(exped[n].sem, exped[n].at(b, s + 1))
                            if jg == 0 and ic:
                                pe.wait_ge(normed[n].sem, normed[n].at(b, CH))
                        jt = 2 * jg + j
                        for ch in range(CH):
                            mm = pe.matmul(ps[:, 2 + ch, :], v[:, jt, tile(ch)], pr[:, s % 2, j, :],
                                           start=jt == 0, stop=jt == NT - 1)
                        if j == 1:
                            mm.then_inc(weighed[n].sem, 1)

                    for jg in range(4):
                        if jg == 0 and ic:
                            pe.wait_ge(inverse[n].sem, inverse[n].at(b, ic))
                        yield from scores(4 * ic + jg)
                        for j in range(2):
                            if jg:
                                weigh(jg - 1, j)
                            yield
                    for j in range(2):
                        weigh(3, j)
                        yield
                    pe.wait_ge(folded[n].sem, folded[n].at(b, ic + 1))
                    pe.matmul(ps[:, 0, :], ones[:], acc[:, 0, :], start=True, stop=True).then_inc(total[n].sem, 1)
                    yield

            def values_slots(b, n, name, src, banks, free):
                for half in range(2):
                    free(half)
                    values(name, src, banks[half], half).then_inc(v_ps[n].sem, 1)
                    yield
                pe.wait_ge(v_sb[n].sem, v_sb[n].at(b, 2))

            def layer1(b):
                pe.wait_ge(l0_res.sem, l0_res.at(b, 8))

                def free(half):
                    if half:
                        pe.wait_ge(qk_lo[1].sem, qk_lo[1].at(b, 2))

                yield from stacks_and_maxima(b, 1, xm, values_slots(b, 1, "v1", xm, (2, 0), free))

                def scores(s):
                    scores01(b, 1, s)
                    yield from ()

                yield from chunks(b, 1, scores)

            def group_norm(b, n, bank):
                g = small_sb[n]
                pe.wait_ge(gn[n]["chan"].sem, gn[n]["chan"].at(b, CH))
                pe.matmul(ps[:, bank, 0:CH], group_avg, g["mv"][:, :, 0], start=True, stop=True)\
                    .then_inc(gn[n]["mean_ps"].sem, 1)
                yield
                pe.wait_ge(gn[n]["var"].sem, gn[n]["var"].at(b, 1))
                pe.matmul(ps[:, bank + 1, 0:CH], group_avg, g["var"][:], start=True, stop=True)\
                    .then_inc(gn[n]["var_ps"].sem, 1)
                yield
                yield
                pe.wait_ge(gn[n]["h"].sem, gn[n]["h"].at(b, CH))

            def layer2(b):
                yield from group_norm(b, 2, 0)
                for name, sig in (("q2", q_ps[2]), ("k2", k_ps[2])):
                    for k in range(4):
                        blk, ic = divmod(k, IC)
                        if name == "k2":
                            pe.wait_ge(q_lo[2].sem, q_lo[2].at(b, k + 1))
                        project(k, name, h, P * blk, P, ic).then_inc(sig.sem, 1)
                    yield
                yield from values_slots(b, 2, "v2", h, (0, 2),
                                        lambda half: pe.wait_ge(k_lo[2].sem, k_lo[2].at(b, 2 * (half + 1))))
                for it in range(NT):
                    if it >= 2:
                        pe.wait_ge(max_sb[2].sem, max_sb[2].at(b, it - 1))
                    for jc in range(IC):
                        for kt in range(CH):
                            mm = pe.matmul(ps[:, 2 * (it % 2) + jc, :], qh2[:, kt, tile(it)], kh2[:, kt, cols(jc)],
                                           start=kt == 0, stop=kt == CH - 1)
                    mm.then_inc(max_ps[2].sem, 1)
                    yield
                pe.wait_ge(max_r[2].sem, max_r[2].at(b, 1))
                shift_rows(2, "front", 0, 0)
                yield

                def scores(s):
                    ic, jg = divmod(s, 4)
                    if s == 0:
                        pe.wait_ge(shift_sb[2].sem, shift_sb[2].at(b, 1))
                    else:
                        pe.wait_ge(exped[2].sem, exped[2].at(b, s))
                    for j in range(2):
                        keys = tile(2 * jg + j)
                        pe.matmul(ps[:, j, :], ones_over_p[:], shift[:, cols(ic)], start=True, stop=False)
                        for kt in range(CH):
                            for kpart, qpart in ((kh2, qh2), (kh2, ql2), (kl2, qh2)):
                                mm = pe.matmul(ps[:, j, :], kpart[:, kt, keys], qpart[:, kt, cols(ic)],
                                               start=False, stop=kt == CH - 1 and kpart is kl2)
                        if j == 1:
                            mm.then_inc(scored[2].sem, 1)
                        yield

                yield from chunks(b, 2, scores)
                pe.wait_ge(normed[2].sem, normed[2].at(b, 4))
                for k in range(4):
                    ic, ch = divmod(k, CH)
                    project(k, "o2", h, P * ch, P, ic).then_inc(l2_proj.sem, 1)
                yield

            def front(b, last=None):
                yield from layer0(b, last)
                yield from layer1(b)
                yield from layer2(b)

            def back(b, last=False):
                yield from group_norm(b, 3, back0)

                def queries_and_keys(blk):
                    for base, name, sig in ((0, "q3", q_ps[3]), (2, "k3", k_ps[3])):
                        for ic in range(IC):
                            project(back0 + base + ic, name, hb, P * blk, P, ic).then_inc(sig.sem, 1)

                queries_and_keys(0)
                yield
                for half in range(2):
                    done = (q_lo, k_lo)[half][3]
                    pe.wait_ge(done.sem, done.at(b, IC))
                    values("v3", hb, back0 + 2 * half, half).then_inc(v_ps[3].sem, 1)
                    yield
                pe.wait_ge(v_sb[3].sem, v_sb[3].at(b, 2))
                def maxima(u):
                    queries, keys, bank = stacks3(u, last)
                    pe.wait_ge(stacked[u].sem, stacked[u].at(b, 16 * 6 * QUAD))
                    for k in range(QUAD * NT):
                        g, it = divmod(k, NT)
                        if u and k == 1 and not last:
                            first_round_taken()
                        max_tile(b, 3, QUAD * NT * u + k, queries[:, g, :], keys[:, g, :], it, bank + 2 * (k % 2))
                        yield

                def first_round_taken():
                    pe.wait_ge(taken.sem, taken.at(b, IC))
                    pe.wait_ge(inverse[3].sem, inverse[3].at(b, IC))

                def middle(u):
                    pe.wait_ge(max_r[3].sem, max_r[3].at(b, u + 1))
                    if u == 0:
                        queries_and_keys(1)
                        yield
                        pe.wait_ge(q_lo[3].sem, q_lo[3].at(b, 2 * IC))
                        pe.wait_ge(k_lo[3].sem, k_lo[3].at(b, 2 * IC))
                    elif last:
                        first_round_taken()
                        pe.wait_ge(last_ones.sem, 1)
                    for g in range(QUAD):
                        if g >= 2:
                            pe.wait_ge(shift_sb[3].sem, shift_sb[3].at(b, QUAD * u + g - 1))
                        shift_rows(3, "back", g, back0 + 2 * (g % 2))
                        if g % 2:
                            yield

                def steps(u):
                    queries, keys, _ = stacks3(u, last)
                    pe.wait_ge(shift_sb[3].sem, shift_sb[3].at(b, QUAD * (u + 1)))

                    def take_turn(use):
                        if use >= 3:
                            done, count = bank_use(u, use - 3)
                            pe.wait_ge(done.sem, done.at(b, count))
                        return turn3[use % 3]

                    def scores(s, pair):
                        ic, jt = divmod(s, NT)
                        for g in (2 * pair, 2 * pair + 1):
                            bank = take_turn(score_use(s, g))
                            stacked_scores(bank, queries[:, g, :], keys[:, g, :], jt, ic).then_inc(scored[3].sem, 1)

                    def weigh(s):
                        ic, jt = divmod(s, NT)
                        n = STEPS3 * u + s
                        pe.wait_ge(exped[3].sem, exped[3].at(b, QUAD * (n + 1)))
                        if jt == 0 and n:
                            pe.wait_ge(taken.sem, taken.at(b, n // NT))
                        for g in range(QUAD):
                            mm = pe.matmul(ps[L * g:L * g + L, back0 + 2, :],
                                           vb[:, jt, L * (QUAD * u + g):L * (QUAD * u + g + 1)],
                                           prb[:, s % 2, g, :], start=jt == 0, stop=jt == NT - 1,
                                           tile_position=(0, L * g))
                        mm.then_inc(weighed[3].sem, 1)

                    def sum_weights(ic):
                        n = IC * u + ic
                        pe.wait_ge(summed_dve.sem, summed_dve.at(b, (NT - 1) * (n + 1)))
                        pe.wait_ge(summed_pool.sem, summed_pool.at(b, (NT - 1) * (n + 1)))
                        bank = take_turn(total_use(ic))
                        for g in range(QUAD):
                            mm = pe.matmul(ps[L * g:L * g + L, bank, :], ones[:, 0:L], accb[:, g, :],
                                           start=True, stop=True, tile_position=(0, L * g))
                        mm.then_inc(total[3].sem, 1)

                    for s in range(STEPS3):
                        scores(s, 0)
                        if s:
                            weigh(s - 1)
                        yield
                        scores(s, 1)
                        if s == NT + 1:
                            sum_weights(0)
                        yield
                    weigh(STEPS3 - 1)
                    yield
                    sum_weights(1)
                    yield

                yield from both_rounds(maxima, middle, steps, last)
                for ic in range(IC):
                    pe.wait_ge(normed[3].sem, normed[3].at(b, 3 + ic))
                    for ch in range(CH):
                        project(back0 + 2 * ic + ch, "o3", hb, P * ch, P, ic).then_inc(l3_proj.sem, 1)
                    yield
                for ic in range(IC):
                    pe.wait_ge(l3_sq.sem, l3_sq.at(b, CH * (ic + 1)))
                    for ch in range(CH):
                        mm = pe.matmul(ps[:, back0 + 2 * ic, :], ones_over_c[:], sq[:, ch, cols(ic)],
                                       start=ch == 0, stop=ch == CH - 1)
                    mm.then_inc(l3_var.sem, 1)
                    if ic == 0:
                        yield
                pe.wait_ge(l3_std.sem, l3_std.at(b, IC))
                yield

            alone(front(0), FRONT_SLOTS)
            with pe.Fori(0, B - 1) as b:
                by_turns(front(b + 1, b), back(b))
            finish_alone(back(B - 1, last=True))

        @block.scalar
        def _(act):
            act.wait_ge(loaded.sem, 16 * 6)
            act.wait_ge(setup_pool.sem, 5)
            act.wait_ge(setup_dve.sem, 12)

            def idle(n):
                for _ in range(n):
                    yield

            def to_stacks(b, n, biased):
                act.wait_ge(qk_ps[n].sem, qk_ps[n].at(b, 1))
                for into, rows in ((qs01[0:STACK, :], slice(0, STACK)), (ks01[L:2 * L, :], slice(STACK, P)),
                                   (ks01[0:L, :], slice(STACK, P))):
                    src = ps[rows, 0:2, :]
                    if biased:
                        act.activation(into, src, ACT.Identity, bias=vcol("bqk1")[rows, :])\
                            .then_inc(qk_hi[n].sem, 1)
                    else:
                        act.activation(into, src, ACT.Copy).then_inc(qk_hi[n].sem, 1)
                yield

            def shift_row(b, n, count, queries, bank):
                act.wait_ge(shift_ps[n].sem, shift_ps[n].at(b, count + 1))
                act.activation(queries[ROW:ROW + 1, :], ps[ROW:ROW + 1, bank:bank + 2, :], ACT.Copy)\
                    .then_inc(shift_sb[n].sem, 1)

            def exps(b, n, s):
                act.wait_ge(scored[n].sem, scored[n].at(b, s + 1))
                if s >= 2:
                    act.wait_ge(weighed[n].sem, weighed[n].at(b, s - 1))
                    ic, jg = divmod(s - 2, 4)
                    act.wait_ge(summed[n].sem, summed[n].at(b, 3 * ic + max(jg, 1)))
                act.activation(pr[:, s % 2, :, :], ps[:, 0:2, :], ACT.Exp).then_inc(exped[n].sem, 1)

            def group_norm(b, n, src, dst, bank):
                g, sig = small_sb[n], gn[n]
                yield
                act.wait_ge(sig["var_ps"].sem, sig["var_ps"].at(b, 1))
                act.activation(g["std"][:], ps[:, bank + 1, 0:CH], ACT.Sqrt, bias=eps[:]).then_inc(sig["std"].sem, 1)
                yield
                act.wait_ge(sig["bias"].sem, sig["bias"].at(b, 1))
                act.activation(dst[:, 1, :], src[:, 1, :], ACT.Identity, bias=g["bias"][:, 1:2],
                               scale=g["scale"][:, 1:2]).then_inc(sig["h"].sem, 1)
                yield

            def high_parts(b, n, blk, ic, which, bank, bias, dst):
                ready, done = ((q_ps, q_hi), (k_ps, k_hi))[which]
                act.wait_ge(ready[n].sem, ready[n].at(b, IC * blk + ic + 1))
                act.activation(dst, ps[:, bank, :], ACT.Identity, bias=vcol(bias, blk)).then_inc(done[n].sem, 1)

            def front(b):
                yield from to_stacks(b, 0, False)
                yield from idle(1 + NT)
                shift_row(b, 0, 0, qs01, 0)
                yield
                for s in range(STEPS):
                    exps(b, 0, s)
                    yield from idle(STEP_SLOTS[0])
                act.wait_ge(weighed[0].sem, weighed[0].at(b, STEPS))
                act.activation(lat_parts, ps[:, 2:4, :], ACT.Copy).then_inc(l0_parts.sem, 1)
                yield
                yield from idle(2)
                act.wait_ge(l0_enc_ps.sem, l0_enc_ps.at(b, 1))
                act.activation(enc, ps[0:L, 0:2, :], ACT.Copy).then_inc(l0_enc.sem, 1)
                yield
                act.wait_ge(l0_d2.sem, l0_d2.at(b, 1))
                act.activation(e2, e2, ACT.Exp).then_inc(l0_e2.sem, 1)
                yield
                act.wait_ge(l0_t2.sem, l0_t2.at(b, 1))
                act.activation(p2t, ps[:, 0:2, :], ACT.Copy).then_inc(l0_p2t.sem, 1)
                yield
                yield from idle(2)
                yield from to_stacks(b, 1, True)
                yield from idle(2 + NT)
                shift_row(b, 1, 0, qs01, 0)
                yield
                for s in range(STEPS):
                    exps(b, 1, s)
                    yield from idle(STEP_SLOTS[1])
                    if s % 4 == 3:
                        yield from idle(3)
                yield from group_norm(b, 2, xm, h, 0)
                for which, bias, dst in ((0, "bq2", qh2), (1, "bk2", kh2)):
                    for k in range(4):
                        blk, ic = divmod(k, IC)
                        high_parts(b, 2, blk, ic, which, k, bias, dst[:, blk, cols(ic)])
                    yield
                yield from idle(2 + NT)
                act.wait_ge(shift_ps[2].sem, shift_ps[2].at(b, 1))
                act.activation(shift[:], ps[:, 0:2, :], ACT.Copy).then_inc(shift_sb[2].sem, 1)
                yield
                for s in range(STEPS):
                    yield
                    exps(b, 2, s)
                    yield from idle(STEP_SLOTS[2] - 1)
                    if s % 4 == 3:
                        yield from idle(3)
                yield

            def back(b, last=False):
                yield from group_norm(b, 3, xm, hb, back0)

                def queries_and_keys(blk):
                    for which, bias in ((0, "bq3"), (1, "bk3")):
                        for ic in range(IC):
                            high_parts(b, 3, blk, ic, which, back0 + 2 * which + ic, bias,
                                       part[:, 2 * which, cols(ic)])
                    yield

                def exps3(u, s, pair):
                    n = STEPS3 * u + s
                    for g in (2 * pair, 2 * pair + 1):
                        act.wait_ge(scored[3].sem, scored[3].at(b, QUAD * n + g + 1))
                        if n >= 2 and g == 2 * pair:
                            act.wait_ge(weighed[3].sem, weighed[3].at(b, n - 1))
                            chunk, j = divmod(n - 2, NT)
                            used = (NT - 1) * chunk + max(j, 1)
                            sig = (summed_dve, summed_pool)[pair]
                            act.wait_ge(sig.sem, sig.at(b, used))
                        if n == g == 0:
                            act.wait_ge(stored.sem, stored.at(b, 1))
                        act.activation(prb[:, s % 2, g, :], ps[:, turn3[score_use(s, g) % 3], :], ACT.Exp)\
                            .then_inc(exped[3].sem, 1)

                def take(u, ic):
                    n = IC * u + ic
                    act.wait_ge(weighed[3].sem, weighed[3].at(b, NT * (n + 1)))
                    act.activation(hb[:, u, cols(ic)], ps[:, back0 + 2, :], ACT.Copy).then_inc(taken.sem, 1)

                yield from queries_and_keys(0)
                yield from idle(2)
                def middle(u):
                    if u == 0:
                        act.wait_ge(stacked[0].sem, stacked[0].at(b, 16 * 6 * QUAD))
                        yield from queries_and_keys(1)
                    for g in range(QUAD):
                        shift_row(b, 3, QUAD * u + g, stacks3(u, last)[0][:, g, :], back0 + 2 * (g % 2))
                        if g % 2:
                            yield

                def steps(u):
                    for s in range(STEPS3):
                        exps3(u, s, 0)
                        if s == NT:
                            take(u, 0)
                        yield
                        exps3(u, s, 1)
                        yield
                    take(u, 1)
                    yield from idle(2)

                yield from both_rounds(lambda u: idle(QUAD * NT), middle, steps, last)
                for ic in range(IC):
                    for ch in range(CH):
                        bank = back0 + 2 * ic + ch
                        act.wait_ge(l3_proj.sem, l3_proj.at(b, CH * ic + ch + 1))
                        act.activation(y[:, ch, cols(ic)], ps[:, bank, :], ACT.Identity, bias=vcol("bo3", ch))\
                            .then_inc(l3_y.sem, 1)
                        act.activation(sq[:, ch, cols(ic)], ps[:, bank, :], ACT.Square, bias=vcol("bo3", ch))\
                            .then_inc(l3_sq.sem, 1)
                    yield

                def finish(ic):
                    for ch in range(CH):
                        act.wait_ge(l3_g.sem, l3_g.at(b, CH * ic + ch + 1))
                        act.activation(y[:, ch, cols(ic)], y[:, ch, cols(ic)], ACT.Identity, bias=vcol("ln_b", ch))\
                            .then_inc(l3_out.sem, 1)

                for ic in range(IC):
                    act.wait_ge(l3_var.sem, l3_var.at(b, ic + 1))
                    act.activation(rstd[:, ic, :], ps[:, back0 + 2 * ic, :], ACT.Sqrt, bias=eps[:])\
                        .then_inc(l3_std.sem, 1)
                    finish(ic)
                    yield

            alone(front(0), FRONT_SLOTS)
            with act.Fori(0, B - 1) as b:
                by_turns(front(b + 1), back(b))
            finish_alone(back(B - 1, last=True))

        @block.vector
        def _(dve):
            dve.wait_ge(loaded.sem, 16 * 6)
            dve.tensor_copy(ident_r[:], ident).then_inc(setup_dve.sem, 1)
            dve.memset(bf32(ks[ROW:ROW + 1, :, :]), 1.0).then_inc(setup_dve.sem, 1)
            dve.memset(bf32(ks01[ROW:ROW + 1, :]), 1.0).then_inc(setup_dve.sem, 1)

            def scale(ap, factor):
                dve.tensor_scalar(ap, ap, factor, None, ALU.mult).then_inc(setup_dve.sem, 1)

            scale(w[:, :, W_COLS["qk0"].start:W_COLS["g"].stop], C ** -0.5)
            scale(wo_con[:, 0:C], L ** -0.5)
            scale(w[:, :, W_COLS["q2"]], C ** -0.5)
            scale(w[:, :, W_COLS["q3"]], L ** -0.25)
            scale(vec[:, V_COLS["bq2"]], C ** -0.5)
            scale(vec[:, V_COLS["bq3"]], L ** -0.25)
            dve.tensor_reduce(wo_mean[:], w[:, :, W_COLS["o3"]], AX.X, ALU.add, negate=True)\
                .then_inc(setup_mean.sem, 1)
            dve.wait_ge(setup_mean.sem, 1)
            dve.tensor_scalar(wo_mean[:], wo_mean[:], 1.0 / C, None, ALU.mult).then_inc(setup_dve.sem, 1)
            dve.wait_ge(setup_dve.sem, 10)
            dve.tensor_tensor(w[:, :, W_COLS["o3"]], w[:, :, W_COLS["o3"]],
                              wo_mean[:].unsqueeze(2).broadcast_to([P, CH, C]), ALU.add).then_inc(setup_dve.sem, 1)
            dve.wait_ge(setup_pe.sem, 1)
            dve.tensor_scalar(vec[:, V_COLS["bo3"]], vec[:, V_COLS["bo3"]], ps[:, 0, 0:1], None, ALU.subtract)\
                .then_inc(setup_dve.sem, 1)

            def idle(n):
                for _ in range(n):
                    yield

            def low_stacks(b, n, biased):
                for count, dst, block, high, rows in ((1, qs01, 1, 1, slice(L, 2 * L)),
                                                      (3, ks01, 2, 0, slice(STACK, P))):
                    dve.wait_ge(qk_hi[n].sem, qk_hi[n].at(b, count))
                    into, high = (dst[L * k:L * k + L, :].rearrange("p (i n) -> p i n", i=IC) for k in (block, high))
                    src = ps[rows, 0:2, :]
                    if biased:
                        dve.scalar_tensor_tensor(out=into, in0=src, scalar=vcol("bqk1")[rows, :], in1=bf32(high),
                                                 op0=ALU.add, op1=ALU.subtract).then_inc(qk_lo[n].sem, 1)
                    else:
                        dve.tensor_tensor(into, src, bf32(high), ALU.subtract).then_inc(qk_lo[n].sem, 1)
                yield

            def low_parts(b, n, blk, ic, which, bank, bias, hi, dst):
                ready, done = ((q_hi, q_lo), (k_hi, k_lo))[which]
                dve.wait_ge(ready[n].sem, ready[n].at(b, IC * blk + ic + 1))
                dve.scalar_tensor_tensor(out=dst, in0=ps[:, bank, :], scalar=vcol(bias, blk), in1=bf32(hi),
                                         op0=ALU.add, op1=ALU.subtract).then_inc(done[n].sem, 1)

            def maximum(b, n, count, side, head, it, bank):
                dve.wait_ge(max_ps[n].sem, max_ps[n].at(b, count + 1))
                dve.tensor_reduce(nmx[side][:, head, it:it + 1], ps[:, bank:bank + 2, :], AX.XY, ALU.max,
                                  negate=True).then_inc(max_sb[n].sem, 1)

            def round_maxima(b, n, side, u=0):
                count = NT * (QUAD if side == "back" else 1)
                dve.wait_ge(max_sb[n].sem, max_sb[n].at(b, count * (u + 1)))
                dve.tensor_copy(nmx_r[side][:], nmx[side][:]).then_inc(max_r[n].sem, 1)

            def maxima(b, n):
                for it in range(NT):
                    maximum(b, n, it, "front", 0, it, 2 * (it % 2))
                    if it == NT - 1:
                        round_maxima(b, n, "front")
                    yield

            def latents(b, n):
                sums = ps[:, 2, 0:NT * (L + 1)].rearrange("p (n c) -> p n c", n=NT)
                dve.reciprocal(rlat[:], sums[:, :, L]).then_inc(l0_rlat.sem, 1)
                dve.wait_ge(l0_rlat.sem, l0_rlat.at(b, n + 1))
                dve.tensor_tensor(lat, sums[:, :, 0:L], rlat[:].unsqueeze(2).broadcast_to([P, NT, L]),
                                  ALU.mult).then_inc(l0_lat.sem, 1)

            def residual0(b, n, last=None):
                src, gamma = ((x_in, "gamma_sa"), (xm, "gamma_moca"))[n]
                if n == 0 and last is not None:
                    dve.wait_ge(xd_copied.sem, xd_copied.at(last, 16))
                for k in range(4):
                    ic, ch = divmod(k, CH)
                    dve.wait_ge(l0_wo.sem, l0_wo.at(b, 4 * n + k + 1))
                    dve.scalar_tensor_tensor(out=xm[:, ch, cols(ic)], in0=ps[:, k, :], scalar=vcol(gamma),
                                             in1=src[:, ch, cols(ic)], op0=ALU.mult, op1=ALU.add)\
                        .then_inc(l0_res.sem, 1)
                yield

            def take_values(b, n, dst, banks):
                for half in range(2):
                    dve.wait_ge(v_ps[n].sem, v_ps[n].at(b, half + 1))
                    base = banks[half]
                    dve.tensor_tensor(dst[:, 4 * half:4 * half + 4, :].rearrange("p (k a) c -> p k a c", a=2),
                                      ps[:, base:base + 2, :].rearrange("p k (a c) -> p k a c", a=2),
                                      vbias[:, n - 1, :].unsqueeze(1).unsqueeze(1).broadcast_to([P, 2, 2, C]),
                                      ALU.add).then_inc(v_sb[n].sem, 1)
                    yield

            def chunks(b, n):
                for ic in range(IC):
                    yield from idle(4 * STEP_SLOTS[n] + 2)
                    dve.wait_ge(total[n].sem, total[n].at(b, ic + 1))
                    dve.reciprocal(rden[:], ps[:, 0, :]).then_inc(inverse[n].sem, 1)
                    dve.wait_ge(inverse[n].sem, inverse[n].at(b, ic + 1))
                    for ch in range(CH):
                        dve.tensor_tensor(h[:, ch, cols(ic)], ps[:, 2 + ch, :], rden[:], ALU.mult)\
                            .then_inc(normed[n].sem, 1)
                    if n == 1:
                        for ch in range(CH):
                            dve.wait_ge(normed[1].sem, normed[1].at(b, CH * ic + ch + 1))
                            dve.scalar_tensor_tensor(out=xm[:, ch, cols(ic)], in0=h[:, ch, cols(ic)],
                                                     scalar=vcol("gamma1"), in1=xm[:, ch, cols(ic)],
                                                     op0=ALU.mult, op1=ALU.add).then_inc(l1_res.sem, 1)
                    yield

            def group_norm(b, n, src, dst, ready, bank):
                sig, g = gn[n], small_sb[n]
                for k in range(4):
                    ic, ch = divmod(k, CH)
                    dve.wait_ge(ready.sem, ready.at(b, k + 1))
                    dve.bn_stats(g["bst"][:, ch, ic, :], src[:, ch, cols(ic)])
                dve.drain()
                for ch in range(CH):
                    dve.bn_aggr(g["mv"][:, ch, :], g["bst"][:, ch, :, :]).then_inc(sig["chan"].sem, 1)
                yield
                dve.wait_ge(sig["mean_ps"].sem, sig["mean_ps"].at(b, 1))
                dve.tensor_copy(g["mean"][:], ps[:, bank, 0:CH]).then_inc(sig["mean"].sem, 1)
                dve.wait_ge(sig["mean"].sem, sig["mean"].at(b, 1))
                dve.tensor_tensor(g["dev"][:], g["mv"][:, :, 0], g["mean"][:], ALU.subtract)\
                    .then_inc(sig["dev"].sem, 1)
                dve.wait_ge(sig["dev"].sem, sig["dev"].at(b, 1))
                dve.tensor_tensor(g["dev_sq"][:], g["dev"][:], g["dev"][:], ALU.mult).then_inc(sig["dev_sq"].sem, 1)
                dve.wait_ge(sig["dev_sq"].sem, sig["dev_sq"].at(b, 1))
                dve.tensor_tensor(g["var"][:], g["dev_sq"][:], g["mv"][:, :, 1], ALU.add).then_inc(sig["var"].sem, 1)
                yield
                dve.wait_ge(sig["std"].sem, sig["std"].at(b, 1))
                dve.reciprocal(g["inv"][:], g["std"][:]).then_inc(sig["inv"].sem, 1)
                dve.wait_ge(sig["inv"].sem, sig["inv"].at(b, 1))
                dve.tensor_tensor(g["scale"][:], g["inv"][:], vec[:, V_COLS[f"gn_w{n}"]], ALU.mult)\
                    .then_inc(sig["scale"].sem, 1)
                dve.wait_ge(sig["scale"].sem, sig["scale"].at(b, 1))
                dve.tensor_tensor(g["ms"][:], g["mean"][:], g["scale"][:], ALU.mult).then_inc(sig["ms"].sem, 1)
                dve.wait_ge(sig["ms"].sem, sig["ms"].at(b, 1))
                dve.tensor_tensor(g["bias"][:], vec[:, V_COLS[f"gn_b{n}"]], g["ms"][:], ALU.subtract)\
                    .then_inc(sig["bias"].sem, 1)
                dve.wait_ge(sig["bias"].sem, sig["bias"].at(b, 1))
                dve.tensor_scalar(dst[:, 0, :], src[:, 0, :], g["scale"][:, 0:1], g["bias"][:, 0:1],
                                  ALU.mult, ALU.add).then_inc(sig["h"].sem, 1)
                yield

            def front(b, last=None):
                yield from low_stacks(b, 0, False)
                dve.wait_ge(l0_g.sem, l0_g.at(b, 1))
                dve.tensor_copy(vg[:], ps[:, 2, 0:NT * L].rearrange("p (n c) -> p n c", n=NT))\
                    .then_inc(l0_v.sem, 1)
                yield
                yield from maxima(b, 0)
                yield from idle(1 + STEP_SLOTS[0] * STEPS + 1)
                dve.wait_ge(l0_lat_sum.sem, l0_lat_sum.at(b, 1))
                latents(b, 0)
                yield
                yield from residual0(b, 0, last)
                yield
                dve.wait_ge(l0_s2.sem, l0_s2.at(b, 1))
                s2 = ps[:, 2:4, :].rearrange("p i (n c) -> p (i n) c", n=4)
                dve.tensor_reduce(m2[:], s2, AX.X, ALU.max).then_inc(l0_m2.sem, 1)
                dve.wait_ge(l0_m2.sem, l0_m2.at(b, 1))
                dve.tensor_tensor(e2, s2, m2[:].unsqueeze(2).broadcast_to([P, NT, P]), ALU.subtract)\
                    .then_inc(l0_d2.sem, 1)
                yield
                yield
                dve.wait_ge(l0_lat_sum.sem, l0_lat_sum.at(b, 2))
                latents(b, 1)
                yield
                yield from residual0(b, 1)
                yield from low_stacks(b, 1, True)
                yield from take_values(b, 1, v, (2, 0))
                yield from maxima(b, 1)
                yield
                yield from chunks(b, 1)
                yield from group_norm(b, 2, xm, h, l1_res, 0)
                for which, bias, hi, lo in ((0, "bq2", qh2, ql2), (1, "bk2", kh2, kl2)):
                    for k in range(4):
                        blk, ic = divmod(k, IC)
                        low_parts(b, 2, blk, ic, which, k, bias, hi[:, blk, cols(ic)], lo[:, blk, cols(ic)])
                    yield
                yield from take_values(b, 2, v, (0, 2))
                yield from maxima(b, 2)
                yield
                yield from chunks(b, 2)
                for k in range(4):
                    ic, ch = divmod(k, CH)
                    dve.wait_ge(l2_proj.sem, l2_proj.at(b, k + 1))
                    dve.scalar_tensor_tensor(out=xm[:, ch, cols(ic)], in0=ps[:, k, :], scalar=vcol("bo2", ch),
                                             in1=xm[:, ch, cols(ic)], op0=ALU.add, op1=ALU.add)\
                        .then_inc(l2_res.sem, 1)
                yield

            def back(b, last=False):
                yield from group_norm(b, 3, xm, hb, l2_res, back0)

                def queries_and_keys(blk):
                    for which, bias in ((0, "bq3"), (1, "bk3")):
                        for ic in range(IC):
                            low_parts(b, 3, blk, ic, which, back0 + 2 * which + ic, bias,
                                      part[:, 2 * which, cols(ic)], part[:, 2 * which + 1, cols(ic)])
                    yield

                def add_weights(u, s):
                    ic, j = divmod(s, NT)
                    n = IC * u + ic
                    if j:
                        dve.wait_ge(exped[3].sem, exped[3].at(b, QUAD * (STEPS3 * u + s) + 2))
                        if j == 1 and n:
                            dve.wait_ge(total[3].sem, total[3].at(b, n))
                        if j > 1:
                            dve.wait_ge(summed_dve.sem, summed_dve.at(b, (NT - 1) * n + j - 1))
                        dve.tensor_tensor(accb[:, 0:2, :], prb[:, (s - 1) % 2, 0:2, :] if j == 1 else
                                          accb[:, 0:2, :], prb[:, s % 2, 0:2, :], ALU.add)\
                            .then_inc(summed_dve.sem, 1)

                def normalise(u, ic):
                    n = IC * u + ic
                    dve.wait_ge(total[3].sem, total[3].at(b, n + 1))
                    dve.reciprocal(rdenb[:], ps[:, turn3[total_use(ic) % 3], :]).then_inc(inverse[3].sem, 1)
                    dve.wait_ge(taken.sem, taken.at(b, n + 1))
                    dve.wait_ge(inverse[3].sem, inverse[3].at(b, n + 1))
                    dve.tensor_tensor(hb[:, u, cols(ic)], hb[:, u, cols(ic)], rdenb[:], ALU.mult)\
                        .then_inc(normed[3].sem, 1)

                yield from queries_and_keys(0)
                yield from take_values(b, 3, vb, (back0, back0 + 2))

                def maxima(u):
                    bank = stacks3(u, last)[2]
                    for k in range(QUAD * NT):
                        g, it = divmod(k, NT)
                        maximum(b, 3, QUAD * NT * u + k, "back", g, it, bank + 2 * (k % 2))
                        if k == QUAD * NT - 1:
                            round_maxima(b, 3, "back", u)
                        yield

                def middle(u):
                    if u == 0:
                        yield from queries_and_keys(1)
                    yield from idle(2)

                def steps(u):
                    for s in range(STEPS3):
                        if s == NT + 2:
                            normalise(u, 0)
                        yield
                        add_weights(u, s)
                        yield
                    yield
                    normalise(u, 1)
                    yield

                yield from both_rounds(maxima, middle, steps, last)
                yield from idle(2)
                dve.wait_ge(xd_copied.sem, xd_copied.at(b, 16))
                for ic in range(IC):
                    dve.wait_ge(l3_std.sem, l3_std.at(b, ic + 1))
                    dve.reciprocal(rstd[:, ic, :], rstd[:, ic, :]).then_inc(l3_rstd.sem, 1)
                    dve.wait_ge(l3_rstd.sem, l3_rstd.at(b, ic + 1))
                    for ch in range(CH):
                        k = CH * ic + ch
                        dve.tensor_tensor(y[:, ch, cols(ic)], y[:, ch, cols(ic)], rstd[:, ic, :], ALU.mult)\
                            .then_inc(l3_n.sem, 1)
                        dve.wait_ge(l3_n.sem, l3_n.at(b, k + 1))
                        dve.scalar_tensor_tensor(out=y[:, ch, cols(ic)], in0=y[:, ch, cols(ic)],
                                                 scalar=vcol("ln_w", ch), in1=xd[:, ch, cols(ic)],
                                                 op0=ALU.mult, op1=ALU.add).then_inc(l3_g.sem, 1)
                    yield

            alone(front(0), FRONT_SLOTS)
            with dve.Fori(0, B - 1) as b:
                by_turns(front(b + 1, b), back(b))
            finish_alone(back(B - 1, last=True))


def kernel(**inputs):
    import numpy as np
    import concourse.bacc as bacc
    from concourse.bass_utils import run_bass_kernel_spmd

    a = {k: np.asarray(t) for k, t in inputs.items()}
    three = lambda t: np.concatenate([t] * 3, axis=-1)
    qkv = a["L2_conv_qkv_w"].T
    weights = np.concatenate([
        three(a["L0_conv_w_theta"].T), a["L0_conv_w_phi"].T, a["L0_conv_w_g"].T,
        three(a["L1_conv_Wq"].T), a["L1_conv_Wk"].T, a["L1_conv_Wv"].T,
        qkv, a["L2_conv_proj_w"].T,
        a["L3_conv_wq"].T, a["L3_conv_wk"].T, a["L3_conv_wv"].T, a["L3_conv_wo"].T], axis=1)
    halves = lambda t: t.reshape(CH, P).T
    spread = lambda t: np.broadcast_to(t.reshape(1, 1), (P, 1))
    qkv_b = a["L2_conv_qkv_b"]
    vectors = np.concatenate([
        halves(a["L2_conv_gn_w"]), halves(a["L2_conv_gn_b"]), halves(qkv_b[0:C]), halves(qkv_b[C:2 * C]),
        halves(a["L2_conv_proj_b"]), halves(a["L3_conv_gn_gamma"]), halves(a["L3_conv_gn_beta"]),
        halves(a["L3_conv_bq"]), halves(a["L3_conv_bk"]), halves(a["L3_conv_bo"]),
        halves(a["L3_conv_ln_gamma"]), halves(a["L3_conv_ln_beta"]),
        np.concatenate([three(a["L1_conv_bq"]), a["L1_conv_bk"]]).reshape(P, 1),
        spread(a["L0_conv_gamma_sa"]), spread(a["L0_conv_gamma_moca"]), spread(a["L1_conv_gamma"])], axis=1)
    value_biases = np.broadcast_to(
        np.stack([a["L1_conv_bv"], qkv_b[2 * C:], a["L3_conv_bv"]])[None], (P, 3, C))
    small = np.concatenate([a["L0_conv_w_o"].T, a["L0_conv_concepts"].T], axis=1)
    concepts = a["L0_conv_concepts"]
    groups = np.kron(np.eye(P // GROUP), np.full((GROUP, GROUP), 1.0 / GROUP))
    constants = np.concatenate([np.eye(P), groups, np.tile(np.eye(L), (QUAD, 1))], axis=1).astype(np.float32)
    x = a["x"].reshape(B, C, T)

    arrays = {"x": x, "weights": weights, "vectors": vectors, "value_biases": value_biases, "small": small,
              "concepts": concepts, "constants": constants}
    arrays = {f"in_{k}": np.ascontiguousarray(t) for k, t in arrays.items()}
    nc = bacc.Bacc("TRN2", target_bir_lowering=False, num_devices=1)
    args = [nc.dram_tensor(k, t.shape, mybir.dt.from_np(t.dtype), kind="ExternalInput").ap()
            for k, t in arrays.items()]
    lat_dram = nc.dram_tensor("latents", (T, L), F32).ap()
    out = nc.dram_tensor("out", (B, C, T), F32, kind="ExternalOutput").ap()
    attention_layers(nc, *args, lat_dram, out)
    r = run_bass_kernel_spmd(nc, [arrays], core_ids=[0])
    return r.results[0]["out"].reshape(B, C, 32, 32)
```
